# Optimizing a Trainium2 kernel written in Bass

```python
import numpy as np
import jax
import jax.numpy as jnp

def _softmax(x, axis=-1):
    return jax.nn.softmax(x, axis=axis)

def _gelu(x):
    return jax.nn.gelu(x, approximate=True)

def _silu(x):
    return jax.nn.silu(x)

def _sigmoid(x):
    return jax.nn.sigmoid(x)

def _layernorm(x, axis=-1, eps=1e-05):
    m = jnp.mean(x, axis=axis, keepdims=True)
    v = jnp.var(x, axis=axis, keepdims=True)
    return (x - m) / jnp.sqrt(v + eps)

def _scatter_add(tgt, idx, src, axis=0):
    return tgt.at[idx].add(src)

def _segment_sum(src, seg, n):
    return jax.ops.segment_sum(src, seg, n)
kernel_name = 'mk_seq_preln_d1_jaxref_r4_7a8758'

def setup_inputs(seed: int=0):
    np.random.seed(seed)
    _w = jnp.asarray

    def _L0_attn_setup():
        import jax, jax.numpy as jnp
        import numpy as np
        B, L, D = (2, 512, 256)
        H, HD = (16, 64)
        LD = 64
        key = jax.random.key(seed)
        ks = jax.random.split(key, 6)
        s = lambda fan_in: 1.0 / np.sqrt(fan_in)
        x_bld = jax.random.normal(ks[0], (B, L, D), dtype=jnp.float32)
        Wq = jax.random.normal(ks[1], (D, H, HD), dtype=jnp.float32) * s(D)
        Wkv_down = jax.random.normal(ks[2], (D, LD), dtype=jnp.float32) * s(D)
        Wk_up = jax.random.normal(ks[3], (LD, H, HD), dtype=jnp.float32) * s(LD)
        Wv_up = jax.random.normal(ks[4], (LD, H, HD), dtype=jnp.float32) * s(LD)
        Wout = jax.random.normal(ks[5], (H, HD, D), dtype=jnp.float32) * s(H * HD)
        return {'x_bld': x_bld, 'Wq': Wq, 'Wkv_down': Wkv_down, 'Wk_up': Wk_up, 'Wv_up': Wv_up, 'Wout': Wout}
    _L0_attn_in = _L0_attn_setup()

    def _L0_ffn_setup():
        import jax, jax.numpy as jnp
        import numpy as np
        H, I, E, NS, C = (256, 256, 6, 2, 2)
        TOPK = 2
        TEMP = 1.0
        EPS = 1e-06
        key = jax.random.key(seed)
        ks = jax.random.split(key, 20)
        sd = 0.02
        inp = {'x': jax.random.normal(ks[0], (4, 512, H), jnp.float32), 'router_W': jax.random.normal(ks[1], (C, H, E), jnp.float32) * sd, 'router_b': jax.random.normal(ks[2], (C, E), jnp.float32) * sd, 'gate_bias': jax.random.normal(ks[3], (C, E), jnp.float32) * sd, 'exp_Wup': jax.random.normal(ks[4], (E, H, I), jnp.float32) * sd, 'exp_bup': jnp.zeros((E, I), jnp.float32), 'exp_Wg': jax.random.normal(ks[5], (E, I, I), jnp.float32) * sd, 'exp_bg': jnp.zeros((E, I), jnp.float32), 'exp_Wdown': jax.random.normal(ks[6], (E, I, H), jnp.float32) * sd, 'exp_bdown': jnp.zeros((E, H), jnp.float32), 'share_Wup': jax.random.normal(ks[7], (H, NS * I), jnp.float32) * sd, 'share_bup': jnp.zeros((NS * I,), jnp.float32), 'share_Wg': jax.random.normal(ks[8], (I, I), jnp.float32) * sd, 'share_bg': jnp.zeros((I,), jnp.float32), 'share_Wdown': jax.random.normal(ks[9], (I, H), jnp.float32) * sd, 'share_bdown': jnp.zeros((H,), jnp.float32), 'norm_w': jnp.ones((C, H), jnp.float32)}
        return inp
    _L0_ffn_in = _L0_ffn_setup()
    _d = {'L0_attn_x_bld': _L0_attn_in['x_bld'], 'L0_attn_Wq': _L0_attn_in['Wq'], 'L0_attn_Wkv_down': _L0_attn_in['Wkv_down'], 'L0_attn_Wk_up': _L0_attn_in['Wk_up'], 'L0_attn_Wv_up': _L0_attn_in['Wv_up'], 'L0_attn_Wout': _L0_attn_in['Wout'], 'L0_ffn_router_W': _L0_ffn_in['router_W'], 'L0_ffn_router_b': _L0_ffn_in['router_b'], 'L0_ffn_gate_bias': _L0_ffn_in['gate_bias'], 'L0_ffn_exp_Wup': _L0_ffn_in['exp_Wup'], 'L0_ffn_exp_bup': _L0_ffn_in['exp_bup'], 'L0_ffn_exp_Wg': _L0_ffn_in['exp_Wg'], 'L0_ffn_exp_bg': _L0_ffn_in['exp_bg'], 'L0_ffn_exp_Wdown': _L0_ffn_in['exp_Wdown'], 'L0_ffn_exp_bdown': _L0_ffn_in['exp_bdown'], 'L0_ffn_share_Wup': _L0_ffn_in['share_Wup'], 'L0_ffn_share_bup': _L0_ffn_in['share_bup'], 'L0_ffn_share_Wg': _L0_ffn_in['share_Wg'], 'L0_ffn_share_bg': _L0_ffn_in['share_bg'], 'L0_ffn_share_Wdown': _L0_ffn_in['share_Wdown'], 'L0_ffn_share_bdown': _L0_ffn_in['share_bdown'], 'L0_ffn_norm_w': _L0_ffn_in['norm_w']}
    _x0 = _d['L0_attn_x_bld']
    _d['L0_attn_x_bld'] = jax.random.normal(jax.random.fold_in(jax.random.key(seed), 1), (2, 2048, 256), dtype=_x0.dtype)
    del _x0
    return _d

def reference(L0_attn_x_bld, L0_attn_Wq, L0_attn_Wkv_down, L0_attn_Wk_up, L0_attn_Wv_up, L0_attn_Wout, L0_ffn_router_W, L0_ffn_router_b, L0_ffn_gate_bias, L0_ffn_exp_Wup, L0_ffn_exp_bup, L0_ffn_exp_Wg, L0_ffn_exp_bg, L0_ffn_exp_Wdown, L0_ffn_exp_bdown, L0_ffn_share_Wup, L0_ffn_share_bup, L0_ffn_share_Wg, L0_ffn_share_bg, L0_ffn_share_Wdown, L0_ffn_share_bdown, L0_ffn_norm_w):

    def _L0_attn_ref(x_bld, Wq, Wkv_down, Wk_up, Wv_up, Wout):
        import jax, jax.numpy as jnp
        import numpy as np
        B, L, D = (2, 512, 256)
        H, HD = (16, 64)
        LD = 64
        q_blhd = jnp.einsum('bld,dhk->blhk', x_bld, Wq)
        latent_bll = jnp.einsum('bld,dc->blc', x_bld, Wkv_down)
        k_blhd = jnp.einsum('blc,chk->blhk', latent_bll, Wk_up)
        v_blhd = jnp.einsum('blc,chk->blhk', latent_bll, Wv_up)
        attn = jnp.einsum('bqhd,bkhd->bhqk', q_blhd, k_blhd) / jnp.sqrt(jnp.asarray(HD, dtype=x_bld.dtype))
        l = x_bld.shape[1]
        mask = (jnp.arange(l)[None, :] <= jnp.arange(l)[:, None])[None, None]
        neg_inf = jnp.finfo(attn.dtype).min
        attn = jax.nn.softmax(jnp.where(mask, attn, neg_inf), axis=-1)
        y_blhd = jnp.einsum('bhqk,bkhd->bqhd', attn, v_blhd)
        return jnp.einsum('bqhd,hdo->bqo', y_blhd, Wout)

    def _L0_ffn_ref(x, router_W, router_b, gate_bias, exp_Wup, exp_bup, exp_Wg, exp_bg, exp_Wdown, exp_bdown, share_Wup, share_bup, share_Wg, share_bg, share_Wdown, share_bdown, norm_w):
        import jax, jax.numpy as jnp
        import numpy as np
        H, I, E, NS, C = (256, 256, 6, 2, 2)
        TOPK = 2
        TEMP = 1.0
        EPS = 1e-06
        B, S, Hd = x.shape
        xf = x.reshape(-1, Hd)
        for j in range(C):
            residual = xf
            gate = (xf @ router_W[j] + router_b[j]) / TEMP
            biased = gate + gate_bias[j]
            _, ids = jax.lax.top_k(biased, TOPK)
            sel = (ids[:, :, None] == jnp.arange(E)[None, None, :]).any(axis=1)
            weights = jax.nn.softmax(jnp.where(sel, gate, -jnp.inf), axis=-1)
            h = jnp.einsum('nh,ehi->eni', xf, exp_Wup) + exp_bup[:, None, :]
            h = jax.nn.silu(jnp.einsum('eni,eij->enj', h, exp_Wg) + exp_bg[:, None, :]) * h
            eo = jnp.einsum('eni,eih->enh', h, exp_Wdown) + exp_bdown[:, None, :]
            combined = jnp.einsum('ne,enh->nh', weights, eo)
            s = (xf @ share_Wup + share_bup).reshape(-1, NS, I)
            s = jax.nn.silu(s @ share_Wg + share_bg) * s
            share_out = (s @ share_Wdown + share_bdown).sum(axis=1)
            z = combined + share_out
            y = residual + z
            y = y * jax.lax.rsqrt(jnp.mean(y * y, axis=-1, keepdims=True) + EPS) * norm_w[j]
            xf = y
        return xf.reshape(B, S, Hd)
    x = L0_attn_x_bld
    x = x + _L0_attn_ref(_layernorm(x, axis=-1), L0_attn_Wq, L0_attn_Wkv_down, L0_attn_Wk_up, L0_attn_Wv_up, L0_attn_Wout)
    x = x + _L0_ffn_ref(_layernorm(x, axis=-1), L0_ffn_router_W, L0_ffn_router_b, L0_ffn_gate_bias, L0_ffn_exp_Wup, L0_ffn_exp_bup, L0_ffn_exp_Wg, L0_ffn_exp_bg, L0_ffn_exp_Wdown, L0_ffn_exp_bdown, L0_ffn_share_Wup, L0_ffn_share_bup, L0_ffn_share_Wg, L0_ffn_share_bg, L0_ffn_share_Wdown, L0_ffn_share_bdown, L0_ffn_norm_w)
    return x

_drawn_inputs = setup_inputs


def setup_inputs(seed=0):
    import zlib

    import numpy as np

    out = dict(_drawn_inputs(seed))
    spreads = {'L0_ffn_exp_bup': (0.0, 0.8),
     'L0_ffn_exp_bg': (0.0, 0.8),
     'L0_ffn_exp_bdown': (0.0, 0.1),
     'L0_ffn_share_bup': (0.0, 0.8),
     'L0_ffn_share_bg': (0.0, 0.8),
     'L0_ffn_share_bdown': (0.0, 0.1),
     'L0_ffn_norm_w': (1.0, 0.2)}
    factors = {'L0_ffn_router_b': 6.295,
     'L0_ffn_gate_bias': 5.317,
     'L0_ffn_exp_Wup': 8.0,
     'L0_ffn_exp_Wg': 8.0,
     'L0_ffn_exp_Wdown': 8.0,
     'L0_ffn_share_Wup': 5.291,
     'L0_ffn_share_Wg': 6.877,
     'L0_ffn_share_Wdown': 5.138}
    for name, (base, spread) in spreads.items():
        noise = np.random.default_rng([zlib.crc32(name.encode()), seed]).standard_normal(out[name].shape)
        drawn = base * np.exp(spread * noise) if base else spread * noise
        out[name] = jnp.asarray(drawn.astype(out[name].dtype))
    for name, factor in factors.items():
        out[name] = (out[name] * factor).astype(out[name].dtype)
    return out
```

```python
from contextlib import ExitStack

import numpy as np
import concourse.bass as bass
from concourse import mybir

F32 = mybir.dt.float32
F32R = mybir.dt.float32r
BF16 = mybir.dt.bfloat16
ALU = mybir.AluOpType
ACT = mybir.ActivationFunctionType
AX = mybir.AxisListType

P = 128
B, L, D = 2, 2048, 256
H, HD, LD = 16, 64, 64
E, I = 6, 256
NE = 8
ROUNDS = 2
DT = D // P
BLK = 512
TPB = BLK // P
QB = L // BLK
KT = L // P
PAIRS = H // 2
NBLK = B * QB
SCALE = float(HD) ** -0.5
MASK = -1.0e30
LN_EPS, RMS_EPS = 1e-5, 1e-6
DMA = 16

SCORE_STEPS = [(qb, kt) for qb in range(QB) for kt in range(TPB * (qb + 1))]
MAX_STEPS = [(TPB * qb + j, c) for qb in range(QB) for j in range(TPB) for c in range(qb + 1)]
STEPS = len(SCORE_STEPS)
INVERT_AFTER = 8
DIVIDE_AFTER = 13
LAG = 4
RING = 5


def f32(ap):
    return ap.bitcast(F32)


def clear_semaphores(nc, sems):
    for s in sems:
        nc.sync.sem_clear(s)
    nc.all_engine_barrier()


def build_weights(nc, T, w):
    with ExitStack() as ctx:
        def sb(name, shape, dt=F32):
            return ctx.enter_context(nc.sbuf_tensor(name, shape, dt))
        names = ["loaded", "zeroed", "made", "m_ready", "n_ready", "hi_done", "lo_done"]
        S = {n: ctx.enter_context(nc.semaphore("w_" + n)) for n in names}
        wq = sb("wq", [HD, H, D])
        wk = sb("wk", [HD, H, LD])
        wv = sb("wv", [HD, H, LD])
        wo = sb("wo", [HD, H, D])
        wd = sb("wd", [P, DT, LD])
        ps = T["ps"]
        with nc.Block() as block:
            @block.sync
            def _(sp):
                sp.dma_start(wq[:, :, :], w["wqT"].rearrange("h k d -> k h d")).then_inc(S["loaded"], DMA)
                sp.dma_start(wk[:, :, :], w["wkT"].rearrange("h k c -> k h c")).then_inc(S["loaded"], DMA)
                sp.dma_start(wv[:, :, :], w["wvT"].rearrange("h k c -> k h c")).then_inc(S["loaded"], DMA)
                sp.dma_start(wo[:, :, :], w["wout"].rearrange("h k d -> k h d")).then_inc(S["loaded"], DMA)
                sp.dma_start(wd[:, :, :], w["wdown"].rearrange("(t p) c -> p t c", p=P)).then_inc(S["loaded"], DMA)

            @block.gpsimd
            def _(pool):
                pool.memset(T["ident"][:, :], 0.0).then_inc(S["zeroed"], 1)
                pool.memset(T["mask_kq"][:, :], 0.0).then_inc(S["zeroed"], 1)
                pool.memset(T["mask_qk"][:, :], 0.0).then_inc(S["zeroed"], 1)
                pool.memset(T["minus_half"][:, :], -0.5).then_inc(S["zeroed"], 1)
                pool.wait_ge(S["zeroed"], 4)
                pool.affine_select(out=T["ident"][:, :], in_=T["ident"][:, :], compare_op=ALU.not_equal, fill=1.0,
                                   base=0, pattern=[[-1, P]], channel_multiplier=1).then_inc(S["made"], 1)
                for mask, sign in ((T["mask_kq"], 1), (T["mask_qk"], -1)):
                    pool.affine_select(out=mask[:, :], in_=mask[:, :], compare_op=ALU.is_ge, fill=MASK,
                                       base=0, pattern=[[sign, P]], channel_multiplier=-sign).then_inc(S["made"], 1)

            @block.tensor
            def _(pe):
                pe.wait_ge(S["loaded"], 5 * DMA)
                for dt in range(DT):
                    for h in range(H):
                        mm = pe.matmul(ps[:, 2 * dt + h // 8, (h % 8) * LD:(h % 8 + 1) * LD],
                                       wq[:, h, dt * P:(dt + 1) * P], wk[:, h, :], start=True, stop=True)
                mm.then_inc(S["m_ready"], 1)
                for h in range(H):
                    half, pr = h % 2, h // 2
                    mm = pe.matmul(ps[half * LD:(half + 1) * LD, 4 + pr // 2, (pr % 2) * D:(pr % 2 + 1) * D],
                                   wv[:, h, :], wo[:, h, :], start=True, stop=True)
                mm.then_inc(S["n_ready"], 1)

            @block.scalar
            def _(act):
                act.wait_ge(S["m_ready"], 1)
                for dt in range(DT):
                    for b2 in range(2):
                        act.activation(T["m_hi"][:, 4 * b2:4 * b2 + 4, dt, :], ps[:, 2 * dt + b2, :].rearrange(
                            "p (a c) -> p a c", c=P), ACT.Copy, scale=SCALE).then_inc(S["hi_done"], 1)
                act.wait_ge(S["n_ready"], 1)
                for b2 in range(4):
                    act.activation(T["n_hi"][:, 2 * b2:2 * b2 + 2, :], ps[:, 4 + b2, :].rearrange(
                        "p (a c) -> p a c", c=D), ACT.Copy).then_inc(S["hi_done"], 1)
                for half in range(2):
                    act.activation(T["wd_hi"][:, :, half * LD:(half + 1) * LD], wd[:, :, :],
                                   ACT.Copy).then_inc(S["hi_done"], 1)

            @block.vector
            def _(dve):
                n = 0
                for dt in range(DT):
                    for b2 in range(2):
                        n += 1
                        dve.wait_ge(S["hi_done"], n)
                        dve.scalar_tensor_tensor(
                            out=T["m_lo"][:, 4 * b2:4 * b2 + 4, dt, :],
                            in0=ps[:, 2 * dt + b2, :].rearrange("p (a c) -> p a c", c=P), scalar=SCALE,
                            in1=f32(T["m_hi"][:, 4 * b2:4 * b2 + 4, dt, :]),
                            op0=ALU.mult, op1=ALU.subtract).then_inc(S["lo_done"], 1)
                for b2 in range(4):
                    n += 1
                    dve.wait_ge(S["hi_done"], n)
                    dve.tensor_tensor(T["n_lo"][:, 2 * b2:2 * b2 + 2, :],
                                      ps[:, 4 + b2, :].rearrange("p (a c) -> p a c", c=D),
                                      f32(T["n_hi"][:, 2 * b2:2 * b2 + 2, :]), ALU.subtract).then_inc(S["lo_done"], 1)
                for half in range(2):
                    n += 1
                    dve.wait_ge(S["hi_done"], n)
                    dve.tensor_tensor(T["wd_lo"][:, :, half * LD:(half + 1) * LD], wd[:, :, :],
                                      f32(T["wd_hi"][:, :, half * LD:(half + 1) * LD]),
                                      ALU.subtract).then_inc(S["lo_done"], 1)
        clear_semaphores(nc, S.values())


def build_latents(nc, T, x_seq):
    with ExitStack() as ctx:
        def sb(name, shape, dt=F32):
            return ctx.enter_context(nc.sbuf_tensor(name, shape, dt))
        names = [f"loaded{g}" for g in range(QB)] + ["stats", "mean", "var", "rstd", "normed", "turned", "x_hi", "x_lo",
                 "lat", "k_hi", "lat_copied", "k_lo", "lat_turned", "v_hi", "v_lo", "filled"]
        S = {n: ctx.enter_context(nc.semaphore("l_" + n)) for n in names}
        x = sb("lx", [P, KT, D])
        xn = sb("lxn", [P, KT, D])
        st = sb("lst", [P, KT, 6])
        mv = sb("lmv", [P, KT, 2])
        rs = sb("lrs", [P, KT, 1])
        ve = sb("lve", [P, KT, 1])
        lat = sb("llat", [LD, L])
        ps, xh, xl, kh, kl, va, vc = (T[k] for k in ("ps", "xt_hi", "xt_lo", "k_hi", "k_lo", "v_hi", "v_lo"))
        x_v = x_seq.rearrange("(t p) d -> p t d", p=P)
        with nc.Block() as block:
            @block.sync
            def _(sp):
                for g in range(QB):
                    sp.dma_start(x[:, TPB * g:TPB * (g + 1), :],
                                 x_v[:, TPB * g:TPB * (g + 1), :]).then_inc(S[f"loaded{g}"], DMA)

            @block.gpsimd
            def _(pool):
                pool.memset(f32(kl[LD:LD + 1, :]), 1.0).then_inc(S["filled"], 1)
                pool.wait_ge(S["filled"], 1)
                pool.memset(f32(va[:, :, LD:P]), 1.0).then_inc(S["filled"], 1)
                pool.memset(f32(vc[:, :, LD:P]), 0.0).then_inc(S["filled"], 1)
                for g in range(QB):
                    ts = slice(TPB * g, TPB * (g + 1))
                    pool.wait_ge(S["mean"], TPB * (g + 1))
                    pool.tensor_scalar(ve[:, ts, :], mv[:, ts, 1:2], LN_EPS, None, ALU.add).then_inc(S["var"], 1)
                    pool.wait_ge(S["var"], g + 1)
                    pool.tensor_tensor(rs[:, ts, :], ve[:, ts, :], T["minus_half"][:, 0:TPB, None],
                                       ALU.pow).then_inc(S["rstd"], 1)

            @block.vector
            def _(dve):
                def norm(g):
                    dve.wait_ge(S[f"loaded{g}"], DMA)
                    for t in range(TPB * g, TPB * (g + 1)):
                        dve.bn_stats(st[:, t, :], x[:, t, :]).then_inc(S["stats"], 1)
                    for t in range(TPB * g, TPB * (g + 1)):
                        dve.wait_ge(S["stats"], t + 1)
                        dve.bn_aggr(mv[:, t, :], st[:, t, :]).then_inc(S["mean"], 1)
                    dve.wait_ge(S["rstd"], g + 1)
                    for t in range(TPB * g, TPB * (g + 1)):
                        dve.tensor_scalar(xn[:, t, :], x[:, t, :], mv[:, t, 0:1], rs[:, t, :],
                                          ALU.subtract, ALU.mult).then_inc(S["normed"], 1)

                def split_x(g):
                    for dt in range(DT):
                        dve.wait_ge(S["x_hi"], DT * g + dt + 1)
                        o = (slice(None), dt, slice(BLK * g, BLK * (g + 1)))
                        dve.tensor_tensor(xl[o], ps[:, 2 * (g % 2) + dt, :], f32(xh[o]), ALU.subtract).then_inc(S["x_lo"], 1)

                def split_k(g):
                    c = slice(BLK * g, BLK * (g + 1))
                    dve.wait_ge(S["lat_copied"], g + 1)
                    dve.tensor_tensor(kl[0:LD, c], lat[:, c], f32(kh[0:LD, c]), ALU.subtract).then_inc(S["k_lo"], 1)

                def split_v(g):
                    dve.wait_ge(S["v_hi"], g + 1)
                    o = (slice(None), slice(TPB * g, TPB * (g + 1)), slice(0, LD))
                    dve.tensor_tensor(vc[o], ps[:, 6 + g % 2, 0:TPB * LD].rearrange("p (t c) -> p t c", c=LD),
                                      f32(va[o]), ALU.subtract).then_inc(S["v_lo"], 1)

                norm(0)
                for g in range(QB):
                    if g + 1 < QB:
                        norm(g + 1)
                    split_x(g)
                    split_k(g)
                    split_v(g)

            @block.tensor
            def _(pe):
                def turn(g):
                    pe.wait_ge(S["normed"], TPB * (g + 1))
                    if g >= 2:
                        pe.wait_ge(S["x_lo"], DT * (g - 1))
                    for dt in range(DT):
                        for j in range(TPB):
                            mm = pe.transpose(ps[:, 2 * (g % 2) + dt, j * P:(j + 1) * P],
                                              xn[:, TPB * g + j, dt * P:(dt + 1) * P], T["ident"][:, :])
                    mm.then_inc(S["turned"], 1)

                def latents(g):
                    c = slice(BLK * g, BLK * (g + 1))
                    pe.wait_ge(S["x_lo"], DT * (g + 1))
                    if g >= 2:
                        pe.wait_ge(S["lat_copied"], g - 1)
                    terms = [(a, m, dt) for a, m in (("wd_hi", xh), ("wd_hi", xl), ("wd_lo", xh)) for dt in range(DT)]
                    for n, (a, m, dt) in enumerate(terms):
                        mm = pe.matmul(ps[:, 4 + g % 2, :], T[a][:, dt, :], m[:, dt, c],
                                       start=n == 0, stop=n == len(terms) - 1)
                    mm.then_inc(S["lat"], 1)

                def turn_latents(g):
                    pe.wait_ge(S["lat_copied"], g + 1)
                    if g >= 2:
                        pe.wait_ge(S["v_lo"], g - 1)
                    for j in range(TPB):
                        t = TPB * g + j
                        mm = pe.transpose(ps[:, 6 + g % 2, j * LD:(j + 1) * LD], lat[:, t * P:(t + 1) * P],
                                          T["ident"][0:LD, 0:LD])
                    mm.then_inc(S["lat_turned"], 1)

                turn(0)
                for g in range(QB):
                    if g + 1 < QB:
                        turn(g + 1)
                    latents(g)
                    turn_latents(g)

            @block.scalar
            def _(act):
                for g in range(QB):
                    c = slice(BLK * g, BLK * (g + 1))
                    act.wait_ge(S["turned"], g + 1)
                    for dt in range(DT):
                        act.activation(xh[:, dt, c], ps[:, 2 * (g % 2) + dt, :], ACT.Copy).then_inc(S["x_hi"], 1)
                    act.wait_ge(S["lat"], g + 1)
                    act.activation(kh[:, c], ps[:, 4 + g % 2, :], ACT.Copy).then_inc(S["k_hi"], 1)
                    act.activation(lat[:, c], ps[0:LD, 4 + g % 2, :], ACT.Copy).then_inc(S["lat_copied"], 1)
                    act.wait_ge(S["lat_turned"], g + 1)
                    act.activation(va[:, TPB * g:TPB * (g + 1), 0:LD],
                                   ps[:, 6 + g % 2, 0:TPB * LD].rearrange("p (t c) -> p t c", c=LD),
                                   ACT.Copy).then_inc(S["v_hi"], 1)
        clear_semaphores(nc, S.values())


BANK_JOBS = [(1, "row", 0, 3), (5, "row", 1, 0), (8, "proj", 2, 0), (13, "row", 1, 1), (16, "proj", 2, 1),
             (25, "row", 1, 2), (28, "proj", 2, 2), (34, "proj", 2, 3), (41, "row", 1, 3),
             (45, "row", 2, 0), (53, "row", 2, 1), (65, "row", 2, 2)]
SPLITS = [(3, 1, 3), (9, 2, 0), (17, 2, 1), (29, 2, 2), (42, 2, 3), (46, 3, 0), (54, 3, 1), (66, 3, 2)]
FIRST_ROWS = 3
FIRST_SPLITS = 7
ON_DVE = [s % 3 == 0 for s in range(2 * STEPS)]
DVE_LOS, POOL_LOS = sum(ON_DVE), 2 * STEPS - sum(ON_DVE)


def los_before(s, on_dve):
    return sum(1 for t in range(s) if ON_DVE[t] == on_dve)


def same_bank_before(s):
    return s - 3 if s >= 3 else max(t for t in range(2 * STEPS) if t % 3 == s) - 2 * STEPS


def is_diagonal(s):
    qb, kt = SCORE_STEPS[s % STEPS]
    return kt >= TPB * qb


def diagonals_before(s):
    return sum(is_diagonal(t) for t in range(s))


DIAGONALS = diagonals_before(2 * STEPS)


def block_end(qb):
    return 2 * (qb + 1) * (qb + 2) - 1


def build_attention(nc, T, y_seq, recip_rows):
    with ExitStack() as ctx:
        def sb(name, shape, dt=F32):
            return ctx.enter_context(nc.sbuf_tensor(name, shape, dt))
        names = ["staged",
                 "max_scored",
                 "max_masked",
                 "max_read",
                 "part_max",
                 "neg_max",
                 "bank_made",
                 "bank_read",
                 "q_hi", "q_lo", "q_copy",
                 "scored",
                 "masked",
                 "probs",
                 "probs_hi",
                 "lo_dve", "lo_pool",
                 "latent_used",
                 "y_copied",
                 "sums_in",
                 "recip",
                 "recip_out",
                 "recip_in",
                 "normed",
                 "stored0", "stored1", "stored2", "stored3",
                 "row_in0", "row_in1", "row_in2", "row_in3"]
        S = {n: ctx.enter_context(nc.semaphore("a_" + n)) for n in names}
        stage_hi = sb("stage_hi", [P, DT, P], F32R)
        stage_lo = sb("stage_lo", [P, DT, P], F32R)
        q_raw = sb("q_raw", [P, L])
        qa = [sb(f"q_parts{i}", [P, L], F32R) for i in range(2)]
        qc = [sb(f"q_row{i}", [LD + 1, L], F32R) for i in range(2)]
        pr = sb("pr", [P, RING, BLK])
        ph = sb("ph", [P, RING, BLK], F32R)
        pl = sb("pl", [P, RING, BLK], F32R)
        part = sb("part", [P, 2, TPB, QB])
        mx = sb("mx", [P, 2, TPB])
        neg = sb("neg", [P, 2, TPB])
        neg_rows = sb("neg_rows", [TPB, QB, P], F32R)
        y = sb("y_sums", [P, QB, BLK])
        sums = sb("sums", [P, QB, TPB])
        rec = sb("rec", [LD, QB, BLK])
        ps, xh, xl, kh, kl, va, vc = (T[k] for k in ("ps", "xt_hi", "xt_lo", "k_hi", "k_lo", "v_hi", "v_lo"))

        SCORE_BANK, MAX_BANK, Y_BANK, BANK = 0, 3, 5, 7

        def jobs_at(s, last):
            kept = [j for j in BANK_JOBS if not (last and j[2] == 2)]
            return [(n, j) for n, j in enumerate(kept) if j[0] == s]

        def splits_at(s, last):
            kept = [j for j in SPLITS if not (last and j[1] >= 2)]
            return [(n, j) for n, j in enumerate(kept) if j[0] == s]

        def row_job(head, qb, last):
            kept = [j for j in BANK_JOBS if not (last and j[2] == 2)]
            at = [n for n, j in enumerate(kept) if j[1:] == ("row", head, qb)]
            if at:
                return at[0] + 1
            at = [n for n, j in enumerate(BANK_JOBS) if j[1:] == ("row", head + 2, qb)]
            return at[0] + 1 - len(BANK_JOBS)

        FIRST_JOBS = QB + FIRST_ROWS
        NJOBS, NSPLITS = len(BANK_JOBS), len(SPLITS)

        def turns(eng, turn):
            turn(0, True, False)
            with eng.Fori(1, PAIRS - 1) as p:
                turn(p, False, False)
            turn(PAIRS - 1, False, True)

        def block_jobs(job, s, after, p, first):
            for half in range(2):
                for qb in range(QB):
                    at = STEPS * half + block_end(qb) + after
                    if at == s:
                        job(p, half, qb)
                    elif at == s + 2 * STEPS and not first:
                        job(p - 1, half, qb)

        def late_jobs(job, after):
            for half in range(2):
                for qb in range(QB):
                    if STEPS * half + block_end(qb) + after >= 2 * STEPS:
                        job(PAIRS - 1, half, qb)

        def split_waits(p, head, qb, first):
            jobs = [n for n, j in enumerate(BANK_JOBS) if j[1:] == ("proj", 2, qb)]
            read = FIRST_JOBS + NJOBS * p + jobs[0] + 1
            if head == 1:
                return (QB, None) if first else (FIRST_JOBS + NJOBS * (p - 1) + jobs[0] + 1, 2 * STEPS * p)
            return read, 2 * STEPS * p + STEPS * (head - 2) + block_end(qb) + 1

        def wait_lo(eng, p, s):
            if s < 0:
                p, s = p - 1, s + 2 * STEPS
            if ON_DVE[s]:
                eng.wait_ge(S["lo_dve"], DVE_LOS * p + los_before(s + 1, True))
            else:
                eng.wait_ge(S["lo_pool"], POOL_LOS * p + los_before(s + 1, False))

        def make_lo(eng, p, s, first, sem):
            qb, kt = SCORE_STEPS[s % STEPS]
            w = BLK - P * max(0, kt - TPB * qb)
            eng.wait_ge(S["probs_hi"], 2 * STEPS * p + s + 1)
            if not (first and s < RING):
                eng.wait_ge(S["latent_used"], 2 * STEPS * p + s - RING + 1)
            eng.tensor_tensor(pl[:, s % RING, 0:w], pr[:, s % RING, 0:w], f32(ph[:, s % RING, 0:w]),
                              ALU.subtract).then_inc(sem, 1)

        with nc.Block() as block:
            @block.sync
            def _(sp):
                def stage(pair, projected):
                    if projected is not None:
                        sp.wait_ge(S["bank_made"], projected)
                    sp.dma_start(f32(stage_hi[:, :, :]), f32(T["m_hi"][:, pair, :, :])).then_inc(S["staged"], DMA)
                    sp.dma_start(f32(stage_lo[:, :, :]), f32(T["m_lo"][:, pair, :, :])).then_inc(S["staged"], DMA)

                def divide(p, half, qb):
                    n = 8 * p + 4 * half + qb
                    sp.wait_ge(S["y_copied"], n + 1)
                    sp.dma_start(sums[:, qb, :], y[LD:LD + 1, qb, :]).then_inc(S["sums_in"], DMA)
                    sp.wait_ge(S["recip"], n + 1)
                    sp.dma_start(recip_rows[qb], sums[:, qb, :]).then_inc(S["recip_out"], DMA)
                    sp.wait_ge(S["recip_out"], DMA * (n + 1))
                    sp.dma_start(rec[:, qb, :], recip_rows[qb:qb + 1, :, :].rearrange("a p j -> a (p j)").broadcast_to(
                        [LD, BLK])).then_inc(S["recip_in"], DMA)

                def store(p, half, qb):
                    sp.wait_ge(S["normed"], 8 * p + 4 * half + qb + 1)
                    sp.dma_start(y_seq[qb, half * LD:(half + 1) * LD, p, :], y[0:LD, qb, :]).then_inc(S[f"stored{qb}"], DMA)

                def turn(p, more, first=False):
                    for half in range(2):
                        for qb in range(QB):
                            divide(p, half, qb)
                            if half or qb:
                                store(p, half - (qb == 0), (qb - 1) % QB)
                            elif not first:
                                store(p - 1, 1, QB - 1)
                            if more and (half, qb) == (0, 2):
                                stage(p + 2, FIRST_JOBS + NJOBS * p + 8)

                stage(0, None)
                stage(1, QB)
                turn(0, True, first=True)
                with sp.Fori(1, PAIRS - 2) as p:
                    turn(p, True)
                with sp.Fori(PAIRS - 2, PAIRS) as p:
                    turn(p, False)
                store(PAIRS - 1, 1, QB - 1)
                for qb in range(QB):
                    sp.wait_ge(S[f"stored{qb}"], DMA * H)

            @block.tensor
            def _(pe):
                def project(pair, qb, job):
                    pe.wait_ge(S["staged"], 2 * DMA * (pair + 1))
                    pe.wait_ge(S["bank_read"], job)
                    c = slice(BLK * qb, BLK * (qb + 1))
                    terms = [(a, m, dt) for a, m in ((stage_hi, xh), (stage_hi, xl), (stage_lo, xh)) for dt in range(DT)]
                    for n, (a, m, dt) in enumerate(terms):
                        mm = pe.matmul(ps[:, BANK, :], a[:, dt, :], m[:, dt, c], start=n == 0, stop=n == len(terms) - 1)
                    mm.then_inc(S["bank_made"], 1)

                def row(qb, block_no, job):
                    pe.wait_ge(S["neg_max"], block_no + 1)
                    pe.wait_ge(S["bank_read"], job)
                    pe.transpose(ps[0:TPB, BANK, 0:P], neg[:, qb % 2, :], T["ident"][:, :]).then_inc(S["bank_made"], 1)

                def max_scores(half, m, split_no, n, first=False):
                    i, c = MAX_STEPS[m]
                    if c == 0 and i % TPB == 0:
                        pe.wait_ge(S["q_hi"], split_no + 1)
                        pe.wait_ge(S["q_lo"], split_no + 1)
                    if not first:
                        pe.wait_ge(S["max_read"], n - 1)
                    w = BLK if c < i // TPB else P * (i % TPB + 1)
                    pe.matmul(ps[:, MAX_BANK + m % 2, 0:w], qa[half][:, i * P:(i + 1) * P],
                              kh[:, c * BLK:c * BLK + w], start=True, stop=True).then_inc(S["max_scored"], 1)

                def scores(half, m, s, p, first, last):
                    qb, kt = SCORE_STEPS[m]
                    off = P * max(0, kt - TPB * qb)
                    if kt == 0:
                        pe.wait_ge(S["q_copy"], 8 * p + 4 * half + qb + 1)
                        pe.wait_ge(S[f"row_in{qb}"], DMA * (2 * p + half + 1))
                    if not (first and s < 3):
                        pe.wait_ge(S["probs_hi"], 2 * STEPS * p + same_bank_before(s) + 1)
                    out = ps[:, SCORE_BANK + s % 3, 0:BLK - off]
                    q = slice(BLK * qb + off, BLK * (qb + 1))
                    k = slice(kt * P, (kt + 1) * P)
                    pe.matmul(out, kh[:, k], qa[half][:, q], start=True, stop=False)
                    pe.matmul(out, kl[0:LD + 1, k], qc[half][:, q], start=False, stop=True).then_inc(S["scored"], 1)

                def use_latents(p, s):
                    half, m = s // STEPS, s % STEPS
                    qb, kt = SCORE_STEPS[m]
                    off = P * max(0, kt - TPB * qb)
                    pe.wait_ge(S["probs_hi"], 2 * STEPS * p + s + 1)
                    if ON_DVE[s]:
                        pe.wait_ge(S["lo_dve"], DVE_LOS * p + los_before(s + 1, True))
                    else:
                        pe.wait_ge(S["lo_pool"], POOL_LOS * p + los_before(s + 1, False))
                    if kt == 0:
                        n = 4 * half + qb
                        if not isinstance(p, int) or 8 * p + n >= 2:
                            pe.wait_ge(S["y_copied"], 8 * p + n - 1)
                    out = ps[:, Y_BANK + qb % 2, off:BLK]
                    b = s % RING
                    w = BLK - off
                    pe.matmul(out, va[:, kt, :], ph[:, b, 0:w], start=kt == 0, stop=False)
                    pe.matmul(out, vc[:, kt, :], ph[:, b, 0:w], start=False, stop=False)
                    pe.matmul(out, va[:, kt, :], pl[:, b, 0:w], start=False,
                              stop=kt == TPB * (qb + 1) - 1).then_inc(S["latent_used"], 1)

                def turn(p, first, last):
                    for s in range(2 * STEPS):
                        half, m = s // STEPS, s % STEPS
                        if not (last and half == 1):
                            split_no = 8 * p + 4 * (half + 1) + MAX_STEPS[m][0] // TPB
                            max_scores(1 - half, m, split_no, STEPS + 2 * STEPS * p + s)
                        for n, (_, kind, head, qb) in jobs_at(s, last):
                            job = FIRST_JOBS + NJOBS * p + n
                            if kind == "row":
                                row(qb, 8 * p + 4 * head + qb, job)
                            else:
                                project(p + 1, qb, job)
                        scores(half, m, s, p, first, last)
                        if s >= LAG:
                            use_latents(p, s - LAG)
                        elif not first:
                            use_latents(p - 1, 2 * STEPS + s - LAG)

                for qb in range(QB):
                    project(0, qb, qb)
                for m in range(STEPS):
                    max_scores(0, m, MAX_STEPS[m][0] // TPB, m, first=m < 2)
                    for qb in range(FIRST_ROWS):
                        if m == block_end(qb) + 2:
                            row(qb, qb, QB + qb)
                turns(pe, turn)
                for s in range(2 * STEPS - LAG, 2 * STEPS):
                    use_latents(PAIRS - 1, s)

            @block.scalar
            def _(act):
                def read_queries(pair, qb, job, first=False):
                    act.wait_ge(S["bank_made"], job + 1)
                    if not first:
                        act.wait_ge(S["q_hi"], 8 * (pair - 1) + 4 + qb + 1)
                        act.wait_ge(S["q_lo"], 8 * (pair - 1) + 4 + qb + 1)
                        act.wait_ge(S["q_copy"], 8 * (pair - 1) + 4 + qb + 1)
                    act.activation(q_raw[:, BLK * qb:BLK * (qb + 1)], ps[:, BANK, :], ACT.Copy).then_inc(S["bank_read"], 1)

                def read_row(head, half, qb, job):
                    act.wait_ge(S["bank_made"], job + 1)
                    if not isinstance(head, int) or head >= 1:
                        act.wait_ge(S[f"row_in{qb}"], DMA * head)
                    act.activation(neg_rows[:, qb, :], ps[0:TPB, BANK, 0:P], ACT.Copy).then_inc(S["bank_read"], 1)
                    act.wait_ge(S["bank_read"], job + 1)
                    act.dma_start(f32(qc[half][LD:LD + 1, BLK * qb:BLK * (qb + 1)]),
                                  f32(neg_rows[:, qb, :])).then_inc(S[f"row_in{qb}"], DMA)

                def copy_queries(half, qb, read, scored):
                    if read is not None:
                        act.wait_ge(S["bank_read"], read)
                    if scored is not None:
                        act.wait_ge(S["scored"], scored)
                    c = slice(BLK * qb, BLK * (qb + 1))
                    act.activation(qc[half][0:LD, c], q_raw[half * LD:(half + 1) * LD, c], ACT.Copy).then_inc(S["q_copy"], 1)

                def copy_sums(p, half, qb):
                    act.wait_ge(S["latent_used"], 2 * STEPS * p + STEPS * half + block_end(qb) + 1)
                    if not isinstance(p, int) or 2 * p + half >= 1:
                        act.wait_ge(S[f"stored{qb}"], DMA * (2 * p + half))
                    act.activation(y[:, qb, :], ps[:, Y_BANK + qb % 2, :], ACT.Copy).then_inc(S["y_copied"], 1)

                def turn(p, first, last):
                    for s in range(2 * STEPS):
                        block_jobs(copy_sums, s, LAG + 1, p, first)
                        qb, kt = SCORE_STEPS[s % STEPS]
                        w = BLK - P * max(0, kt - TPB * qb)
                        if is_diagonal(s):
                            act.wait_ge(S["masked"], DIAGONALS * p + diagonals_before(s + 1))
                        else:
                            act.wait_ge(S["scored"], 2 * STEPS * p + s + 1)
                        src = ps[:, SCORE_BANK + s % 3, 0:w]
                        if not (first and s < RING):
                            wait_lo(act, p, s - RING)
                        act.activation(pr[:, s % RING, 0:w], src, ACT.Exp).then_inc(S["probs"], 1)
                        if not (first and s < RING):
                            act.wait_ge(S["latent_used"], 2 * STEPS * p + s - RING + 1)
                        act.activation(ph[:, s % RING, 0:w], src, ACT.Exp).then_inc(S["probs_hi"], 1)
                        for n, (_, kind, head, jqb) in jobs_at(s, last):
                            job = FIRST_JOBS + NJOBS * p + n
                            if kind == "row":
                                read_row(2 * p + head, head % 2, jqb, job)
                            else:
                                read_queries(p + 1, jqb, job)
                        for n, (_, head, jqb) in splits_at(s, last):
                            copy_queries(head % 2, jqb, *split_waits(p, head, jqb, first))

                for qb in range(QB):
                    read_queries(0, qb, qb, first=True)
                for n in range(FIRST_SPLITS):
                    copy_queries(n // QB, n % QB, n % QB + 1, None)
                for qb in range(FIRST_ROWS):
                    read_row(0, 0, qb, QB + qb)
                turns(act, turn)
                late_jobs(copy_sums, LAG + 1)

            @block.gpsimd
            def _(pool):
                def split_lo(half, qb, no, los=None):
                    if los is not None:
                        pool.wait_ge(S["lo_pool"], los)
                    c = slice(BLK * qb, BLK * (qb + 1))
                    hi, lo = slice(half * LD, (half + 1) * LD), slice((1 - half) * LD, (2 - half) * LD)
                    pool.wait_ge(S["q_hi"], no + 1)
                    pool.tensor_tensor(qa[half][lo, c], q_raw[hi, c], f32(qa[half][hi, c]),
                                       ALU.subtract).then_inc(S["q_lo"], 1)
                    pool.wait_ge(S["q_lo"], no + 1)

                def turn(p, first, last):
                    for s in range(2 * STEPS):
                        if not ON_DVE[s]:
                            make_lo(pool, p, s, first, S["lo_pool"])
                        for n, (_, head, qb) in splits_at(s, last):
                            split_lo(head % 2, qb, FIRST_SPLITS + NSPLITS * p + n,
                                     POOL_LOS * p + los_before(s + 1, False))

                for n in range(FIRST_SPLITS):
                    split_lo(n // QB, n % QB, n)
                turns(pool, turn)

            @block.vector
            def _(dve):
                def split_hi(half, qb, read, scored):
                    dve.wait_ge(S["bank_read"], read)
                    if scored is not None:
                        dve.wait_ge(S["scored"], scored)
                    c = slice(BLK * qb, BLK * (qb + 1))
                    hi = slice(half * LD, (half + 1) * LD)
                    dve.tensor_copy(qa[half][hi, c], q_raw[hi, c]).then_inc(S["q_hi"], 1)

                def mask_scores(p, s):
                    src = ps[:, SCORE_BANK + s % 3, 0:P]
                    dve.wait_ge(S["scored"], 2 * STEPS * p + s + 1)
                    dve.tensor_tensor(src, src, T["mask_kq"][:, :], ALU.add).then_inc(S["masked"], 1)

                def invert(p, half, qb):
                    dve.wait_ge(S["sums_in"], DMA * (8 * p + 4 * half + qb + 1))
                    dve.reciprocal(sums[:, qb, :], sums[:, qb, :]).then_inc(S["recip"], 1)

                def divide(p, half, qb):
                    dve.wait_ge(S["recip_in"], DMA * (8 * p + 4 * half + qb + 1))
                    dve.tensor_tensor(y[0:LD, qb, :], y[0:LD, qb, :], rec[:, qb, :], ALU.mult).then_inc(S["normed"], 1)

                def turn(p, first, last):
                    for s in range(2 * STEPS):
                        half, m = s // STEPS, s % STEPS
                        if not (last and half == 1):
                            qb = MAX_STEPS[m][0] // TPB
                            h2, q2 = (half + 1, qb - 2) if qb >= 2 else (half, qb + 2)
                            kept = [j for j in BANK_JOBS if not (last and j[2] == 2)]
                            at = [k for k, j in enumerate(kept) if j[1:] == ("row", h2, q2)]
                            if at:
                                made = FIRST_JOBS + NJOBS * p + at[0] + 1
                            else:
                                made = FIRST_JOBS + NJOBS * p + row_job(h2, q2, last)
                            read_max(m, STEPS + 2 * STEPS * p + s, 8 * p + 4 * (half + 1) + qb, made)
                        if is_diagonal(s):
                            mask_scores(p, s)
                        for n, (_, head, qb) in splits_at(s, last):
                            split_hi(head % 2, qb, *split_waits(p, head, qb, first))
                        if s and ON_DVE[s - 1]:
                            make_lo(dve, p, s - 1, first, S["lo_dve"])
                        block_jobs(invert, s, INVERT_AFTER, p, first)
                        block_jobs(divide, s, DIVIDE_AFTER, p, first)

                def read_max(m, n, block_no, made):
                    i, c = MAX_STEPS[m]
                    j, qb = i % TPB, i // TPB
                    src = ps[:, MAX_BANK + m % 2, :]
                    dst = part[:, qb % 2, j, c:c + 1]
                    dve.wait_ge(S["max_scored"], n + 1)
                    w = BLK if c < qb else P * (j + 1)
                    if c == qb:
                        dve.tensor_tensor(src[:, w - P:w], src[:, w - P:w], T["mask_qk"][:, :],
                                          ALU.add).then_inc(S["max_masked"], 1)
                        dve.wait_ge(S["max_masked"], TPB * block_no + j + 1)
                    ins = dve.tensor_reduce(dst, src[:, 0:w], AX.X, ALU.max)
                    ins.then_inc(S["max_read"], 1)
                    if j == TPB - 1 and c == qb:
                        dve.wait_ge(S["max_read"], n + 1)
                        dve.tensor_reduce(mx[:, qb % 2, :], part[:, qb % 2, :, 0:qb + 1], AX.X,
                                          ALU.max).then_inc(S["part_max"], 1)
                        dve.wait_ge(S["part_max"], block_no + 1)
                        if made is not None:
                            dve.wait_ge(S["bank_made"], made)
                        dve.tensor_scalar(neg[:, qb % 2, :], mx[:, qb % 2, :], -1.0, None,
                                          ALU.mult).then_inc(S["neg_max"], 1)

                for n in range(FIRST_SPLITS):
                    split_hi(n // QB, n % QB, n % QB + 1, None)
                for m in range(STEPS):
                    qb = MAX_STEPS[m][0] // TPB
                    read_max(m, m, qb, QB + qb - 1 if qb >= 2 else None)
                turns(dve, turn)
                late_jobs(invert, INVERT_AFTER)
                late_jobs(divide, DIVIDE_AFTER)
        clear_semaphores(nc, S.values())




def shared_tensors(nc, ctx):
    def sb(name, shape, dt=F32):
        return ctx.enter_context(nc.sbuf_tensor(name, shape, dt))
    return {
        "ps": ctx.enter_context(nc.psum_tensor("ps", [P, 8, BLK], F32)),
        "ident": sb("ident", [P, P]), "minus_half": sb("minus_half", [P, TPB]),
        "n_hi": sb("n_hi", [P, PAIRS, D], F32R), "n_lo": sb("n_lo", [P, PAIRS, D], F32R),
    }


def attention_tensors(nc, ctx):
    def sb(name, shape, dt=F32):
        return ctx.enter_context(nc.sbuf_tensor(name, shape, dt))
    return {
        "mask_kq": sb("mask_kq", [P, P]), "mask_qk": sb("mask_qk", [P, P]),
        "m_hi": sb("m_hi", [P, PAIRS, DT, P], F32R), "m_lo": sb("m_lo", [P, PAIRS, DT, P], F32R),
        "wd_hi": sb("wd_hi", [P, DT, P], F32R), "wd_lo": sb("wd_lo", [P, DT, P], F32R),
        "xt_hi": sb("xt_hi", [P, DT, L], F32R), "xt_lo": sb("xt_lo", [P, DT, L], F32R),
        "k_hi": sb("k_hi", [P, L], F32R), "k_lo": sb("k_lo", [LD + 1, L], F32R),
        "v_hi": sb("v_hi", [P, KT, P], F32R), "v_lo": sb("v_lo", [P, KT, P], F32R),
    }


def build_mixture_weights(nc, W, w):
    with ExitStack() as ctx:
        def sb(name, shape, dt=F32):
            return ctx.enter_context(nc.sbuf_tensor(name, shape, dt))
        S = {n: ctx.enter_context(nc.semaphore("mw_" + n)) for n in ("up_in", "gate_in", "down_in", "small_in", "hi", "lo", "filled")}
        raw = {"up": sb("up_raw", [P, NE, DT, I]), "gate": sb("gate_raw", [P, E + 1, DT, I]),
               "down": sb("down_raw", [P, E + 1, DT, D]), "router": sb("router_raw", [P, ROUNDS, DT, E])}
        small = ["b_up", "b_gate", "b_down", "router_b", "gate_bias", "norm_w"]
        units = [("router", "small_in", slice(0, ROUNDS))] + [
            (k, s, slice(e, e + 2)) for k, s, n in (("up", "up_in", NE), ("gate", "gate_in", E), ("down", "down_in", E))
            for e in range(0, n, 2)] + [("gate", "gate_in", slice(E, E + 1)), ("down", "down_in", slice(E, E + 1))]
        total = {"small_in": DMA * (len(small) + ROUNDS), "up_in": DMA * (E + 2), "gate_in": DMA * (E + 1), "down_in": DMA * (E + 1)}
        with nc.Block() as block:
            @block.sync
            def _(sp):
                for k in small:
                    dst = W[k]
                    sp.dma_start(dst[tuple(slice(None) for _ in dst.shape)], w[k]).then_inc(S["small_in"], DMA)
                for c in range(ROUNDS):
                    sp.dma_start(raw["router"][:, c, :, :],
                                 w["router_w"][c].rearrange("(t p) e -> p t e", p=P)).then_inc(S["small_in"], DMA)
                for k, s, src, shared in (("up", "up_in", "exp_up", "share_up"), ("gate", "gate_in", "exp_gate", "share_gate"),
                                          ("down", "down_in", "exp_down", "share_down")):
                    for e in range(E):
                        sp.dma_start(raw[k][:, e, :, :], w[src][e].rearrange("(t p) i -> p t i", p=P)).then_inc(S[s], DMA)
                    for e in range(2 if k == "up" else 1):
                        sp.dma_start(raw[k][:, E + e, :, :],
                                     w[shared][:, e * I:(e + 1) * I].rearrange("(t p) i -> p t i", p=P)).then_inc(S[s], DMA)

            @block.scalar
            def _(act):
                for k, s, es in units:
                    act.wait_ge(S[s], total[s])
                    act.activation(W[k + "_hi"][:, es, :, :], raw[k][:, es, :, :], ACT.Copy).then_inc(S["hi"], 1)

            @block.vector
            def _(dve):
                for n, (k, s, es) in enumerate(units):
                    dve.wait_ge(S["hi"], n + 1)
                    dve.tensor_tensor(W[k + "_lo"][:, es, :, :], raw[k][:, es, :, :], f32(W[k + "_hi"][:, es, :, :]),
                                      ALU.subtract).then_inc(S["lo"], 1)

            @block.gpsimd
            def _(pool):
                pool.memset(W["earlier"][:, :, :, :], 1.0).then_inc(S["filled"], 1)
                pool.wait_ge(S["filled"], 1)
                pool.affine_select(out=W["earlier"][:, :, :, :], in_=W["earlier"][:, :, :, :], compare_op=ALU.is_gt, fill=0.0,
                                   base=0, pattern=[[0, TPB], [1, E], [-1, E]], channel_multiplier=0).then_inc(S["filled"], 1)
        clear_semaphores(nc, S.values())


def build_tokens(nc, W, F, y_next, x_next, out_block, t, inputs):
    with ExitStack() as ctx:
        names = ["y_hi", "y_lo", "proj", "x1", "stats", "mean", "var", "rstd", "x_norm", "turned", "xt_hi", "xt_lo",
                 "up", "h", "h_hi", "h_lo", "gate", "silu", "g", "g_hi", "g_lo", "down", "sum",
                 "routed", "route", "diff", "tanh", "weights", "w_turned", "w_copied", "bias", "seeded",
                 "squares", "scale_var", "scale", "scaled", "out_ready", "stored", "ones"]
        S = {n: ctx.enter_context(nc.semaphore(f"f{inputs['tag']}_" + n)) for n in names}
        y_in, x_in = inputs["y_in"], inputs["x_in"]
        ps, ident = W["ps"], W["ident"]
        UP, GATE, DOWN, AUX = 0, 2, 4, 6
        h, s_, xf, x1, acc = F["h"], F["s"], F["xf"], F["x1"], F["acc"]
        y_raw, x_raw, xth, xtl = F["y_raw"], F["x_raw"], F["xt_hi"], F["xt_lo"]
        parts = F["parts"]
        y_hi, y_lo = (parts[:, i].rearrange("p k m n -> p (k m) n") for i in range(2))
        H_HI, H_LO, G_HI, G_LO = range(4)
        full = slice(None)

        with nc.Block() as block:
            @block.sync
            def _(sp):
                if y_next is not None:
                    sp.wait_ge(S["y_lo"], PAIRS)
                    sp.dma_start(y_raw[:, :, :], y_next).then_inc(y_in, DMA)
                    sp.wait_ge(S["x1"], 2)
                    sp.dma_start(x_raw[:, :, :], x_next).then_inc(x_in, DMA)
                for j in range(TPB):
                    sp.wait_ge(S["out_ready"], j + 1)
                    sp.dma_start(out_block[:, j, :], xf[:, j, :]).then_inc(S["stored"], DMA)
                sp.wait_ge(S["stored"], DMA * TPB)

            @block.tensor
            def _(pe):
                def turn_tokens(c):
                    pe.wait_ge(S["xt_lo"], DT * c)
                    if c:
                        pe.wait_ge(S["seeded"], 2 * c)
                    for j in range(TPB):
                        pe.wait_ge(S["x_norm"] if c == 0 else S["scaled"], j + 1)
                        for dt in range(DT):
                            mm = pe.transpose(ps[:, AUX + dt, j * P:(j + 1) * P], xf[:, j, dt * P:(dt + 1) * P], ident[:, :])
                    mm.then_inc(S["turned"], 1)

                def wide(out, w_hi, w_lo, m, hi, lo):
                    terms = [(a, b, dt) for a, b in ((w_hi, hi), (w_lo, hi), (w_hi, lo)) for dt in range(DT)]
                    for n, (a, b, dt) in enumerate(terms):
                        mm = pe.matmul(out, a[:, dt, m * P:(m + 1) * P], b[:, dt, :], start=n == 0, stop=n == len(terms) - 1)
                    return mm

                def up(c, e):
                    q = NE * c + e
                    if e == 0:
                        pe.wait_ge(S["xt_hi"], DT * (c + 1))
                        pe.wait_ge(S["xt_lo"], DT * (c + 1))
                    for m in range(2):
                        if q:
                            pe.wait_ge(S["h"], 2 * (q - 1) + m + 1)
                        wide(ps[:, UP + m, :], W["up_hi"][:, e], W["up_lo"][:, e], m, xth, xtl).then_inc(S["up"], 1)

                def gate(c, e):
                    q, k = NE * c + e, min(e, E)
                    pe.wait_ge(S["h_hi"], 2 * (q + 1))
                    pe.wait_ge(S["h_lo"], 2 * (q + 1))
                    for m in range(2):
                        if q:
                            pe.wait_ge(S["silu"], 2 * (q - 1) + m + 1)
                        wide(ps[:, GATE + m, :], W["gate_hi"][:, k], W["gate_lo"][:, k], m,
                             parts[:, q % 2, H_HI], parts[:, q % 2, H_LO]).then_inc(S["gate"], 1)

                def down(c, e):
                    q, k = NE * c + e, min(e, E)
                    pe.wait_ge(S["g_hi"], 2 * (q + 1))
                    pe.wait_ge(S["g_lo"], 2 * (q + 1))
                    for j in range(TPB):
                        if j % 2 == 0:
                            if q:
                                pe.wait_ge(S["sum"], TPB * (q - 1) + j + 2)
                            else:
                                pe.wait_ge(S["x1"], 2)
                        terms = [(a, b, dt) for a, b in ((G_HI, "hi"), (G_HI, "lo"), (G_LO, "hi")) for dt in range(DT)]
                        for n, (a, b, dt) in enumerate(terms):
                            mm = pe.matmul(ps[:, DOWN + j // 2, (j % 2) * D:(j % 2 + 1) * D],
                                           parts[:, q % 2, a, dt, j * P:(j + 1) * P], W["down_" + b][:, k, dt, :],
                                           start=n == 0, stop=n == len(terms) - 1)
                        if j % 2:
                            mm.then_inc(S["down"], 1)

                def route(c):
                    for j in range(TPB):
                        terms = [(a, b, dt) for a, b in ((xth, "hi"), (xth, "lo"), (xtl, "hi")) for dt in range(DT)]
                        for n, (a, b, dt) in enumerate(terms):
                            mm = pe.matmul(ps[:, AUX, j * NE:j * NE + E], a[:, dt, j * P:(j + 1) * P],
                                           W["router_" + b][:, c, dt, :], start=n == 0, stop=n == len(terms) - 1)
                    mm.then_inc(S["routed"], 1)

                def turn_weights(c):
                    pe.wait_ge(S["weights"], c + 1)
                    for j in range(TPB):
                        mm = pe.transpose(ps[0:NE, AUX + 1, j * P:(j + 1) * P], F["weights"][:, j, :], ident[:, :])
                    mm.then_inc(S["w_turned"], 1)

                def biases(c):
                    pe.wait_ge(S["w_copied"], c + 1)
                    for j in range(TPB):
                        mm = pe.matmul(ps[:, AUX + j // 2, (j % 2) * D:(j % 2 + 1) * D], F["weights_t"][:, j * P:(j + 1) * P],
                                       W["b_down"][:, :], start=True, stop=True)
                        if j % 2:
                            mm.then_inc(S["bias"], 1)

                for pair in range(PAIRS):
                    pe.wait_ge(S["y_hi"], pair + 1)
                    pe.wait_ge(S["y_lo"], pair + 1)
                    for j in range(TPB):
                        for n, (a, b) in enumerate(((y_hi, "hi"), (y_hi, "lo"), (y_lo, "hi"))):
                            mm = pe.matmul(ps[:, DOWN + j // 2, (j % 2) * D:(j % 2 + 1) * D], a[:, pair, j * P:(j + 1) * P],
                                           W["n_" + b][:, pair, :], start=pair == 0 and n == 0 and j % 2 == 0,
                                           stop=pair == PAIRS - 1 and n == 2, skip_group_check=True)
                        if pair == PAIRS - 1 and j % 2:
                            mm.then_inc(S["proj"], 1)
                for c in range(ROUNDS):
                    turn_tokens(c)
                    for e in range(NE + 2):
                        if e < NE:
                            up(c, e)
                        if e == 0:
                            route(c)
                        if 1 <= e <= NE:
                            gate(c, e - 1)
                        if e == 1:
                            turn_weights(c)
                        if e == 2:
                            biases(c)
                        if e >= 2:
                            down(c, e - 2)

            @block.scalar
            def _(act):
                def hidden(c, e):
                    q = NE * c + e
                    for m in range(2):
                        act.wait_ge(S["up"], 2 * q + m + 1)
                        if q >= 2:
                            act.wait_ge(S["g"], 2 * (q - 2) + m + 1)
                            act.wait_ge(S["h_lo"], 2 * (q - 2) + m + 1)
                        act.activation(h[:, q % 2, m, :], ps[:, UP + m, :], ACT.Identity,
                                       bias=W["b_up"][:, 2 * e + m:2 * e + m + 1]).then_inc(S["h"], 1)

                def silu(c, e):
                    q = NE * c + e
                    for m in range(2):
                        act.wait_ge(S["gate"], 2 * q + m + 1)
                        if q >= 2:
                            act.wait_ge(S["g_lo"], 2 * (q - 2) + m + 1)
                        act.activation(s_[:, q % 2, m, :], ps[:, GATE + m, :], ACT.Silu,
                                       bias=W["b_gate"][:, 2 * e + m:2 * e + m + 1]).then_inc(S["silu"], 1)

                act.wait_ge(y_in, DMA * (t + 1))
                for pair in range(PAIRS):
                    act.activation(y_hi[:, pair, :], y_raw[:, pair, :], ACT.Copy).then_inc(S["y_hi"], 1)
                for c in range(ROUNDS):
                    act.wait_ge(S["turned"], c + 1)
                    for dt in range(DT):
                        act.activation(xth[:, dt, :], ps[:, AUX + dt, :], ACT.Copy).then_inc(S["xt_hi"], 1)
                    for e in range(NE + 1):
                        if e < NE:
                            hidden(c, e)
                        if e == 1:
                            act.wait_ge(S["diff"], c + 1)
                            act.activation(F["tanh"][:, :, :], F["diff"][:, :, :], ACT.Tanh, scale=0.5).then_inc(S["tanh"], 1)
                        if e >= 1:
                            silu(c, e - 1)
                        if e == 1:
                            act.wait_ge(S["w_turned"], c + 1)
                            act.activation(F["weights_t"][:, :], ps[0:NE, AUX + 1, :], ACT.Copy).then_inc(S["w_copied"], 1)

            @block.gpsimd
            def _(pool):
                def rsqrt(dst, var, src, a, b, ready, n, var_done, done):
                    pool.wait_ge(ready, n)
                    pool.tensor_scalar(var, src, a, b, ALU.mult, ALU.add).then_inc(var_done, 1)

                for pair in range(1, PAIRS, 2):
                    pool.wait_ge(S["y_lo"], pair)
                    pool.wait_ge(S["y_hi"], pair + 1)
                    pool.tensor_tensor(y_lo[:, pair, :], y_raw[:, pair, :], f32(y_hi[:, pair, :]), ALU.subtract).then_inc(S["y_lo"], 1)
                pool.wait_ge(S["mean"], TPB)
                pool.tensor_scalar(F["var"][:, :, :], F["mv"][:, :, 1:2], LN_EPS, None, ALU.add).then_inc(S["var"], 1)
                pool.wait_ge(S["var"], 1)
                pool.tensor_tensor(F["rs"][:, :, :], F["var"][:, :, :], W["minus_half"][:, :, None], ALU.pow).then_inc(S["rstd"], 1)
                for c in range(ROUNDS):
                    for e in range(NE + 1):
                        if e < NE:
                            q = NE * c + e
                            for m in range(2):
                                pool.wait_ge(S["h_hi"], 2 * q + m + 1)
                                pool.tensor_tensor(parts[:, q % 2, H_LO, m, :], h[:, q % 2, m, :],
                                                   f32(parts[:, q % 2, H_HI, m, :]), ALU.subtract).then_inc(S["h_lo"], 1)
                        if e >= 1:
                            q = NE * c + e - 1
                            for m in range(2):
                                pool.wait_ge(S["g_hi"], 2 * q + m + 1)
                                pool.tensor_tensor(parts[:, q % 2, G_LO, m, :], s_[:, q % 2, m, :],
                                                   f32(parts[:, q % 2, G_HI, m, :]), ALU.subtract).then_inc(S["g_lo"], 1)
                    for j in range(TPB):
                        n = TPB * c + j
                        pool.wait_ge(S["squares"], n + 1)
                        pool.tensor_scalar(F["var"][:, j, :], F["ss"][:, j, :], 1.0 / D, RMS_EPS, ALU.mult,
                                           ALU.add).then_inc(S["scale_var"], 1)
                        pool.wait_ge(S["scale_var"], n + 1)
                        pool.tensor_tensor(F["rs"][:, j, :], F["var"][:, j, :], W["minus_half"][:, 0:1], ALU.pow).then_inc(S["scale"], 1)

            @block.vector
            def _(dve):
                steps = [0]

                def route_step(ins):
                    steps[0] += 1
                    ins.then_inc(S["route"], 1)
                    dve.wait_ge(S["route"], steps[0])

                def choose(c):
                    g, b, r, pair = F["g"], F["biased"], F["rank"], F["beaten"]
                    eq = F["equal"]
                    src = ps[:, AUX, 0:TPB * NE].rearrange("p (j e) -> p j e", e=NE)[:, :, 0:E]
                    dve.wait_ge(S["routed"], c + 1)
                    route_step(dve.tensor_tensor(g[:, :, :], src, W["router_b"][:, c, None, :].broadcast_to([P, TPB, E]), ALU.add))
                    route_step(dve.tensor_tensor(b[:, :, :], g[:, :, :], W["gate_bias"][:, c, None, :].broadcast_to([P, TPB, E]), ALU.add))
                    other = b[:, :, None, :].broadcast_to([P, TPB, E, E])
                    own = b[:, :, :, None].broadcast_to([P, TPB, E, E])
                    route_step(dve.tensor_tensor(pair[:, :, :, :], other, own, ALU.is_gt))
                    route_step(dve.tensor_tensor(eq[:, :, :, :], other, own, ALU.is_equal))
                    route_step(dve.tensor_tensor(eq[:, :, :, :], eq[:, :, :, :], W["earlier"][:, :, :, :], ALU.mult))
                    route_step(dve.tensor_tensor(pair[:, :, :, :], pair[:, :, :, :], eq[:, :, :, :], ALU.add))
                    route_step(dve.tensor_reduce(r[:, :, :], pair[:, :, :, :], AX.X, ALU.add))
                    route_step(dve.tensor_scalar(F["chosen"][:, :, :], r[:, :, :], 2.0, None, ALU.is_lt))
                    route_step(dve.tensor_tensor(b[:, :, :], F["chosen"][:, :, :], g[:, :, :], ALU.mult))
                    route_step(dve.tensor_reduce(F["both"][:, :], b[:, :, :], AX.X, ALU.add))
                    route_step(dve.tensor_tensor(b[:, :, :], g[:, :, :], F["both"][:, :, None].broadcast_to([P, TPB, E]), ALU.subtract))
                    dve.tensor_tensor(F["diff"][:, :, :], b[:, :, :], g[:, :, :], ALU.add).then_inc(S["diff"], 1)

                def weigh(c):
                    dve.wait_ge(S["tanh"], c + 1)
                    route_step(dve.tensor_scalar(F["tanh"][:, :, :], F["tanh"][:, :, :], 0.5, 0.5, ALU.mult, ALU.add))
                    dve.tensor_tensor(F["weights"][:, :, 0:E], F["tanh"][:, :, :], F["chosen"][:, :, :],
                                      ALU.mult).then_inc(S["weights"], 1)

                def split_hidden(c, e):
                    q = NE * c + e
                    for m in range(2):
                        dve.wait_ge(S["h"], 2 * q + m + 1)
                        if q >= 2:
                            dve.wait_ge(S["gate"], 2 * (q - 1))
                        dve.tensor_copy(parts[:, q % 2, H_HI, m, :], h[:, q % 2, m, :]).then_inc(S["h_hi"], 1)

                def gated(c, e):
                    q = NE * c + e
                    for m in range(2):
                        dve.wait_ge(S["silu"], 2 * q + m + 1)
                        dve.tensor_tensor(s_[:, q % 2, m, :], s_[:, q % 2, m, :], h[:, q % 2, m, :], ALU.mult).then_inc(S["g"], 1)
                    for m in range(2):
                        dve.wait_ge(S["g"], 2 * q + m + 1)
                        if q >= 2:
                            dve.wait_ge(S["down"], 2 * (q - 1))
                        dve.tensor_copy(parts[:, q % 2, G_HI, m, :], s_[:, q % 2, m, :]).then_inc(S["g_hi"], 1)

                def add_expert(c, e):
                    q = NE * c + e
                    for j in range(TPB):
                        dve.wait_ge(S["down"], 2 * q + j // 2 + 1)
                        if e:
                            dve.wait_ge(S["sum"], TPB * (q - 1) + j + 1)
                        else:
                            dve.wait_ge(S["seeded"], 2 * c + j // 2 + 1)
                        dve.scalar_tensor_tensor(out=acc[:, j, :], in0=ps[:, DOWN + j // 2, (j % 2) * D:(j % 2 + 1) * D],
                                                 scalar=F["weights"][:, j, e:e + 1], in1=acc[:, j, :],
                                                 op0=ALU.mult, op1=ALU.add).then_inc(S["sum"], 1)

                dve.memset(F["weights"][:, :, E:NE], 1.0).then_inc(S["ones"], 1)
                for pair in range(0, PAIRS, 2):
                    dve.wait_ge(S["y_hi"], pair + 1)
                    dve.wait_ge(S["y_lo"], pair)
                    dve.tensor_tensor(y_lo[:, pair, :], y_raw[:, pair, :], f32(y_hi[:, pair, :]), ALU.subtract).then_inc(S["y_lo"], 1)
                dve.wait_ge(x_in, DMA * (t + 1))
                for k in range(2):
                    dve.wait_ge(S["proj"], k + 1)
                    two = (full, slice(2 * k, 2 * k + 2), full)
                    dve.tensor_tensor(x1[two], ps[:, DOWN + k, :].rearrange("p (j d) -> p j d", d=D), x_raw[two],
                                      ALU.add).then_inc(S["x1"], 1)
                for j in range(TPB):
                    dve.wait_ge(S["x1"], j // 2 + 1)
                    dve.bn_stats(F["st"][:, j, :], x1[:, j, :]).then_inc(S["stats"], 1)
                for j in range(TPB):
                    dve.wait_ge(S["stats"], j + 1)
                    dve.bn_aggr(F["mv"][:, j, :], F["st"][:, j, :]).then_inc(S["mean"], 1)
                dve.wait_ge(S["rstd"], 1)
                for j in range(TPB):
                    dve.tensor_scalar(xf[:, j, :], x1[:, j, :], F["mv"][:, j, 0:1], F["rs"][:, j, :],
                                      ALU.subtract, ALU.mult).then_inc(S["x_norm"], 1)
                for c in range(ROUNDS):
                    for dt in range(DT):
                        dve.wait_ge(S["xt_hi"], DT * c + dt + 1)
                        dve.tensor_tensor(xtl[:, dt, :], ps[:, AUX + dt, :], f32(xth[:, dt, :]), ALU.subtract).then_inc(S["xt_lo"], 1)
                    for e in range(NE + 2):
                        if e < NE:
                            split_hidden(c, e)
                        if e == 0:
                            choose(c)
                        if e == 1:
                            weigh(c)
                        if 1 <= e <= NE:
                            gated(c, e - 1)
                        if e == 2:
                            for k in range(2):
                                dve.wait_ge(S["bias"], 2 * c + k + 1)
                                two = (full, slice(2 * k, 2 * k + 2), full)
                                dve.tensor_tensor(acc[two], ps[:, AUX + k, :].rearrange("p (j d) -> p j d", d=D), xf[two],
                                                  ALU.add).then_inc(S["seeded"], 1)
                        if e >= 2:
                            add_expert(c, e - 2)
                    for j in range(TPB):
                        n = TPB * c + j
                        dve.wait_ge(S["sum"], TPB * (NE * (c + 1) - 1) + j + 1)
                        if n:
                            dve.wait_ge(S["squares"], n)
                        dve.tensor_tensor_reduce(F["junk"][:, :], acc[:, j, :], acc[:, j, :], 1.0, 0.0, ALU.mult, ALU.add,
                                                 F["ss"][:, j, :]).then_inc(S["squares"], 1)
                    for j in range(TPB):
                        n = TPB * c + j
                        dve.wait_ge(S["scale"], n + 1)
                        dve.scalar_tensor_tensor(out=xf[:, j, :], in0=acc[:, j, :], scalar=F["rs"][:, j, :],
                                                 in1=W["norm_w"][:, c, :], op0=ALU.mult, op1=ALU.mult).then_inc(S["scaled"], 1)
                        if c == ROUNDS - 1:
                            dve.wait_ge(S["scaled"], n + 1)
                            dve.tensor_tensor(xf[:, j, :], xf[:, j, :], x1[:, j, :], ALU.add).then_inc(S["out_ready"], 1)
        clear_semaphores(nc, S.values())


def build_mixture(nc, W, w, y_dram, out):
    with ExitStack() as ctx:
        def sb(name, shape, dt=F32):
            return ctx.enter_context(nc.sbuf_tensor(name, shape, dt))
        W = dict(W)
        for k, n in (("up", NE), ("gate", E + 1), ("down", E + 1)):
            W[k + "_hi"] = sb(k + "_hi", [P, n, DT, I], F32R)
            W[k + "_lo"] = sb(k + "_lo", [P, n, DT, I], F32R)
        W["router_hi"] = sb("router_hi", [P, ROUNDS, DT, E], F32R)
        W["router_lo"] = sb("router_lo", [P, ROUNDS, DT, E], F32R)
        W["b_up"], W["b_gate"] = sb("b_up", [P, 2 * NE]), sb("b_gate", [P, 2 * NE])
        W["b_down"] = sb("b_down", [NE, D])
        W["router_b"], W["gate_bias"] = sb("router_b", [P, ROUNDS, E]), sb("gate_bias", [P, ROUNDS, E])
        W["norm_w"] = sb("norm_w", [P, ROUNDS, D])
        W["earlier"] = sb("earlier", [P, TPB, E, E])
        build_mixture_weights(nc, W, w)
        F = {"y_raw": sb("y_raw", [P, PAIRS, BLK]), "x_raw": sb("x_raw", [P, TPB, D]), "x1": sb("x1", [P, TPB, D]),
             "xf": sb("xf", [P, TPB, D]), "acc": sb("acc", [P, TPB, D]),
             "parts": sb("parts", [P, 2, 4, 2, BLK], F32R), "h": sb("h", [P, 2, 2, BLK]), "s": sb("s", [P, 2, 2, BLK]),
             "xt_hi": sb("xft_hi", [P, DT, BLK], F32R), "xt_lo": sb("xft_lo", [P, DT, BLK], F32R),
             "st": sb("st", [P, TPB, 6]), "mv": sb("mv", [P, TPB, 2]), "var": sb("var", [P, TPB, 1]),
             "rs": sb("rs", [P, TPB, 1]), "ss": sb("ss", [P, TPB, 1]), "junk": sb("fjunk", [P, D], BF16),
             "g": sb("g", [P, TPB, E]), "biased": sb("biased", [P, TPB, E]), "rank": sb("rank", [P, TPB, E]),
             "chosen": sb("chosen", [P, TPB, E]), "both": sb("both", [P, TPB]), "diff": sb("diff", [P, TPB, E]),
             "tanh": sb("tanh", [P, TPB, E]), "beaten": sb("beaten", [P, TPB, E, E]), "equal": sb("equal", [P, TPB, E, E]),
             "weights": sb("weights", [P, TPB, NE]), "weights_t": sb("weights_t", [NE, BLK])}
        y_in = ctx.enter_context(nc.semaphore("y_in"))
        x_in = ctx.enter_context(nc.semaphore("x_in"))
        x_v = w["x"].rearrange("b (q j p) d -> (b q) p j d", p=P, j=TPB)
        out_v = out.rearrange("b (q j p) d -> (b q) p j d", p=P, j=TPB)
        y_v = y_dram.rearrange("b q p h n -> (b q) p h n")
        nc.sync.dma_start(F["y_raw"][:, :, :], y_v[0]).then_inc(y_in, DMA)
        nc.sync.dma_start(F["x_raw"][:, :, :], x_v[0]).then_inc(x_in, DMA)
        with nc.Fori(0, NBLK - 1) as t:
            build_tokens(nc, W, F, y_v[t + 1], x_v[t + 1], out_v[t], t, {"y_in": y_in, "x_in": x_in, "tag": "a"})
        build_tokens(nc, W, F, None, None, out_v[NBLK - 1], NBLK - 1, {"y_in": y_in, "x_in": x_in, "tag": "b"})


def build(nc, w, out):
    y_dram = nc.dram_tensor("y_latent", [B, QB, P, PAIRS, BLK], F32).ap()
    recip_rows = nc.dram_tensor("recip_rows", [QB, P, TPB], F32).ap()
    with ExitStack() as ctx:
        T = shared_tensors(nc, ctx)
        with ExitStack() as attention:
            A = dict(T) | attention_tensors(nc, attention)
            build_weights(nc, A, w)
            with nc.Fori(0, B) as b:
                build_latents(nc, A, w["x"][b])
                nc.disable_value_cache = True
                build_attention(nc, A, y_dram[b], recip_rows)
                nc.disable_value_cache = False
        build_mixture(nc, T, w, y_dram, out)


def kernel(L0_attn_x_bld, L0_attn_Wq, L0_attn_Wkv_down, L0_attn_Wk_up, L0_attn_Wv_up, L0_attn_Wout,
           L0_ffn_router_W, L0_ffn_router_b, L0_ffn_gate_bias, L0_ffn_exp_Wup, L0_ffn_exp_bup, L0_ffn_exp_Wg,
           L0_ffn_exp_bg, L0_ffn_exp_Wdown, L0_ffn_exp_bdown, L0_ffn_share_Wup, L0_ffn_share_bup, L0_ffn_share_Wg,
           L0_ffn_share_bg, L0_ffn_share_Wdown, L0_ffn_share_bdown, L0_ffn_norm_w):
    import concourse.bacc as bacc
    from concourse.bass_utils import run_bass_kernel_spmd as run

    def per_partition(*biases):
        rows = np.concatenate([np.asarray(b).reshape(-1, 2, P) for b in biases])
        return rows.transpose(2, 0, 1).reshape(P, -1)

    def every_partition(a):
        return np.broadcast_to(np.asarray(a)[None], (P, *np.asarray(a).shape))

    a = np.asarray
    arrays = {
        "x": a(L0_attn_x_bld), "wqT": a(L0_attn_Wq).transpose(1, 2, 0), "wkT": a(L0_attn_Wk_up).transpose(1, 2, 0),
        "wvT": a(L0_attn_Wv_up).transpose(1, 2, 0), "wout": a(L0_attn_Wout), "wdown": a(L0_attn_Wkv_down),
        "router_w": a(L0_ffn_router_W), "router_b": every_partition(L0_ffn_router_b),
        "gate_bias": every_partition(L0_ffn_gate_bias), "norm_w": every_partition(L0_ffn_norm_w),
        "exp_up": a(L0_ffn_exp_Wup), "exp_gate": a(L0_ffn_exp_Wg), "exp_down": a(L0_ffn_exp_Wdown),
        "share_up": a(L0_ffn_share_Wup), "share_gate": a(L0_ffn_share_Wg), "share_down": a(L0_ffn_share_Wdown),
        "b_up": per_partition(L0_ffn_exp_bup, L0_ffn_share_bup),
        "b_gate": per_partition(L0_ffn_exp_bg, L0_ffn_share_bg, L0_ffn_share_bg),
        "b_down": np.concatenate([a(L0_ffn_exp_bdown), a(L0_ffn_share_bdown)[None], a(L0_ffn_share_bdown)[None]]),
    }
    arrays = {n: np.ascontiguousarray(v) for n, v in arrays.items()}
    nc = bacc.Bacc("TRN2", target_bir_lowering=False, num_devices=1)
    w = {n: nc.dram_tensor("in_" + n, v.shape, mybir.dt.from_np(v.dtype), kind="ExternalInput").ap() for n, v in arrays.items()}
    out = nc.dram_tensor("out", (B, L, D), F32, kind="ExternalOutput").ap()
    build(nc, w, out)
    r = run(nc, [{"in_" + n: v for n, v in arrays.items()}], core_ids=[0])
    return r.results[0]["out"]
```

```python
from contextlib import ExitStack

import numpy as np
import concourse.bass as bass
from concourse import mybir

F32 = mybir.dt.float32
F32R = mybir.dt.float32r
BF16 = mybir.dt.bfloat16
ALU = mybir.AluOpType
ACT = mybir.ActivationFunctionType
AX = mybir.AxisListType

P = 128
B, L, D = 2, 2048, 256
H, HD, LD = 16, 64, 64
E, I = 6, 256
NE = 8
ROUNDS = 2
DT = D // P
BLK = 512
TPB = BLK // P
QB = L // BLK
KT = L // P
PAIRS = H // 2
NBLK = B * QB
SCALE = float(HD) ** -0.5
MASK = -1.0e30
LN_EPS, RMS_EPS = 1e-5, 1e-6
DMA = 16

SCORE_STEPS = [(qb, kt) for qb in range(QB) for kt in range(TPB * (qb + 1))]
MAX_STEPS = [(TPB * qb + j, c) for qb in range(QB) for j in range(TPB) for c in range(qb + 1)]
STEPS = len(SCORE_STEPS)
INVERT_AFTER = 8
DIVIDE_AFTER = 13
LAG = 4
RING = 5


def f32(ap):
    return ap.bitcast(F32)


def clear_semaphores(nc, sems):
    for s in sems:
        nc.sync.sem_clear(s)
    nc.all_engine_barrier()


def build_weights(nc, T, w):
    with ExitStack() as ctx:
        def sb(name, shape, dt=F32):
            return ctx.enter_context(nc.sbuf_tensor(name, shape, dt))
        names = ["loaded", "zeroed", "made", "m_ready", "n_ready", "hi_done", "lo_done"]
        S = {n: ctx.enter_context(nc.semaphore("w_" + n)) for n in names}
        wq = sb("wq", [HD, H, D])
        wk = sb("wk", [HD, H, LD])
        wv = sb("wv", [HD, H, LD])
        wo = sb("wo", [HD, H, D])
        wd = sb("wd", [P, DT, LD])
        ps = T["ps"]
        with nc.Block() as block:
            @block.sync
            def _(sp):
                sp.dma_start(wq[:, :, :], w["wqT"].rearrange("h k d -> k h d")).then_inc(S["loaded"], DMA)
                sp.dma_start(wk[:, :, :], w["wkT"].rearrange("h k c -> k h c")).then_inc(S["loaded"], DMA)
                sp.dma_start(wv[:, :, :], w["wvT"].rearrange("h k c -> k h c")).then_inc(S["loaded"], DMA)
                sp.dma_start(wo[:, :, :], w["wout"].rearrange("h k d -> k h d")).then_inc(S["loaded"], DMA)
                sp.dma_start(wd[:, :, :], w["wdown"].rearrange("(t p) c -> p t c", p=P)).then_inc(S["loaded"], DMA)

            @block.gpsimd
            def _(pool):
                pool.memset(T["ident"][:, :], 0.0).then_inc(S["zeroed"], 1)
                pool.memset(T["mask_kq"][:, :], 0.0).then_inc(S["zeroed"], 1)
                pool.memset(T["mask_qk"][:, :], 0.0).then_inc(S["zeroed"], 1)
                pool.memset(T["minus_half"][:, :], -0.5).then_inc(S["zeroed"], 1)
                pool.wait_ge(S["zeroed"], 4)
                pool.affine_select(out=T["ident"][:, :], in_=T["ident"][:, :], compare_op=ALU.not_equal, fill=1.0,
                                   base=0, pattern=[[-1, P]], channel_multiplier=1).then_inc(S["made"], 1)
                for mask, sign in ((T["mask_kq"], 1), (T["mask_qk"], -1)):
                    pool.affine_select(out=mask[:, :], in_=mask[:, :], compare_op=ALU.is_ge, fill=MASK,
                                       base=0, pattern=[[sign, P]], channel_multiplier=-sign).then_inc(S["made"], 1)

            @block.tensor
            def _(pe):
                pe.wait_ge(S["loaded"], 5 * DMA)
                for dt in range(DT):
                    for h in range(H):
                        mm = pe.matmul(ps[:, 2 * dt + h // 8, (h % 8) * LD:(h % 8 + 1) * LD],
                                       wq[:, h, dt * P:(dt + 1) * P], wk[:, h, :], start=True, stop=True)
                mm.then_inc(S["m_ready"], 1)
                for h in range(H):
                    half, pr = h % 2, h // 2
                    mm = pe.matmul(ps[half * LD:(half + 1) * LD, 4 + pr // 2, (pr % 2) * D:(pr % 2 + 1) * D],
                                   wv[:, h, :], wo[:, h, :], start=True, stop=True)
                mm.then_inc(S["n_ready"], 1)

            @block.scalar
            def _(act):
                act.wait_ge(S["m_ready"], 1)
                for dt in range(DT):
                    for b2 in range(2):
                        act.activation(T["m_hi"][:, 4 * b2:4 * b2 + 4, dt, :], ps[:, 2 * dt + b2, :].rearrange(
                            "p (a c) -> p a c", c=P), ACT.Copy, scale=SCALE).then_inc(S["hi_done"], 1)
                act.wait_ge(S["n_ready"], 1)
                for b2 in range(4):
                    act.activation(T["n_hi"][:, 2 * b2:2 * b2 + 2, :], ps[:, 4 + b2, :].rearrange(
                        "p (a c) -> p a c", c=D), ACT.Copy).then_inc(S["hi_done"], 1)
                for half in range(2):
                    act.activation(T["wd_hi"][:, :, half * LD:(half + 1) * LD], wd[:, :, :],
                                   ACT.Copy).then_inc(S["hi_done"], 1)

            @block.vector
            def _(dve):
                n = 0
                for dt in range(DT):
                    for b2 in range(2):
                        n += 1
                        dve.wait_ge(S["hi_done"], n)
                        dve.scalar_tensor_tensor(
                            out=T["m_lo"][:, 4 * b2:4 * b2 + 4, dt, :],
                            in0=ps[:, 2 * dt + b2, :].rearrange("p (a c) -> p a c", c=P), scalar=SCALE,
                            in1=f32(T["m_hi"][:, 4 * b2:4 * b2 + 4, dt, :]),
                            op0=ALU.mult, op1=ALU.subtract).then_inc(S["lo_done"], 1)
                for b2 in range(4):
                    n += 1
                    dve.wait_ge(S["hi_done"], n)
                    dve.tensor_tensor(T["n_lo"][:, 2 * b2:2 * b2 + 2, :],
                                      ps[:, 4 + b2, :].rearrange("p (a c) -> p a c", c=D),
                                      f32(T["n_hi"][:, 2 * b2:2 * b2 + 2, :]), ALU.subtract).then_inc(S["lo_done"], 1)
                for half in range(2):
                    n += 1
                    dve.wait_ge(S["hi_done"], n)
                    dve.tensor_tensor(T["wd_lo"][:, :, half * LD:(half + 1) * LD], wd[:, :, :],
                                      f32(T["wd_hi"][:, :, half * LD:(half + 1) * LD]),
                                      ALU.subtract).then_inc(S["lo_done"], 1)
        clear_semaphores(nc, S.values())


def build_latents(nc, T, x_seq):
    with ExitStack() as ctx:
        def sb(name, shape, dt=F32):
            return ctx.enter_context(nc.sbuf_tensor(name, shape, dt))
        names = [f"loaded{g}" for g in range(QB)] + ["stats", "mean", "var", "rstd", "normed", "turned", "x_hi", "x_lo",
                 "lat", "k_hi", "lat_copied", "k_lo", "lat_turned", "v_hi", "v_lo", "filled"]
        S = {n: ctx.enter_context(nc.semaphore("l_" + n)) for n in names}
        x = sb("lx", [P, KT, D])
        xn = sb("lxn", [P, KT, D])
        st = sb("lst", [P, KT, 6])
        mv = sb("lmv", [P, KT, 2])
        rs = sb("lrs", [P, KT, 1])
        ve = sb("lve", [P, KT, 1])
        lat = sb("llat", [LD, L])
        ps, xh, xl, kh, kl, va, vc = (T[k] for k in ("ps", "xt_hi", "xt_lo", "k_hi", "k_lo", "v_hi", "v_lo"))
        x_v = x_seq.rearrange("(t p) d -> p t d", p=P)
        with nc.Block() as block:
            @block.sync
            def _(sp):
                for g in range(QB):
                    sp.dma_start(x[:, TPB * g:TPB * (g + 1), :],
                                 x_v[:, TPB * g:TPB * (g + 1), :]).then_inc(S[f"loaded{g}"], DMA)

            @block.gpsimd
            def _(pool):
                pool.memset(f32(kl[LD:LD + 1, :]), 1.0).then_inc(S["filled"], 1)
                pool.wait_ge(S["filled"], 1)
                pool.memset(f32(va[:, :, LD:P]), 1.0).then_inc(S["filled"], 1)
                pool.memset(f32(vc[:, :, LD:P]), 0.0).then_inc(S["filled"], 1)
                for g in range(QB):
                    ts = slice(TPB * g, TPB * (g + 1))
                    pool.wait_ge(S["mean"], TPB * (g + 1))
                    pool.tensor_scalar(ve[:, ts, :], mv[:, ts, 1:2], LN_EPS, None, ALU.add).then_inc(S["var"], 1)
                    pool.wait_ge(S["var"], g + 1)
                    pool.tensor_tensor(rs[:, ts, :], ve[:, ts, :], T["minus_half"][:, 0:TPB, None],
                                       ALU.pow).then_inc(S["rstd"], 1)

            @block.vector
            def _(dve):
                def norm(g):
                    dve.wait_ge(S[f"loaded{g}"], DMA)
                    for t in range(TPB * g, TPB * (g + 1)):
                        dve.bn_stats(st[:, t, :], x[:, t, :]).then_inc(S["stats"], 1)
                    for t in range(TPB * g, TPB * (g + 1)):
                        dve.wait_ge(S["stats"], t + 1)
                        dve.bn_aggr(mv[:, t, :], st[:, t, :]).then_inc(S["mean"], 1)
                    dve.wait_ge(S["rstd"], g + 1)
                    for t in range(TPB * g, TPB * (g + 1)):
                        dve.tensor_scalar(xn[:, t, :], x[:, t, :], mv[:, t, 0:1], rs[:, t, :],
                                          ALU.subtract, ALU.mult).then_inc(S["normed"], 1)

                def split_x(g):
                    for dt in range(DT):
                        dve.wait_ge(S["x_hi"], DT * g + dt + 1)
                        o = (slice(None), dt, slice(BLK * g, BLK * (g + 1)))
                        dve.tensor_tensor(xl[o], ps[:, 2 * (g % 2) + dt, :], f32(xh[o]), ALU.subtract).then_inc(S["x_lo"], 1)

                def split_k(g):
                    c = slice(BLK * g, BLK * (g + 1))
                    dve.wait_ge(S["lat_copied"], g + 1)
                    dve.tensor_tensor(kl[0:LD, c], lat[:, c], f32(kh[0:LD, c]), ALU.subtract).then_inc(S["k_lo"], 1)

                def split_v(g):
                    dve.wait_ge(S["v_hi"], g + 1)
                    o = (slice(None), slice(TPB * g, TPB * (g + 1)), slice(0, LD))
                    dve.tensor_tensor(vc[o], ps[:, 6 + g % 2, 0:TPB * LD].rearrange("p (t c) -> p t c", c=LD),
                                      f32(va[o]), ALU.subtract).then_inc(S["v_lo"], 1)

                norm(0)
                for g in range(QB):
                    if g + 1 < QB:
                        norm(g + 1)
                    split_x(g)
                    split_k(g)
                    split_v(g)

            @block.tensor
            def _(pe):
                def turn(g):
                    pe.wait_ge(S["normed"], TPB * (g + 1))
                    if g >= 2:
                        pe.wait_ge(S["x_lo"], DT * (g - 1))
                    for dt in range(DT):
                        for j in range(TPB):
                            mm = pe.transpose(ps[:, 2 * (g % 2) + dt, j * P:(j + 1) * P],
                                              xn[:, TPB * g + j, dt * P:(dt + 1) * P], T["ident"][:, :])
                    mm.then_inc(S["turned"], 1)

                def latents(g):
                    c = slice(BLK * g, BLK * (g + 1))
                    pe.wait_ge(S["x_lo"], DT * (g + 1))
                    if g >= 2:
                        pe.wait_ge(S["lat_copied"], g - 1)
                    terms = [(a, m, dt) for a, m in (("wd_hi", xh), ("wd_hi", xl), ("wd_lo", xh)) for dt in range(DT)]
                    for n, (a, m, dt) in enumerate(terms):
                        mm = pe.matmul(ps[:, 4 + g % 2, :], T[a][:, dt, :], m[:, dt, c],
                                       start=n == 0, stop=n == len(terms) - 1)
                    mm.then_inc(S["lat"], 1)

                def turn_latents(g):
                    pe.wait_ge(S["lat_copied"], g + 1)
                    if g >= 2:
                        pe.wait_ge(S["v_lo"], g - 1)
                    for j in range(TPB):
                        t = TPB * g + j
                        mm = pe.transpose(ps[:, 6 + g % 2, j * LD:(j + 1) * LD], lat[:, t * P:(t + 1) * P],
                                          T["ident"][0:LD, 0:LD])
                    mm.then_inc(S["lat_turned"], 1)

                turn(0)
                for g in range(QB):
                    if g + 1 < QB:
                        turn(g + 1)
                    latents(g)
                    turn_latents(g)

            @block.scalar
            def _(act):
                for g in range(QB):
                    c = slice(BLK * g, BLK * (g + 1))
                    act.wait_ge(S["turned"], g + 1)
                    for dt in range(DT):
                        act.activation(xh[:, dt, c], ps[:, 2 * (g % 2) + dt, :], ACT.Copy).then_inc(S["x_hi"], 1)
                    act.wait_ge(S["lat"], g + 1)
                    act.activation(kh[:, c], ps[:, 4 + g % 2, :], ACT.Copy).then_inc(S["k_hi"], 1)
                    act.activation(lat[:, c], ps[0:LD, 4 + g % 2, :], ACT.Copy).then_inc(S["lat_copied"], 1)
                    act.wait_ge(S["lat_turned"], g + 1)
                    act.activation(va[:, TPB * g:TPB * (g + 1), 0:LD],
                                   ps[:, 6 + g % 2, 0:TPB * LD].rearrange("p (t c) -> p t c", c=LD),
                                   ACT.Copy).then_inc(S["v_hi"], 1)
        clear_semaphores(nc, S.values())


BANK_JOBS = [(1, "row", 0, 3), (5, "row", 1, 0), (8, "proj", 2, 0), (13, "row", 1, 1), (16, "proj", 2, 1),
             (25, "row", 1, 2), (28, "proj", 2, 2), (34, "proj", 2, 3), (41, "row", 1, 3),
             (45, "row", 2, 0), (53, "row", 2, 1), (65, "row", 2, 2)]
SPLITS = [(3, 1, 3), (9, 2, 0), (17, 2, 1), (29, 2, 2), (42, 2, 3), (46, 3, 0), (54, 3, 1), (66, 3, 2)]
FIRST_ROWS = 3
FIRST_SPLITS = 7
ON_DVE = [s % 3 == 0 for s in range(2 * STEPS)]
DVE_LOS, POOL_LOS = sum(ON_DVE), 2 * STEPS - sum(ON_DVE)


def los_before(s, on_dve):
    return sum(1 for t in range(s) if ON_DVE[t] == on_dve)


def same_bank_before(s):
    return s - 3 if s >= 3 else max(t for t in range(2 * STEPS) if t % 3 == s) - 2 * STEPS


def is_diagonal(s):
    qb, kt = SCORE_STEPS[s % STEPS]
    return kt >= TPB * qb


def diagonals_before(s):
    return sum(is_diagonal(t) for t in range(s))


DIAGONALS = diagonals_before(2 * STEPS)


def block_end(qb):
    return 2 * (qb + 1) * (qb + 2) - 1


def build_attention(nc, T, y_seq, recip_rows):
    with ExitStack() as ctx:
        def sb(name, shape, dt=F32):
            return ctx.enter_context(nc.sbuf_tensor(name, shape, dt))
        names = ["staged",
                 "max_scored",
                 "max_masked",
                 "max_read",
                 "part_max",
                 "neg_max",
                 "bank_made",
                 "bank_read",
                 "q_hi", "q_lo", "q_copy",
                 "scored",
                 "masked",
                 "probs",
                 "probs_hi",
                 "lo_dve", "lo_pool",
                 "latent_used",
                 "y_copied",
                 "sums_in",
                 "recip",
                 "recip_out",
                 "recip_in",
                 "normed",
                 "stored0", "stored1", "stored2", "stored3",
                 "row_in0", "row_in1", "row_in2", "row_in3"]
        S = {n: ctx.enter_context(nc.semaphore("a_" + n)) for n in names}
        stage_hi = sb("stage_hi", [P, DT, P], F32R)
        stage_lo = sb("stage_lo", [P, DT, P], F32R)
        q_raw = sb("q_raw", [P, L])
        qa = [sb(f"q_parts{i}", [P, L], F32R) for i in range(2)]
        qc = [sb(f"q_row{i}", [LD + 1, L], F32R) for i in range(2)]
        pr = sb("pr", [P, RING, BLK])
        ph = sb("ph", [P, RING, BLK], F32R)
        pl = sb("pl", [P, RING, BLK], F32R)
        part = sb("part", [P, 2, TPB, QB])
        mx = sb("mx", [P, 2, TPB])
        neg = sb("neg", [P, 2, TPB])
        neg_rows = sb("neg_rows", [TPB, QB, P], F32R)
        y = sb("y_sums", [P, QB, BLK])
        sums = sb("sums", [P, QB, TPB])
        rec = sb("rec", [LD, QB, BLK])
        ps, xh, xl, kh, kl, va, vc = (T[k] for k in ("ps", "xt_hi", "xt_lo", "k_hi", "k_lo", "v_hi", "v_lo"))

        SCORE_BANK, MAX_BANK, Y_BANK, BANK = 0, 3, 5, 7

        def jobs_at(s, last):
            kept = [j for j in BANK_JOBS if not (last and j[2] == 2)]
            return [(n, j) for n, j in enumerate(kept) if j[0] == s]

        def splits_at(s, last):
            kept = [j for j in SPLITS if not (last and j[1] >= 2)]
            return [(n, j) for n, j in enumerate(kept) if j[0] == s]

        def row_job(head, qb, last):
            kept = [j for j in BANK_JOBS if not (last and j[2] == 2)]
            at = [n for n, j in enumerate(kept) if j[1:] == ("row", head, qb)]
            if at:
                return at[0] + 1
            at = [n for n, j in enumerate(BANK_JOBS) if j[1:] == ("row", head + 2, qb)]
            return at[0] + 1 - len(BANK_JOBS)

        FIRST_JOBS = QB + FIRST_ROWS
        NJOBS, NSPLITS = len(BANK_JOBS), len(SPLITS)

        def turns(eng, turn):
            turn(0, True, False)
            with eng.Fori(1, PAIRS - 1) as p:
                turn(p, False, False)
            turn(PAIRS - 1, False, True)

        def block_jobs(job, s, after, p, first):
            for half in range(2):
                for qb in range(QB):
                    at = STEPS * half + block_end(qb) + after
                    if at == s:
                        job(p, half, qb)
                    elif at == s + 2 * STEPS and not first:
                        job(p - 1, half, qb)

        def late_jobs(job, after):
            for half in range(2):
                for qb in range(QB):
                    if STEPS * half + block_end(qb) + after >= 2 * STEPS:
                        job(PAIRS - 1, half, qb)

        def split_waits(p, head, qb, first):
            jobs = [n for n, j in enumerate(BANK_JOBS) if j[1:] == ("proj", 2, qb)]
            read = FIRST_JOBS + NJOBS * p + jobs[0] + 1
            if head == 1:
                return (QB, None) if first else (FIRST_JOBS + NJOBS * (p - 1) + jobs[0] + 1, 2 * STEPS * p)
            return read, 2 * STEPS * p + STEPS * (head - 2) + block_end(qb) + 1

        def wait_lo(eng, p, s):
            if s < 0:
                p, s = p - 1, s + 2 * STEPS
            if ON_DVE[s]:
                eng.wait_ge(S["lo_dve"], DVE_LOS * p + los_before(s + 1, True))
            else:
                eng.wait_ge(S["lo_pool"], POOL_LOS * p + los_before(s + 1, False))

        def make_lo(eng, p, s, first, sem):
            qb, kt = SCORE_STEPS[s % STEPS]
            w = BLK - P * max(0, kt - TPB * qb)
            eng.wait_ge(S["probs_hi"], 2 * STEPS * p + s + 1)
            if not (first and s < RING):
                eng.wait_ge(S["latent_used"], 2 * STEPS * p + s - RING + 1)
            eng.tensor_tensor(pl[:, s % RING, 0:w], pr[:, s % RING, 0:w], f32(ph[:, s % RING, 0:w]),
                              ALU.subtract).then_inc(sem, 1)

        with nc.Block() as block:
            @block.sync
            def _(sp):
                def stage(pair, projected):
                    if projected is not None:
                        sp.wait_ge(S["bank_made"], projected)
                    sp.dma_start(f32(stage_hi[:, :, :]), f32(T["m_hi"][:, pair, :, :])).then_inc(S["staged"], DMA)
                    sp.dma_start(f32(stage_lo[:, :, :]), f32(T["m_lo"][:, pair, :, :])).then_inc(S["staged"], DMA)

                def divide(p, half, qb):
                    n = 8 * p + 4 * half + qb
                    sp.wait_ge(S["y_copied"], n + 1)
                    sp.dma_start(sums[:, qb, :], y[LD:LD + 1, qb, :]).then_inc(S["sums_in"], DMA)
                    sp.wait_ge(S["recip"], n + 1)
                    sp.dma_start(recip_rows[qb], sums[:, qb, :]).then_inc(S["recip_out"], DMA)
                    sp.wait_ge(S["recip_out"], DMA * (n + 1))
                    sp.dma_start(rec[:, qb, :], recip_rows[qb:qb + 1, :, :].rearrange("a p j -> a (p j)").broadcast_to(
                        [LD, BLK])).then_inc(S["recip_in"], DMA)

                def store(p, half, qb):
                    sp.wait_ge(S["normed"], 8 * p + 4 * half + qb + 1)
                    sp.dma_start(y_seq[qb, half * LD:(half + 1) * LD, p, :], y[0:LD, qb, :]).then_inc(S[f"stored{qb}"], DMA)

                def turn(p, more, first=False):
                    for half in range(2):
                        for qb in range(QB):
                            divide(p, half, qb)
                            if half or qb:
                                store(p, half - (qb == 0), (qb - 1) % QB)
                            elif not first:
                                store(p - 1, 1, QB - 1)
                            if more and (half, qb) == (0, 2):
                                stage(p + 2, FIRST_JOBS + NJOBS * p + 8)

                stage(0, None)
                stage(1, QB)
                turn(0, True, first=True)
                with sp.Fori(1, PAIRS - 2) as p:
                    turn(p, True)
                with sp.Fori(PAIRS - 2, PAIRS) as p:
                    turn(p, False)
                store(PAIRS - 1, 1, QB - 1)
                for qb in range(QB):
                    sp.wait_ge(S[f"stored{qb}"], DMA * H)

            @block.tensor
            def _(pe):
                def project(pair, qb, job):
                    pe.wait_ge(S["staged"], 2 * DMA * (pair + 1))
                    pe.wait_ge(S["bank_read"], job)
                    c = slice(BLK * qb, BLK * (qb + 1))
                    terms = [(a, m, dt) for a, m in ((stage_hi, xh), (stage_hi, xl), (stage_lo, xh)) for dt in range(DT)]
                    for n, (a, m, dt) in enumerate(terms):
                        mm = pe.matmul(ps[:, BANK, :], a[:, dt, :], m[:, dt, c], start=n == 0, stop=n == len(terms) - 1)
                    mm.then_inc(S["bank_made"], 1)

                def row(qb, block_no, job):
                    pe.wait_ge(S["neg_max"], block_no + 1)
                    pe.wait_ge(S["bank_read"], job)
                    pe.transpose(ps[0:TPB, BANK, 0:P], neg[:, qb % 2, :], T["ident"][:, :]).then_inc(S["bank_made"], 1)

                def max_scores(half, m, split_no, n, first=False):
                    i, c = MAX_STEPS[m]
                    if c == 0 and i % TPB == 0:
                        pe.wait_ge(S["q_hi"], split_no + 1)
                        pe.wait_ge(S["q_lo"], split_no + 1)
                    if not first:
                        pe.wait_ge(S["max_read"], n - 1)
                    w = BLK if c < i // TPB else P * (i % TPB + 1)
                    pe.matmul(ps[:, MAX_BANK + m % 2, 0:w], qa[half][:, i * P:(i + 1) * P],
                              kh[:, c * BLK:c * BLK + w], start=True, stop=True).then_inc(S["max_scored"], 1)

                def scores(half, m, s, p, first, last):
                    qb, kt = SCORE_STEPS[m]
                    off = P * max(0, kt - TPB * qb)
                    if kt == 0:
                        pe.wait_ge(S["q_copy"], 8 * p + 4 * half + qb + 1)
                        pe.wait_ge(S[f"row_in{qb}"], DMA * (2 * p + half + 1))
                    if not (first and s < 3):
                        pe.wait_ge(S["probs_hi"], 2 * STEPS * p + same_bank_before(s) + 1)
                    out = ps[:, SCORE_BANK + s % 3, 0:BLK - off]
                    q = slice(BLK * qb + off, BLK * (qb + 1))
                    k = slice(kt * P, (kt + 1) * P)
                    pe.matmul(out, kh[:, k], qa[half][:, q], start=True, stop=False)
                    pe.matmul(out, kl[0:LD + 1, k], qc[half][:, q], start=False, stop=True).then_inc(S["scored"], 1)

                def use_latents(p, s):
                    half, m = s // STEPS, s % STEPS
                    qb, kt = SCORE_STEPS[m]
                    off = P * max(0, kt - TPB * qb)
                    pe.wait_ge(S["probs_hi"], 2 * STEPS * p + s + 1)
                    if ON_DVE[s]:
                        pe.wait_ge(S["lo_dve"], DVE_LOS * p + los_before(s + 1, True))
                    else:
                        pe.wait_ge(S["lo_pool"], POOL_LOS * p + los_before(s + 1, False))
                    if kt == 0:
                        n = 4 * half + qb
                        if not isinstance(p, int) or 8 * p + n >= 2:
                            pe.wait_ge(S["y_copied"], 8 * p + n - 1)
                    out = ps[:, Y_BANK + qb % 2, off:BLK]
                    b = s % RING
                    w = BLK - off
                    pe.matmul(out, va[:, kt, :], ph[:, b, 0:w], start=kt == 0, stop=False)
                    pe.matmul(out, vc[:, kt, :], ph[:, b, 0:w], start=False, stop=False)
                    pe.matmul(out, va[:, kt, :], pl[:, b, 0:w], start=False,
                              stop=kt == TPB * (qb + 1) - 1).then_inc(S["latent_used"], 1)

                def turn(p, first, last):
                    for s in range(2 * STEPS):
                        half, m = s // STEPS, s % STEPS
                        if not (last and half == 1):
                            split_no = 8 * p + 4 * (half + 1) + MAX_STEPS[m][0] // TPB
                            max_scores(1 - half, m, split_no, STEPS + 2 * STEPS * p + s)
                        for n, (_, kind, head, qb) in jobs_at(s, last):
                            job = FIRST_JOBS + NJOBS * p + n
                            if kind == "row":
                                row(qb, 8 * p + 4 * head + qb, job)
                            else:
                                project(p + 1, qb, job)
                        scores(half, m, s, p, first, last)
                        if s >= LAG:
                            use_latents(p, s - LAG)
                        elif not first:
                            use_latents(p - 1, 2 * STEPS + s - LAG)

                for qb in range(QB):
                    project(0, qb, qb)
                for m in range(STEPS):
                    max_scores(0, m, MAX_STEPS[m][0] // TPB, m, first=m < 2)
                    for qb in range(FIRST_ROWS):
                        if m == block_end(qb) + 2:
                            row(qb, qb, QB + qb)
                turns(pe, turn)
                for s in range(2 * STEPS - LAG, 2 * STEPS):
                    use_latents(PAIRS - 1, s)

            @block.scalar
            def _(act):
                def read_queries(pair, qb, job, first=False):
                    act.wait_ge(S["bank_made"], job + 1)
                    if not first:
                        act.wait_ge(S["q_hi"], 8 * (pair - 1) + 4 + qb + 1)
                        act.wait_ge(S["q_lo"], 8 * (pair - 1) + 4 + qb + 1)
                        act.wait_ge(S["q_copy"], 8 * (pair - 1) + 4 + qb + 1)
                    act.activation(q_raw[:, BLK * qb:BLK * (qb + 1)], ps[:, BANK, :], ACT.Copy).then_inc(S["bank_read"], 1)

                def read_row(head, half, qb, job):
                    act.wait_ge(S["bank_made"], job + 1)
                    if not isinstance(head, int) or head >= 1:
                        act.wait_ge(S[f"row_in{qb}"], DMA * head)
                    act.activation(neg_rows[:, qb, :], ps[0:TPB, BANK, 0:P], ACT.Copy).then_inc(S["bank_read"], 1)
                    act.wait_ge(S["bank_read"], job + 1)
                    act.dma_start(f32(qc[half][LD:LD + 1, BLK * qb:BLK * (qb + 1)]),
                                  f32(neg_rows[:, qb, :])).then_inc(S[f"row_in{qb}"], DMA)

                def copy_queries(half, qb, read, scored):
                    if read is not None:
                        act.wait_ge(S["bank_read"], read)
                    if scored is not None:
                        act.wait_ge(S["scored"], scored)
                    c = slice(BLK * qb, BLK * (qb + 1))
                    act.activation(qc[half][0:LD, c], q_raw[half * LD:(half + 1) * LD, c], ACT.Copy).then_inc(S["q_copy"], 1)

                def copy_sums(p, half, qb):
                    act.wait_ge(S["latent_used"], 2 * STEPS * p + STEPS * half + block_end(qb) + 1)
                    if not isinstance(p, int) or 2 * p + half >= 1:
                        act.wait_ge(S[f"stored{qb}"], DMA * (2 * p + half))
                    act.activation(y[:, qb, :], ps[:, Y_BANK + qb % 2, :], ACT.Copy).then_inc(S["y_copied"], 1)

                def turn(p, first, last):
                    for s in range(2 * STEPS):
                        block_jobs(copy_sums, s, LAG + 1, p, first)
                        qb, kt = SCORE_STEPS[s % STEPS]
                        w = BLK - P * max(0, kt - TPB * qb)
                        if is_diagonal(s):
                            act.wait_ge(S["masked"], DIAGONALS * p + diagonals_before(s + 1))
                        else:
                            act.wait_ge(S["scored"], 2 * STEPS * p + s + 1)
                        src = ps[:, SCORE_BANK + s % 3, 0:w]
                        if not (first and s < RING):
                            wait_lo(act, p, s - RING)
                        act.activation(pr[:, s % RING, 0:w], src, ACT.Exp).then_inc(S["probs"], 1)
                        if not (first and s < RING):
                            act.wait_ge(S["latent_used"], 2 * STEPS * p + s - RING + 1)
                        act.activation(ph[:, s % RING, 0:w], src, ACT.Exp).then_inc(S["probs_hi"], 1)
                        for n, (_, kind, head, jqb) in jobs_at(s, last):
                            job = FIRST_JOBS + NJOBS * p + n
                            if kind == "row":
                                read_row(2 * p + head, head % 2, jqb, job)
                            else:
                                read_queries(p + 1, jqb, job)
                        for n, (_, head, jqb) in splits_at(s, last):
                            copy_queries(head % 2, jqb, *split_waits(p, head, jqb, first))

                for qb in range(QB):
                    read_queries(0, qb, qb, first=True)
                for n in range(FIRST_SPLITS):
                    copy_queries(n // QB, n % QB, n % QB + 1, None)
                for qb in range(FIRST_ROWS):
                    read_row(0, 0, qb, QB + qb)
                turns(act, turn)
                late_jobs(copy_sums, LAG + 1)

            @block.gpsimd
            def _(pool):
                def split_lo(half, qb, no, los=None):
                    if los is not None:
                        pool.wait_ge(S["lo_pool"], los)
                    c = slice(BLK * qb, BLK * (qb + 1))
                    hi, lo = slice(half * LD, (half + 1) * LD), slice((1 - half) * LD, (2 - half) * LD)
                    pool.wait_ge(S["q_hi"], no + 1)
                    pool.tensor_tensor(qa[half][lo, c], q_raw[hi, c], f32(qa[half][hi, c]),
                                       ALU.subtract).then_inc(S["q_lo"], 1)
                    pool.wait_ge(S["q_lo"], no + 1)

                def turn(p, first, last):
                    for s in range(2 * STEPS):
                        if not ON_DVE[s]:
                            make_lo(pool, p, s, first, S["lo_pool"])
                        for n, (_, head, qb) in splits_at(s, last):
                            split_lo(head % 2, qb, FIRST_SPLITS + NSPLITS * p + n,
                                     POOL_LOS * p + los_before(s + 1, False))

                for n in range(FIRST_SPLITS):
                    split_lo(n // QB, n % QB, n)
                turns(pool, turn)

            @block.vector
            def _(dve):
                def split_hi(half, qb, read, scored):
                    dve.wait_ge(S["bank_read"], read)
                    if scored is not None:
                        dve.wait_ge(S["scored"], scored)
                    c = slice(BLK * qb, BLK * (qb + 1))
                    hi = slice(half * LD, (half + 1) * LD)
                    dve.tensor_copy(qa[half][hi, c], q_raw[hi, c]).then_inc(S["q_hi"], 1)

                def mask_scores(p, s):
                    src = ps[:, SCORE_BANK + s % 3, 0:P]
                    dve.wait_ge(S["scored"], 2 * STEPS * p + s + 1)
                    dve.tensor_tensor(src, src, T["mask_kq"][:, :], ALU.add).then_inc(S["masked"], 1)

                def invert(p, half, qb):
                    dve.wait_ge(S["sums_in"], DMA * (8 * p + 4 * half + qb + 1))
                    dve.reciprocal(sums[:, qb, :], sums[:, qb, :]).then_inc(S["recip"], 1)

                def divide(p, half, qb):
                    dve.wait_ge(S["recip_in"], DMA * (8 * p + 4 * half + qb + 1))
                    dve.tensor_tensor(y[0:LD, qb, :], y[0:LD, qb, :], rec[:, qb, :], ALU.mult).then_inc(S["normed"], 1)

                def turn(p, first, last):
                    for s in range(2 * STEPS):
                        half, m = s // STEPS, s % STEPS
                        if not (last and half == 1):
                            qb = MAX_STEPS[m][0] // TPB
                            h2, q2 = (half + 1, qb - 2) if qb >= 2 else (half, qb + 2)
                            kept = [j for j in BANK_JOBS if not (last and j[2] == 2)]
                            at = [k for k, j in enumerate(kept) if j[1:] == ("row", h2, q2)]
                            if at:
                                made = FIRST_JOBS + NJOBS * p + at[0] + 1
                            else:
                                made = FIRST_JOBS + NJOBS * p + row_job(h2, q2, last)
                            read_max(m, STEPS + 2 * STEPS * p + s, 8 * p + 4 * (half + 1) + qb, made)
                        if is_diagonal(s):
                            mask_scores(p, s)
                        for n, (_, head, qb) in splits_at(s, last):
                            split_hi(head % 2, qb, *split_waits(p, head, qb, first))
                        if s and ON_DVE[s - 1]:
                            make_lo(dve, p, s - 1, first, S["lo_dve"])
                        block_jobs(invert, s, INVERT_AFTER, p, first)
                        block_jobs(divide, s, DIVIDE_AFTER, p, first)

                def read_max(m, n, block_no, made):
                    i, c = MAX_STEPS[m]
                    j, qb = i % TPB, i // TPB
                    src = ps[:, MAX_BANK + m % 2, :]
                    dst = part[:, qb % 2, j, c:c + 1]
                    dve.wait_ge(S["max_scored"], n + 1)
                    w = BLK if c < qb else P * (j + 1)
                    if c == qb:
                        dve.tensor_tensor(src[:, w - P:w], src[:, w - P:w], T["mask_qk"][:, :],
                                          ALU.add).then_inc(S["max_masked"], 1)
                        dve.wait_ge(S["max_masked"], TPB * block_no + j + 1)
                    ins = dve.tensor_reduce(dst, src[:, 0:w], AX.X, ALU.max)
                    ins.then_inc(S["max_read"], 1)
                    if j == TPB - 1 and c == qb:
                        dve.wait_ge(S["max_read"], n + 1)
                        dve.tensor_reduce(mx[:, qb % 2, :], part[:, qb % 2, :, 0:qb + 1], AX.X,
                                          ALU.max).then_inc(S["part_max"], 1)
                        dve.wait_ge(S["part_max"], block_no + 1)
                        if made is not None:
                            dve.wait_ge(S["bank_made"], made)
                        dve.tensor_scalar(neg[:, qb % 2, :], mx[:, qb % 2, :], -1.0, None,
                                          ALU.mult).then_inc(S["neg_max"], 1)

                for n in range(FIRST_SPLITS):
                    split_hi(n // QB, n % QB, n % QB + 1, None)
                for m in range(STEPS):
                    qb = MAX_STEPS[m][0] // TPB
                    read_max(m, m, qb, QB + qb - 1 if qb >= 2 else None)
                turns(dve, turn)
                late_jobs(invert, INVERT_AFTER)
                late_jobs(divide, DIVIDE_AFTER)
        clear_semaphores(nc, S.values())




def shared_tensors(nc, ctx):
    def sb(name, shape, dt=F32):
        return ctx.enter_context(nc.sbuf_tensor(name, shape, dt))
    return {
        "ps": ctx.enter_context(nc.psum_tensor("ps", [P, 8, BLK], F32)),
        "ident": sb("ident", [P, P]), "minus_half": sb("minus_half", [P, TPB]),
        "n_hi": sb("n_hi", [P, PAIRS, D], F32R), "n_lo": sb("n_lo", [P, PAIRS, D], F32R),
    }


def attention_tensors(nc, ctx):
    def sb(name, shape, dt=F32):
        return ctx.enter_context(nc.sbuf_tensor(name, shape, dt))
    return {
        "mask_kq": sb("mask_kq", [P, P]), "mask_qk": sb("mask_qk", [P, P]),
        "m_hi": sb("m_hi", [P, PAIRS, DT, P], F32R), "m_lo": sb("m_lo", [P, PAIRS, DT, P], F32R),
        "wd_hi": sb("wd_hi", [P, DT, P], F32R), "wd_lo": sb("wd_lo", [P, DT, P], F32R),
        "xt_hi": sb("xt_hi", [P, DT, L], F32R), "xt_lo": sb("xt_lo", [P, DT, L], F32R),
        "k_hi": sb("k_hi", [P, L], F32R), "k_lo": sb("k_lo", [LD + 1, L], F32R),
        "v_hi": sb("v_hi", [P, KT, P], F32R), "v_lo": sb("v_lo", [P, KT, P], F32R),
    }


def build_mixture_weights(nc, W, w):
    with ExitStack() as ctx:
        def sb(name, shape, dt=F32):
            return ctx.enter_context(nc.sbuf_tensor(name, shape, dt))
        S = {n: ctx.enter_context(nc.semaphore("mw_" + n)) for n in ("up_in", "gate_in", "down_in", "small_in", "hi", "lo", "filled")}
        raw = {"up": sb("up_raw", [P, NE, DT, I]), "gate": sb("gate_raw", [P, E + 1, DT, I]),
               "down": sb("down_raw", [P, E + 1, DT, D]), "router": sb("router_raw", [P, ROUNDS, DT, E])}
        small = ["b_up", "b_gate", "b_down", "router_b", "gate_bias", "norm_w"]
        units = [("router", "small_in", slice(0, ROUNDS))] + [
            (k, s, slice(e, e + 2)) for k, s, n in (("up", "up_in", NE), ("gate", "gate_in", E), ("down", "down_in", E))
            for e in range(0, n, 2)] + [("gate", "gate_in", slice(E, E + 1)), ("down", "down_in", slice(E, E + 1))]
        total = {"small_in": DMA * (len(small) + ROUNDS), "up_in": DMA * (E + 2), "gate_in": DMA * (E + 1), "down_in": DMA * (E + 1)}
        with nc.Block() as block:
            @block.sync
            def _(sp):
                for k in small:
                    dst = W[k]
                    sp.dma_start(dst[tuple(slice(None) for _ in dst.shape)], w[k]).then_inc(S["small_in"], DMA)
                for c in range(ROUNDS):
                    sp.dma_start(raw["router"][:, c, :, :],
                                 w["router_w"][c].rearrange("(t p) e -> p t e", p=P)).then_inc(S["small_in"], DMA)
                for k, s, src, shared in (("up", "up_in", "exp_up", "share_up"), ("gate", "gate_in", "exp_gate", "share_gate"),
                                          ("down", "down_in", "exp_down", "share_down")):
                    for e in range(E):
                        sp.dma_start(raw[k][:, e, :, :], w[src][e].rearrange("(t p) i -> p t i", p=P)).then_inc(S[s], DMA)
                    for e in range(2 if k == "up" else 1):
                        sp.dma_start(raw[k][:, E + e, :, :],
                                     w[shared][:, e * I:(e + 1) * I].rearrange("(t p) i -> p t i", p=P)).then_inc(S[s], DMA)

            @block.scalar
            def _(act):
                for k, s, es in units:
                    act.wait_ge(S[s], total[s])
                    act.activation(W[k + "_hi"][:, es, :, :], raw[k][:, es, :, :], ACT.Copy).then_inc(S["hi"], 1)

            @block.vector
            def _(dve):
                for n, (k, s, es) in enumerate(units):
                    dve.wait_ge(S["hi"], n + 1)
                    dve.tensor_tensor(W[k + "_lo"][:, es, :, :], raw[k][:, es, :, :], f32(W[k + "_hi"][:, es, :, :]),
                                      ALU.subtract).then_inc(S["lo"], 1)

            @block.gpsimd
            def _(pool):
                pool.memset(W["earlier"][:, :, :, :], 1.0).then_inc(S["filled"], 1)
                pool.wait_ge(S["filled"], 1)
                pool.affine_select(out=W["earlier"][:, :, :, :], in_=W["earlier"][:, :, :, :], compare_op=ALU.is_gt, fill=0.0,
                                   base=0, pattern=[[0, TPB], [1, E], [-1, E]], channel_multiplier=0).then_inc(S["filled"], 1)
        clear_semaphores(nc, S.values())


def build_tokens(nc, W, F, y_v, x_v, out_v):
    with ExitStack() as ctx:
        names = ["y_in",
                 "x_in",
                 "y_hi", "y_lo_even", "y_lo_odd",
                 "proj",
                 "x1",
                 "stats", "mean", "var", "rstd",
                 "x_norm",
                 "x1_kept",
                 "turned",
                 "xt_hi", "xt_lo",
                 "up", "h", "h_hi", "h_lo",
                 "gate", "silu", "g", "g_hi", "g_lo",
                 "down",
                 "sum",
                 "routed", "route", "diff", "tanh", "weights",
                 "w_turned", "w_copied", "bias",
                 "seeded",
                 "squared", "squares", "scale_var", "scale",
                 "scaled",
                 "out_ready",
                 "stored",
                 "ones"]
        S = {n: ctx.enter_context(nc.semaphore("f_" + n)) for n in names}
        ps, ident = W["ps"], W["ident"]
        UP, GATE, DOWN, AUX = 0, 2, 4, 6
        PROJ = GATE
        h, s_, xn, xf, x1, x1_next, acc = (F[k] for k in ("h", "s", "xn", "xf", "x1", "x1_next", "acc"))
        y_raw, xth, xtl = F["y_raw"], F["xt_hi"], F["xt_lo"]
        parts = F["parts"]
        y_hi, y_lo = (parts[:, i].rearrange("p k m n -> p (k m) n") for i in range(2))
        H_HI, H_LO, G_HI, G_LO = range(4)
        full = slice(None)
        Q = ROUNDS * NE

        def later(t, n):
            return not (isinstance(t, int) and t == 0) or n > 0

        def blocks(eng, turn):
            turn(0, False)
            with eng.Fori(1, NBLK - 1) as t:
                turn(t, False)
            turn(NBLK - 1, True)

        with nc.Block() as block:
            @block.sync
            def _(sp):
                def turn(t):
                    if not (isinstance(t, int) and t == NBLK - 1):
                        sp.wait_ge(S["x1_kept"], t + 1)
                        sp.dma_start(x1_next[:, :, :], x_v[t + 1]).then_inc(S["x_in"], DMA)
                    if not (isinstance(t, int) and t >= NBLK - 2):
                        sp.wait_ge(S["y_lo_even"], PAIRS // 2 * (t + 2))
                        sp.wait_ge(S["y_lo_odd"], PAIRS // 2 * (t + 2))
                        sp.dma_start(y_raw[:, :, :], y_v[t + 2]).then_inc(S["y_in"], DMA)
                    for j in range(TPB):
                        sp.wait_ge(S["out_ready"], TPB * t + j + 1)
                        sp.dma_start(out_v[t][:, j, :], xf[:, j, :]).then_inc(S["stored"], DMA)

                sp.dma_start(y_raw[:, :, :], y_v[0]).then_inc(S["y_in"], DMA)
                sp.dma_start(x1_next[:, :, :], x_v[0]).then_inc(S["x_in"], DMA)
                sp.wait_ge(S["y_lo_even"], PAIRS // 2)
                sp.wait_ge(S["y_lo_odd"], PAIRS // 2)
                sp.dma_start(y_raw[:, :, :], y_v[1]).then_inc(S["y_in"], DMA)
                with sp.Fori(0, NBLK - 2) as t:
                    turn(t)
                turn(NBLK - 2)
                turn(NBLK - 1)
                sp.wait_ge(S["stored"], DMA * TPB * NBLK)

            @block.tensor
            def _(pe):
                def project(t, pairs=range(PAIRS)):
                    for pair in pairs:
                        pe.wait_ge(S["y_hi"], PAIRS * t + pair + 1)
                        pe.wait_ge(S["y_lo_odd" if pair % 2 else "y_lo_even"], PAIRS // 2 * t + pair // 2 + 1)
                        if pair == 0 and later(t, 0):
                            pe.wait_ge(S["silu"], 2 * Q * t - Q)
                        for j in range(TPB):
                            for n, (a, b) in enumerate(((y_hi, "hi"), (y_hi, "lo"), (y_lo, "hi"))):
                                mm = pe.matmul(ps[:, PROJ + j // 2, (j % 2) * D:(j % 2 + 1) * D], a[:, pair, j * P:(j + 1) * P],
                                               W["n_" + b][:, pair, :], start=pair == 0 and n == 0 and j % 2 == 0,
                                               stop=pair == PAIRS - 1 and n == 2, skip_group_check=True)
                            if pair == PAIRS - 1 and j % 2:
                                mm.then_inc(S["proj"], 1)

                def turn_tokens(t, c):
                    r = ROUNDS * t + c
                    if later(t, r):
                        pe.wait_ge(S["seeded"], 2 * r)
                    for j in range(TPB):
                        src = xf if c else xn
                        if c:
                            pe.wait_ge(S["scaled"], TPB * r + j + 1 - TPB)
                        else:
                            pe.wait_ge(S["x_norm"], TPB * t + j + 1)
                        for dt in range(DT):
                            mm = pe.transpose(ps[:, AUX + dt, j * P:(j + 1) * P], src[:, j, dt * P:(dt + 1) * P], ident[:, :])
                    mm.then_inc(S["turned"], 1)

                def wide(out, w_hi, w_lo, m, hi, lo):
                    terms = [(a, b, dt) for a, b in ((w_hi, hi), (w_lo, hi), (w_hi, lo)) for dt in range(DT)]
                    for n, (a, b, dt) in enumerate(terms):
                        mm = pe.matmul(out, a[:, dt, m * P:(m + 1) * P], b[:, dt, :], start=n == 0, stop=n == len(terms) - 1)
                    return mm

                def up(t, c, e):
                    q = Q * t + NE * c + e
                    if e == 0:
                        pe.wait_ge(S["xt_hi"], DT * (ROUNDS * t + c + 1))
                        pe.wait_ge(S["xt_lo"], DT * (ROUNDS * t + c + 1))
                    for m in range(2):
                        if later(t, NE * c + e):
                            pe.wait_ge(S["h"], 2 * q - 1 + m)
                        wide(ps[:, UP + m, :], W["up_hi"][:, e], W["up_lo"][:, e], m, xth, xtl).then_inc(S["up"], 1)

                def gate(t, c, e):
                    q, k = Q * t + NE * c + e, min(e, E)
                    pe.wait_ge(S["h_hi"], 2 * q + 2)
                    pe.wait_ge(S["h_lo"], 2 * q + 2)
                    if not e and not (c and isinstance(t, int) and t == NBLK - 1):
                        pe.wait_ge(S["x1"], 2 * (t + c) + 2)
                    for m in range(2):
                        if later(t, NE * c + e):
                            pe.wait_ge(S["silu"], 2 * q - 1 + m)
                        wide(ps[:, GATE + m, :], W["gate_hi"][:, k], W["gate_lo"][:, k], m,
                             parts[:, e % 2, H_HI], parts[:, e % 2, H_LO]).then_inc(S["gate"], 1)

                def down(t, c, e):
                    q, k = Q * t + NE * c + e, min(e, E)
                    pe.wait_ge(S["g_hi"], 2 * q + 2)
                    pe.wait_ge(S["g_lo"], 2 * q + 2)
                    for j in range(TPB):
                        if j % 2 == 0 and later(t, NE * c + e):
                            pe.wait_ge(S["sum"], TPB * q - TPB + j + 2)
                        terms = [(a, b, dt) for a, b in ((G_HI, "hi"), (G_HI, "lo"), (G_LO, "hi")) for dt in range(DT)]
                        for n, (a, b, dt) in enumerate(terms):
                            mm = pe.matmul(ps[:, DOWN + j // 2, (j % 2) * D:(j % 2 + 1) * D],
                                           parts[:, e % 2, a, dt, j * P:(j + 1) * P], W["down_" + b][:, k, dt, :],
                                           start=n == 0, stop=n == len(terms) - 1)
                        if j % 2:
                            mm.then_inc(S["down"], 1)

                def route(c):
                    for j in range(TPB):
                        terms = [(a, b, dt) for a, b in ((xth, "hi"), (xth, "lo"), (xtl, "hi")) for dt in range(DT)]
                        for n, (a, b, dt) in enumerate(terms):
                            mm = pe.matmul(ps[:, AUX, j * NE:j * NE + E], a[:, dt, j * P:(j + 1) * P],
                                           W["router_" + b][:, c, dt, :], start=n == 0, stop=n == len(terms) - 1)
                    mm.then_inc(S["routed"], 1)

                def turn_weights(t, c):
                    pe.wait_ge(S["weights"], ROUNDS * t + c + 1)
                    for j in range(TPB):
                        mm = pe.transpose(ps[0:NE, AUX + 1, j * P:(j + 1) * P], F["weights"][:, j, :], ident[:, :])
                    mm.then_inc(S["w_turned"], 1)

                def biases(t, c):
                    pe.wait_ge(S["w_copied"], ROUNDS * t + c + 1)
                    for j in range(TPB):
                        mm = pe.matmul(ps[:, AUX + j // 2, (j % 2) * D:(j % 2 + 1) * D], F["weights_t"][:, j * P:(j + 1) * P],
                                       W["b_down"][:, :], start=True, stop=True)
                        if j % 2:
                            mm.then_inc(S["bias"], 1)

                def turn(t, last):
                    for c in range(ROUNDS):
                        if c and not last:
                            project(t + 1, range(PAIRS - 2))
                            turn_tokens(t, c)
                            project(t + 1, range(PAIRS - 2, PAIRS))
                        elif c:
                            turn_tokens(t, c)
                        for e in range(NE + 2 - c):
                            if e < NE:
                                up(t, c, e)
                            if e == 0:
                                route(c)
                                if c == 0 and later(t, 0):
                                    down(t - 1, ROUNDS - 1, NE - 1)
                            if 1 <= e <= NE:
                                gate(t, c, e - 1)
                            if e == 1:
                                turn_weights(t, c)
                            if e == 2:
                                biases(t, c)
                            if e == NE and c and not last:
                                turn_tokens(t + 1, 0)
                            if e >= 2:
                                down(t, c, e - 2)

                project(0)
                turn_tokens(0, 0)
                blocks(pe, turn)
                down(NBLK - 1, ROUNDS - 1, NE - 1)

            @block.scalar
            def _(act):
                def split_y(t, pair):
                    if pair == 0:
                        act.wait_ge(S["y_in"], DMA * (t + 1))
                    if later(t, 0):
                        if pair < PAIRS // 2:
                            act.wait_ge(S["gate"], 2 * Q * t - Q - 2)
                        else:
                            act.wait_ge(S["down"], 2 * Q * t - Q - 2)
                    act.activation(y_hi[:, pair, :], y_raw[:, pair, :], ACT.Copy).then_inc(S["y_hi"], 1)

                def hidden(t, c, e):
                    q = Q * t + NE * c + e
                    for m in range(2):
                        act.wait_ge(S["up"], 2 * q + m + 1)
                        if later(t, NE * c + e - 1):
                            act.wait_ge(S["g"], 2 * q - 3 + m)
                            act.wait_ge(S["h_lo"], 2 * q - 3 + m)
                        act.activation(h[:, e % 2, m, :], ps[:, UP + m, :], ACT.Identity,
                                       bias=W["b_up"][:, 2 * e + m:2 * e + m + 1]).then_inc(S["h"], 1)

                def silu(t, c, e):
                    q = Q * t + NE * c + e
                    for m in range(2):
                        act.wait_ge(S["gate"], 2 * q + m + 1)
                        if later(t, NE * c + e - 1):
                            act.wait_ge(S["g_lo"], 2 * q - 3 + m)
                        act.activation(s_[:, e % 2, m, :], ps[:, GATE + m, :], ACT.Silu,
                                       bias=W["b_gate"][:, 2 * e + m:2 * e + m + 1]).then_inc(S["silu"], 1)

                def xt_hi(t, c):
                    act.wait_ge(S["turned"], ROUNDS * t + c + 1)
                    for dt in range(DT):
                        act.activation(xth[:, dt, :], ps[:, AUX + dt, :], ACT.Copy).then_inc(S["xt_hi"], 1)

                def turn(t, last):
                    for c in range(ROUNDS):
                        r = ROUNDS * t + c
                        if c:
                            xt_hi(t, c)
                        for e in range(NE + 1):
                            if e < NE:
                                hidden(t, c, e)
                            if e == 1:
                                act.wait_ge(S["diff"], r + 1)
                                act.activation(F["tanh"][:, :, :], F["diff"][:, :, :], ACT.Tanh, scale=0.5).then_inc(S["tanh"], 1)
                            if e >= 1:
                                silu(t, c, e - 1)
                            if e == 1:
                                act.wait_ge(S["w_turned"], r + 1)
                                act.activation(F["weights_t"][:, :], ps[0:NE, AUX + 1, :], ACT.Copy).then_inc(S["w_copied"], 1)
                        if c == 0 and not last:
                            for pair in range(PAIRS):
                                split_y(t + 1, pair)
                        if c and not last:
                            xt_hi(t + 1, 0)

                for pair in range(PAIRS):
                    split_y(0, pair)
                xt_hi(0, 0)
                blocks(act, turn)

            def y_lo_parts(eng, t, pair):
                eng.wait_ge(S["y_hi"], PAIRS * t + pair + 1)
                if later(t, 0):
                    if pair < PAIRS // 2:
                        eng.wait_ge(S["gate"], 2 * Q * t - Q)
                    else:
                        eng.wait_ge(S["down"], 2 * Q * t - Q)
                eng.tensor_tensor(y_lo[:, pair, :], y_raw[:, pair, :], f32(y_hi[:, pair, :]),
                                  ALU.subtract).then_inc(S["y_lo_odd" if pair % 2 else "y_lo_even"], 1)

            @block.gpsimd
            def _(pool):
                def rstd(t):
                    pool.wait_ge(S["var"], t + 1)
                    pool.tensor_tensor(F["rs"][:, :, :], F["var"][:, :, :], W["minus_half"][:, :, None], ALU.pow).then_inc(S["rstd"], 1)

                def h_lo(t, c, e):
                    q = Q * t + NE * c + e
                    for m in range(2):
                        pool.wait_ge(S["h_hi"], 2 * q + m + 1)
                        pool.tensor_tensor(parts[:, e % 2, H_LO, m, :], h[:, e % 2, m, :],
                                           f32(parts[:, e % 2, H_HI, m, :]), ALU.subtract).then_inc(S["h_lo"], 1)

                def g_lo(t, c, e):
                    q = Q * t + NE * c + e
                    for m in range(2):
                        pool.wait_ge(S["g_hi"], 2 * q + m + 1)
                        pool.tensor_tensor(parts[:, e % 2, G_LO, m, :], s_[:, e % 2, m, :],
                                           f32(parts[:, e % 2, G_HI, m, :]), ALU.subtract).then_inc(S["g_lo"], 1)

                def rms(t, c):
                    r = ROUNDS * t + c
                    pool.wait_ge(S["scale_var"], r + 1)
                    pool.tensor_tensor(F["rms"][:, :], F["rms_var"][:, :], W["minus_half"][:, :], ALU.pow).then_inc(S["scale"], 1)

                def turn(t, last):
                    for c in range(ROUNDS):
                        for e in range(NE + 1):
                            if e < NE:
                                h_lo(t, c, e)
                            if e == 0 and c == 0 and later(t, 0):
                                rms(t - 1, ROUNDS - 1)
                            if e == 2 and c and not last:
                                rstd(t + 1)
                            if e >= 1:
                                g_lo(t, c, e - 1)
                        if c == 0:
                            if not last:
                                y_lo_parts(pool, t + 1, 1)
                                y_lo_parts(pool, t + 1, 3)
                            rms(t, c)
                            if not last:
                                y_lo_parts(pool, t + 1, 5)
                                y_lo_parts(pool, t + 1, 7)

                for pair in range(1, PAIRS, 2):
                    y_lo_parts(pool, 0, pair)
                rstd(0)
                blocks(pool, turn)
                rms(NBLK - 1, ROUNDS - 1)

            @block.vector
            def _(dve):
                ROUTE_STEPS = 12

                def choose(t, c):
                    g, b, r, pair, eq = F["g"], F["biased"], F["rank"], F["beaten"], F["equal"]
                    src = ps[:, AUX, 0:TPB * NE].rearrange("p (j e) -> p j e", e=NE)[:, :, 0:E]
                    other = b[:, :, None, :].broadcast_to([P, TPB, E, E])
                    own = b[:, :, :, None].broadcast_to([P, TPB, E, E])
                    base = ROUTE_STEPS * (ROUNDS * t + c)
                    dve.wait_ge(S["routed"], ROUNDS * t + c + 1)
                    dve.tensor_tensor(g[:, :, :], src, W["router_b"][:, c, None, :].broadcast_to([P, TPB, E]), ALU.add).then_inc(S["route"], 1)
                    dve.wait_ge(S["route"], base + 1)
                    dve.tensor_tensor(b[:, :, :], g[:, :, :], W["gate_bias"][:, c, None, :].broadcast_to([P, TPB, E]), ALU.add).then_inc(S["route"], 1)
                    dve.wait_ge(S["route"], base + 2)
                    dve.tensor_tensor(pair[:, :, :, :], other, own, ALU.is_gt).then_inc(S["route"], 1)
                    dve.tensor_tensor(eq[:, :, :, :], other, own, ALU.is_equal).then_inc(S["route"], 1)
                    dve.wait_ge(S["route"], base + 4)
                    dve.tensor_tensor(eq[:, :, :, :], eq[:, :, :, :], W["earlier"][:, :, :, :], ALU.mult).then_inc(S["route"], 1)
                    dve.wait_ge(S["route"], base + 5)
                    dve.tensor_tensor(pair[:, :, :, :], pair[:, :, :, :], eq[:, :, :, :], ALU.add).then_inc(S["route"], 1)
                    dve.wait_ge(S["route"], base + 6)
                    dve.tensor_reduce(r[:, :, :], pair[:, :, :, :], AX.X, ALU.add).then_inc(S["route"], 1)
                    dve.wait_ge(S["route"], base + 7)
                    dve.tensor_scalar(F["chosen"][:, :, :], r[:, :, :], 2.0, None, ALU.is_lt).then_inc(S["route"], 1)
                    dve.wait_ge(S["route"], base + 8)
                    dve.tensor_tensor(b[:, :, :], F["chosen"][:, :, :], g[:, :, :], ALU.mult).then_inc(S["route"], 1)
                    dve.wait_ge(S["route"], base + 9)
                    dve.tensor_reduce(F["both"][:, :], b[:, :, :], AX.X, ALU.add).then_inc(S["route"], 1)
                    dve.wait_ge(S["route"], base + 10)
                    dve.tensor_tensor(b[:, :, :], g[:, :, :], F["both"][:, :, None].broadcast_to([P, TPB, E]), ALU.subtract).then_inc(S["route"], 1)
                    dve.wait_ge(S["route"], base + 11)
                    dve.tensor_tensor(F["diff"][:, :, :], b[:, :, :], g[:, :, :], ALU.add).then_inc(S["diff"], 1)

                def weigh(t, c):
                    r = ROUNDS * t + c
                    dve.wait_ge(S["tanh"], r + 1)
                    dve.tensor_scalar(F["tanh"][:, :, :], F["tanh"][:, :, :], 0.5, 0.5, ALU.mult, ALU.add).then_inc(S["route"], 1)
                    dve.wait_ge(S["route"], ROUTE_STEPS * (r + 1))
                    dve.tensor_tensor(F["weights"][:, :, 0:E], F["tanh"][:, :, :], F["chosen"][:, :, :],
                                      ALU.mult).then_inc(S["weights"], 1)

                def split_hidden(t, c, e):
                    q = Q * t + NE * c + e
                    for m in range(2):
                        dve.wait_ge(S["h"], 2 * q + m + 1)
                        if later(t, NE * c + e - 1):
                            dve.wait_ge(S["gate"], 2 * q - 2)
                        if e < 2 and not (c and isinstance(t, int) and t == NBLK - 1):
                            dve.wait_ge(S["proj"], 2 * (t + c) + 2)
                        dve.tensor_copy(parts[:, e % 2, H_HI, m, :], h[:, e % 2, m, :]).then_inc(S["h_hi"], 1)

                def gated(t, c, e):
                    q = Q * t + NE * c + e
                    for m in range(2):
                        dve.wait_ge(S["silu"], 2 * q + m + 1)
                        dve.tensor_tensor(s_[:, e % 2, m, :], s_[:, e % 2, m, :], h[:, e % 2, m, :], ALU.mult).then_inc(S["g"], 1)
                    for m in range(2):
                        dve.wait_ge(S["g"], 2 * q + m + 1)
                        if later(t, NE * c + e - 1):
                            dve.wait_ge(S["down"], 2 * q - 2)
                        dve.tensor_copy(parts[:, e % 2, G_HI, m, :], s_[:, e % 2, m, :]).then_inc(S["g_hi"], 1)

                def seed(t, c, moments_next):
                    if moments_next:
                        dve.wait_ge(S["stats"], TPB * (t + 2))
                    for k in range(2):
                        dve.wait_ge(S["bias"], 2 * (ROUNDS * t + c) + k + 1)
                        two = (full, slice(2 * k, 2 * k + 2), full)
                        dve.tensor_tensor(acc[two], ps[:, AUX + k, :].rearrange("p (j d) -> p j d", d=D), (xf if c else xn)[two],
                                          ALU.add).then_inc(S["seeded"], 1)

                def add_expert(t, c, e):
                    q = Q * t + NE * c + e
                    for j in range(TPB):
                        dve.wait_ge(S["down"], 2 * q + j // 2 + 1)
                        if e:
                            dve.wait_ge(S["sum"], TPB * (q - 1) + j + 1)
                        else:
                            dve.wait_ge(S["seeded"], 2 * (ROUNDS * t + c) + j // 2 + 1)
                        dve.scalar_tensor_tensor(out=acc[:, j, :], in0=ps[:, DOWN + j // 2, (j % 2) * D:(j % 2 + 1) * D],
                                                 scalar=F["weights"][:, j, e:e + 1], in1=acc[:, j, :],
                                                 op0=ALU.mult, op1=ALU.add).then_inc(S["sum"], 1)

                def square(t, c):
                    r = ROUNDS * t + c
                    if not c and later(t, 0):
                        dve.wait_ge(S["stored"], DMA * TPB * t)
                    dve.wait_ge(S["sum"], TPB * (Q * t + NE * (c + 1)))
                    dve.tensor_tensor(xf[:, :, :], acc[:, :, :], acc[:, :, :], ALU.mult).then_inc(S["squared"], 1)
                    dve.wait_ge(S["squared"], r + 1)
                    dve.tensor_reduce(F["ss"][:, :], xf[:, :, :], AX.X, ALU.add).then_inc(S["squares"], 1)
                    dve.wait_ge(S["squares"], r + 1)
                    dve.tensor_scalar(F["rms_var"][:, :], F["ss"][:, :], 1.0 / D, RMS_EPS, ALU.mult, ALU.add).then_inc(S["scale_var"], 1)

                def normalize(t, c):
                    r = ROUNDS * t + c
                    dve.wait_ge(S["scale"], r + 1)
                    for j in range(TPB):
                        dve.scalar_tensor_tensor(out=xf[:, j, :], in0=acc[:, j, :], scalar=F["rms"][:, j:j + 1],
                                                 in1=W["norm_w"][:, c, :], op0=ALU.mult, op1=ALU.mult).then_inc(S["scaled"], 1)
                    if c:
                        for j in range(TPB):
                            dve.wait_ge(S["scaled"], TPB * r + j + 1)
                            dve.tensor_tensor(xf[:, j, :], xf[:, j, :], x1[:, j, :], ALU.add).then_inc(S["out_ready"], 1)

                def residual(t):
                    dve.wait_ge(S["x_in"], DMA * (t + 1))
                    for k in range(2):
                        dve.wait_ge(S["proj"], 2 * t + k + 1)
                        two = (full, slice(2 * k, 2 * k + 2), full)
                        dve.tensor_tensor(x1_next[two], ps[:, PROJ + k, :].rearrange("p (j d) -> p j d", d=D), x1_next[two],
                                          ALU.add).then_inc(S["x1"], 1)

                def stats(t):
                    for j in range(TPB):
                        dve.wait_ge(S["x1"], 2 * t + j // 2 + 1)
                        dve.bn_stats(F["st"][:, j, :], x1_next[:, j, :]).then_inc(S["stats"], 1)

                def moments(t):
                    for j in range(TPB):
                        dve.bn_aggr(F["mv"][:, j, :], F["st"][:, j, :]).then_inc(S["mean"], 1)
                    dve.wait_ge(S["mean"], TPB * (t + 1))
                    dve.tensor_scalar(F["var"][:, :, :], F["mv"][:, :, 1:2], LN_EPS, None, ALU.add).then_inc(S["var"], 1)

                def layernorm(t):
                    dve.wait_ge(S["rstd"], t + 1)
                    for j in range(TPB):
                        dve.tensor_scalar(xn[:, j, :], x1_next[:, j, :], F["mv"][:, j, 0:1], F["rs"][:, j, :],
                                          ALU.subtract, ALU.mult).then_inc(S["x_norm"], 1)

                def xt_lo(t, c):
                    for dt in range(DT):
                        dve.wait_ge(S["xt_hi"], DT * (ROUNDS * t + c) + dt + 1)
                        dve.tensor_tensor(xtl[:, dt, :], ps[:, AUX + dt, :], f32(xth[:, dt, :]), ALU.subtract).then_inc(S["xt_lo"], 1)

                def keep_residual(t):
                    if later(t, 0):
                        dve.wait_ge(S["out_ready"], TPB * t)
                    dve.wait_ge(S["x1"], 2 * t + 2)
                    dve.tensor_copy(x1[:, :, :], x1_next[:, :, :]).then_inc(S["x1_kept"], 1)

                def turn(t, last):
                    for c in range(ROUNDS):
                        if c:
                            if not last:
                                residual(t + 1)
                            xt_lo(t, c)
                        for e in range(NE + 2 - c):
                            if e < NE:
                                split_hidden(t, c, e)
                            if e == 0:
                                choose(t, c)
                                if c == 0 and later(t, 0):
                                    add_expert(t - 1, ROUNDS - 1, NE - 1)
                                    square(t - 1, ROUNDS - 1)
                            if e == 1:
                                weigh(t, c)
                            if 1 <= e <= NE:
                                gated(t, c, e - 1)
                            if e == 1 and c == 0:
                                if later(t, 0):
                                    normalize(t - 1, ROUNDS - 1)
                                keep_residual(t)
                            if e == 2:
                                if c and not last:
                                    stats(t + 1)
                                seed(t, c, c and not last)
                                if c and not last:
                                    moments(t + 1)
                            if e == 3 and c and not last:
                                layernorm(t + 1)
                            if e == NE and c and not last:
                                xt_lo(t + 1, 0)
                            if e >= 2:
                                add_expert(t, c, e - 2)
                            if e == NE and c == 0 and not last:
                                for pair in (0, 2):
                                    y_lo_parts(dve, t + 1, pair)
                        if c == 0:
                            square(t, c)
                            if not last:
                                y_lo_parts(dve, t + 1, 4)
                            normalize(t, c)
                            if not last:
                                y_lo_parts(dve, t + 1, 6)

                dve.memset(F["weights"][:, :, E:NE], 1.0).then_inc(S["ones"], 1)
                for pair in range(0, PAIRS, 2):
                    y_lo_parts(dve, 0, pair)
                residual(0)
                stats(0)
                dve.wait_ge(S["stats"], TPB)
                moments(0)
                layernorm(0)
                xt_lo(0, 0)
                blocks(dve, turn)
                add_expert(NBLK - 1, ROUNDS - 1, NE - 1)
                square(NBLK - 1, ROUNDS - 1)
                normalize(NBLK - 1, ROUNDS - 1)
        clear_semaphores(nc, S.values())


def build_mixture(nc, W, w, y_dram, out):
    with ExitStack() as ctx:
        def sb(name, shape, dt=F32):
            return ctx.enter_context(nc.sbuf_tensor(name, shape, dt))
        W = dict(W)
        for k, n in (("up", NE), ("gate", E + 1), ("down", E + 1)):
            W[k + "_hi"] = sb(k + "_hi", [P, n, DT, I], F32R)
            W[k + "_lo"] = sb(k + "_lo", [P, n, DT, I], F32R)
        W["router_hi"] = sb("router_hi", [P, ROUNDS, DT, E], F32R)
        W["router_lo"] = sb("router_lo", [P, ROUNDS, DT, E], F32R)
        W["b_up"], W["b_gate"] = sb("b_up", [P, 2 * NE]), sb("b_gate", [P, 2 * NE])
        W["b_down"] = sb("b_down", [NE, D])
        W["router_b"], W["gate_bias"] = sb("router_b", [P, ROUNDS, E]), sb("gate_bias", [P, ROUNDS, E])
        W["norm_w"] = sb("norm_w", [P, ROUNDS, D])
        W["earlier"] = sb("earlier", [P, TPB, E, E])
        build_mixture_weights(nc, W, w)
        F = {"y_raw": sb("y_raw", [P, PAIRS, BLK]), "x1": sb("x1", [P, TPB, D]),
             "x1_next": sb("x1_next", [P, TPB, D]), "xn": sb("xn", [P, TPB, D]),
             "xf": sb("xf", [P, TPB, D]), "acc": sb("acc", [P, TPB, D]),
             "parts": sb("parts", [P, 2, 4, 2, BLK], F32R), "h": sb("h", [P, 2, 2, BLK]), "s": sb("s", [P, 2, 2, BLK]),
             "xt_hi": sb("xft_hi", [P, DT, BLK], F32R), "xt_lo": sb("xft_lo", [P, DT, BLK], F32R),
             "st": sb("st", [P, TPB, 6]), "mv": sb("mv", [P, TPB, 2]), "var": sb("var", [P, TPB, 1]),
             "rs": sb("rs", [P, TPB, 1]), "ss": sb("ss", [P, TPB]), "rms": sb("rms", [P, TPB]), "rms_var": sb("rms_var", [P, TPB]),
             "g": sb("g", [P, TPB, E]), "biased": sb("biased", [P, TPB, E]), "rank": sb("rank", [P, TPB, E]),
             "chosen": sb("chosen", [P, TPB, E]), "both": sb("both", [P, TPB]), "diff": sb("diff", [P, TPB, E]),
             "tanh": sb("tanh", [P, TPB, E]), "beaten": sb("beaten", [P, TPB, E, E]), "equal": sb("equal", [P, TPB, E, E]),
             "weights": sb("weights", [P, TPB, NE]), "weights_t": sb("weights_t", [NE, BLK])}
        x_v = w["x"].rearrange("b (q j p) d -> (b q) p j d", p=P, j=TPB)
        out_v = out.rearrange("b (q j p) d -> (b q) p j d", p=P, j=TPB)
        y_v = y_dram.rearrange("b q p h n -> (b q) p h n")
        nc.disable_value_cache = True
        build_tokens(nc, W, F, y_v, x_v, out_v)
        nc.disable_value_cache = False


def build(nc, w, out):
    y_dram = nc.dram_tensor("y_latent", [B, QB, P, PAIRS, BLK], F32).ap()
    recip_rows = nc.dram_tensor("recip_rows", [QB, P, TPB], F32).ap()
    with ExitStack() as ctx:
        T = shared_tensors(nc, ctx)
        with ExitStack() as attention:
            A = dict(T) | attention_tensors(nc, attention)
            build_weights(nc, A, w)
            with nc.Fori(0, B) as b:
                build_latents(nc, A, w["x"][b])
                nc.disable_value_cache = True
                build_attention(nc, A, y_dram[b], recip_rows)
                nc.disable_value_cache = False
        build_mixture(nc, T, w, y_dram, out)


def kernel(L0_attn_x_bld, L0_attn_Wq, L0_attn_Wkv_down, L0_attn_Wk_up, L0_attn_Wv_up, L0_attn_Wout,
           L0_ffn_router_W, L0_ffn_router_b, L0_ffn_gate_bias, L0_ffn_exp_Wup, L0_ffn_exp_bup, L0_ffn_exp_Wg,
           L0_ffn_exp_bg, L0_ffn_exp_Wdown, L0_ffn_exp_bdown, L0_ffn_share_Wup, L0_ffn_share_bup, L0_ffn_share_Wg,
           L0_ffn_share_bg, L0_ffn_share_Wdown, L0_ffn_share_bdown, L0_ffn_norm_w):
    import concourse.bacc as bacc
    from concourse.bass_utils import run_bass_kernel_spmd as run

    def per_partition(*biases):
        rows = np.concatenate([np.asarray(b).reshape(-1, 2, P) for b in biases])
        return rows.transpose(2, 0, 1).reshape(P, -1)

    def every_partition(a):
        return np.broadcast_to(np.asarray(a)[None], (P, *np.asarray(a).shape))

    a = np.asarray
    arrays = {
        "x": a(L0_attn_x_bld), "wqT": a(L0_attn_Wq).transpose(1, 2, 0), "wkT": a(L0_attn_Wk_up).transpose(1, 2, 0),
        "wvT": a(L0_attn_Wv_up).transpose(1, 2, 0), "wout": a(L0_attn_Wout), "wdown": a(L0_attn_Wkv_down),
        "router_w": a(L0_ffn_router_W), "router_b": every_partition(L0_ffn_router_b),
        "gate_bias": every_partition(L0_ffn_gate_bias), "norm_w": every_partition(L0_ffn_norm_w),
        "exp_up": a(L0_ffn_exp_Wup), "exp_gate": a(L0_ffn_exp_Wg), "exp_down": a(L0_ffn_exp_Wdown),
        "share_up": a(L0_ffn_share_Wup), "share_gate": a(L0_ffn_share_Wg), "share_down": a(L0_ffn_share_Wdown),
        "b_up": per_partition(L0_ffn_exp_bup, L0_ffn_share_bup),
        "b_gate": per_partition(L0_ffn_exp_bg, L0_ffn_share_bg, L0_ffn_share_bg),
        "b_down": np.concatenate([a(L0_ffn_exp_bdown), a(L0_ffn_share_bdown)[None], a(L0_ffn_share_bdown)[None]]),
    }
    arrays = {n: np.ascontiguousarray(v) for n, v in arrays.items()}
    nc = bacc.Bacc("TRN2", target_bir_lowering=False, num_devices=1)
    w = {n: nc.dram_tensor("in_" + n, v.shape, mybir.dt.from_np(v.dtype), kind="ExternalInput").ap() for n, v in arrays.items()}
    out = nc.dram_tensor("out", (B, L, D), F32, kind="ExternalOutput").ap()
    build(nc, w, out)
    r = run(nc, [{"in_" + n: v for n, v in arrays.items()}], core_ids=[0])
    return r.results[0]["out"]
```

```python
from contextlib import ExitStack

import numpy as np
import concourse.bass as bass
from concourse import mybir

F32 = mybir.dt.float32
F32R = mybir.dt.float32r
ALU = mybir.AluOpType
ACT = mybir.ActivationFunctionType
AX = mybir.AxisListType

P = 128
B, L, D = 2, 2048, 256
H, HD, LD = 16, 64, 64
E, I = 6, 256
NE = 8
ROUNDS = 2
DT = D // P
BLK = 512
TPB = BLK // P
QB = L // BLK
KT = L // P
PAIRS = H // 2
NBLK = B * QB
SCALE = float(HD) ** -0.5
MASK = -1.0e30
LN_EPS, RMS_EPS = 1e-5, 1e-6
DMA = 16

SCORE_STEPS = [(qb, kt) for qb in range(QB) for kt in range(TPB * (qb + 1))]
MAX_STEPS = [(TPB * qb + j, c) for qb in range(QB) for j in range(TPB) for c in range(qb + 1)]
STEPS = len(SCORE_STEPS)
INVERT_AFTER = 8
DIVIDE_AFTER = 13
LAG = 5
RING = 8


def f32(ap):
    return ap.bitcast(F32)


def clear_semaphores(nc, sems):
    for s in sems:
        nc.sync.sem_clear(s)
    nc.all_engine_barrier()


def build_weights(nc, T, w):
    with ExitStack() as ctx:
        def sb(name, shape, dt=F32):
            return ctx.enter_context(nc.sbuf_tensor(name, shape, dt))
        names = ["qk_loaded", "vo_loaded", "d_loaded", "zeroed", "made", "m_ready", "n_ready", "hi_done", "lo_done"]
        S = {n: ctx.enter_context(nc.semaphore("w_" + n)) for n in names}
        wq = sb("wq", [HD, H, D])
        wk = sb("wk", [HD, H, LD])
        wv = sb("wv", [HD, H, LD])
        wo = sb("wo", [HD, H, D])
        wd = sb("wd", [P, DT, LD])
        ps = T["ps"]
        with nc.Block() as block:
            @block.sync
            def _(sp):
                sp.dma_start(wq[:, :, :], w["wqT"].rearrange("h k d -> k h d")).then_inc(S["qk_loaded"], DMA)
                sp.dma_start(wk[:, :, :], w["wkT"].rearrange("h k c -> k h c")).then_inc(S["qk_loaded"], DMA)
                sp.dma_start(wv[:, :, :], w["wvT"].rearrange("h k c -> k h c")).then_inc(S["vo_loaded"], DMA)
                sp.dma_start(wo[:, :, :], w["wout"].rearrange("h k d -> k h d")).then_inc(S["vo_loaded"], DMA)
                sp.dma_start(wd[:, :, :], w["wdown"].rearrange("(t p) c -> p t c", p=P)).then_inc(S["d_loaded"], DMA)

            @block.gpsimd
            def _(pool):
                pool.memset(T["ident"][:, :], 0.0).then_inc(S["zeroed"], 1)
                pool.memset(T["mask_kq"][:, :], 0.0).then_inc(S["zeroed"], 1)
                pool.memset(T["mask_qk"][:, :], 0.0).then_inc(S["zeroed"], 1)
                pool.memset(T["minus_half"][:, :], -0.5).then_inc(S["zeroed"], 1)
                pool.wait_ge(S["zeroed"], 4)
                pool.affine_select(out=T["ident"][:, :], in_=T["ident"][:, :], compare_op=ALU.not_equal, fill=1.0,
                                   base=0, pattern=[[-1, P]], channel_multiplier=1).then_inc(S["made"], 1)
                for mask, sign in ((T["mask_kq"], 1), (T["mask_qk"], -1)):
                    pool.affine_select(out=mask[:, :], in_=mask[:, :], compare_op=ALU.is_ge, fill=MASK,
                                       base=0, pattern=[[sign, P]], channel_multiplier=-sign).then_inc(S["made"], 1)

            @block.tensor
            def _(pe):
                pe.wait_ge(S["qk_loaded"], 2 * DMA)
                for dt in range(DT):
                    for h in range(H):
                        mm = pe.matmul(ps[:, 2 * dt + h // 8, (h % 8) * LD:(h % 8 + 1) * LD],
                                       wq[:, h, dt * P:(dt + 1) * P], wk[:, h, :], start=True, stop=True)
                mm.then_inc(S["m_ready"], 1)
                pe.wait_ge(S["vo_loaded"], 2 * DMA)
                for h in range(H):
                    half, pr = h % 2, h // 2
                    mm = pe.matmul(ps[half * LD:(half + 1) * LD, 4 + pr // 2, (pr % 2) * D:(pr % 2 + 1) * D],
                                   wv[:, h, :], wo[:, h, :], start=True, stop=True)
                mm.then_inc(S["n_ready"], 1)

            @block.scalar
            def _(act):
                act.wait_ge(S["m_ready"], 1)
                for dt in range(DT):
                    for b2 in range(2):
                        act.activation(T["m_hi"][:, 4 * b2:4 * b2 + 4, dt, :], ps[:, 2 * dt + b2, :].rearrange(
                            "p (a c) -> p a c", c=P), ACT.Copy, scale=SCALE).then_inc(S["hi_done"], 1)
                act.wait_ge(S["n_ready"], 1)
                for b2 in range(4):
                    act.activation(T["n_hi"][:, 2 * b2:2 * b2 + 2, :], ps[:, 4 + b2, :].rearrange(
                        "p (a c) -> p a c", c=D), ACT.Copy).then_inc(S["hi_done"], 1)
                act.wait_ge(S["d_loaded"], DMA)
                for half in range(2):
                    act.activation(T["wd_hi"][:, :, half * LD:(half + 1) * LD], wd[:, :, :],
                                   ACT.Copy).then_inc(S["hi_done"], 1)

            @block.vector
            def _(dve):
                n = 0
                for dt in range(DT):
                    for b2 in range(2):
                        n += 1
                        dve.wait_ge(S["hi_done"], n)
                        dve.scalar_tensor_tensor(
                            out=T["m_lo"][:, 4 * b2:4 * b2 + 4, dt, :],
                            in0=ps[:, 2 * dt + b2, :].rearrange("p (a c) -> p a c", c=P), scalar=SCALE,
                            in1=f32(T["m_hi"][:, 4 * b2:4 * b2 + 4, dt, :]),
                            op0=ALU.mult, op1=ALU.subtract).then_inc(S["lo_done"], 1)
                for b2 in range(4):
                    n += 1
                    dve.wait_ge(S["hi_done"], n)
                    dve.tensor_tensor(T["n_lo"][:, 2 * b2:2 * b2 + 2, :],
                                      ps[:, 4 + b2, :].rearrange("p (a c) -> p a c", c=D),
                                      f32(T["n_hi"][:, 2 * b2:2 * b2 + 2, :]), ALU.subtract).then_inc(S["lo_done"], 1)
                for half in range(2):
                    n += 1
                    dve.wait_ge(S["hi_done"], n)
                    dve.tensor_tensor(T["wd_lo"][:, :, half * LD:(half + 1) * LD], wd[:, :, :],
                                      f32(T["wd_hi"][:, :, half * LD:(half + 1) * LD]),
                                      ALU.subtract).then_inc(S["lo_done"], 1)
        clear_semaphores(nc, S.values())


BANK_JOBS = [(1, "row", 0, 3), (5, "row", 1, 0), (8, "proj", 2, 0), (13, "row", 1, 1), (16, "proj", 2, 1),
             (25, "row", 1, 2), (28, "proj", 2, 2), (34, "proj", 2, 3), (41, "row", 1, 3),
             (45, "row", 2, 0), (53, "row", 2, 1), (65, "row", 2, 2)]
SPLITS = [(6, 1, 3), (9, 2, 0), (17, 2, 1), (29, 2, 2), (44, 2, 3), (47, 3, 0), (54, 3, 1), (66, 3, 2)]
FIRST_ROWS = 3
FIRST_SPLITS = 7
ON_DVE = [s % STEPS in (10, 20, 30) for s in range(2 * STEPS)]
DVE_LOS, POOL_LOS = sum(ON_DVE), 2 * STEPS - sum(ON_DVE)


def los_before(s, on_dve):
    return sum(1 for t in range(s) if ON_DVE[t] == on_dve)


def same_bank_before(s):
    return s - 3 if s >= 3 else max(t for t in range(2 * STEPS) if t % 3 == s) - 2 * STEPS


def is_diagonal(s):
    qb, kt = SCORE_STEPS[s % STEPS]
    return kt >= TPB * qb


def diagonals_before(s):
    return sum(is_diagonal(t) for t in range(s))


DIAGONALS = diagonals_before(2 * STEPS)


def block_end(qb):
    return 2 * (qb + 1) * (qb + 2) - 1


def build_attention(nc, T, x_seq, y_seq, recip_rows):
    with ExitStack() as ctx:
        def sb(name, shape, dt=F32):
            return ctx.enter_context(nc.sbuf_tensor(name, shape, dt))
        names = ["loaded0", "loaded1", "loaded2", "loaded3",
                 "stats", "mean", "var", "rstd",
                 "x_normed",
                 "turned",
                 "x_hi", "x_lo",
                 "lat",
                 "k_hi", "lat_copied", "k_lo",
                 "lat_turned",
                 "v_hi", "v_lo",
                 "filled",
                 "staged",
                 "max_scored",
                 "max_masked",
                 "max_read",
                 "block_max",
                 "bank_made",
                 "bank_read",
                 "q_hi", "q_lo", "q_copy",
                 "scored",
                 "masked",
                 "probs",
                 "probs_hi",
                 "lo_dve", "lo_pool",
                 "latent_used",
                 "y_copied",
                 "sums_in",
                 "recip",
                 "recip_out",
                 "recip_in",
                 "normed",
                 "stored0", "stored1", "stored2", "stored3",
                 "row_in0", "row_in1", "row_in2", "row_in3"]
        S = {n: ctx.enter_context(nc.semaphore("a_" + n)) for n in names}
        stage_hi = sb("stage_hi", [P, DT, P], F32R)
        stage_lo = sb("stage_lo", [P, DT, P], F32R)
        q_raw = sb("q_raw", [P, L])
        qa = [sb(f"q_parts{i}", [P, L], F32R) for i in range(2)]
        qc = [sb(f"q_row{i}", [LD + 1, L], F32R) for i in range(2)]
        pr = sb("pr", [P, RING, BLK])
        ph = sb("ph", [P, RING, BLK], F32R)
        pl = sb("pl", [P, RING, BLK], F32R)
        part = sb("part", [P, 2, TPB, QB])
        mx = sb("mx", [P, 2, TPB])
        max_rows = sb("max_rows", [TPB, QB, P], F32R)
        y = sb("y_sums", [P, QB, BLK])
        sums = sb("sums", [P, QB, TPB])
        rec = sb("rec", [LD, QB, BLK])
        lat = rec[:, :, :].rearrange("p q n -> p (q n)")
        x = pr[:, :, :].rearrange("p r (t d) -> p (r t) d", d=D)
        st, mv, rs, ve = (y[:, i, 0:KT * n].rearrange("p (t n) -> p t n", n=n)
                          for i, n in enumerate((6, 2, 1, 1)))
        x_v = x_seq.rearrange("(t p) d -> p t d", p=P)
        ps, xh, xl, kh, kl, va, vc = (T[k] for k in ("ps", "xt_hi", "xt_lo", "k_hi", "k_lo", "v_hi", "v_lo"))

        SCORE_BANK, MAX_BANK, Y_BANK, BANK = 0, 3, 5, 7
        TURN_BANKS = [(0, 1), (2, 5)]
        LAT_BANK = 6

        START_JOBS = [("proj", 0), ("proj", 1), ("row", 0), ("proj", 2), ("row", 1), ("proj", 3), ("row", 2)]

        def project_job(qb):
            return START_JOBS.index(("proj", qb))

        def first_row_job(qb):
            return START_JOBS.index(("row", qb))

        def first_max_steps(g):
            steps = [m for m in range(STEPS) if MAX_STEPS[m][0] // TPB == g]
            return steps[:TPB], steps[TPB:]

        def jobs_at(s, last):
            kept = [j for j in BANK_JOBS if not (last and j[2] == 2)]
            return [(n, j) for n, j in enumerate(kept) if j[0] == s]

        def splits_at(s, last):
            kept = [j for j in SPLITS if not (last and j[1] >= 2)]
            return [(n, j) for n, j in enumerate(kept) if j[0] == s]

        def row_job(head, qb, last):
            kept = [j for j in BANK_JOBS if not (last and j[2] == 2)]
            at = [n for n, j in enumerate(kept) if j[1:] == ("row", head, qb)]
            if at:
                return at[0] + 1
            at = [n for n, j in enumerate(BANK_JOBS) if j[1:] == ("row", head + 2, qb)]
            return at[0] + 1 - len(BANK_JOBS)

        FIRST_JOBS = QB + FIRST_ROWS
        NJOBS, NSPLITS = len(BANK_JOBS), len(SPLITS)

        def turns(eng, turn):
            turn(0, True, False)
            with eng.Fori(1, PAIRS - 1) as p:
                turn(p, False, False)
            turn(PAIRS - 1, False, True)

        def block_jobs(job, s, after, p, first):
            for half in range(2):
                for qb in range(QB):
                    at = STEPS * half + block_end(qb) + after
                    if at == s:
                        job(p, half, qb)
                    elif at == s + 2 * STEPS and not first:
                        job(p - 1, half, qb)

        def late_jobs(job, after):
            for half in range(2):
                for qb in range(QB):
                    if STEPS * half + block_end(qb) + after >= 2 * STEPS:
                        job(PAIRS - 1, half, qb)

        def split_waits(p, head, qb, first):
            jobs = [n for n, j in enumerate(BANK_JOBS) if j[1:] == ("proj", 2, qb)]
            read = FIRST_JOBS + NJOBS * p + jobs[0] + 1
            if head == 1:
                return (project_job(QB - 1) + 1, None) if first else (FIRST_JOBS + NJOBS * (p - 1) + jobs[0] + 1, 2 * STEPS * p)
            return read, 2 * STEPS * p + STEPS * (head - 2) + block_end(qb) + 1

        def wait_lo(eng, p, s):
            if s < 0:
                p, s = p - 1, s + 2 * STEPS
            if ON_DVE[s]:
                eng.wait_ge(S["lo_dve"], DVE_LOS * p + los_before(s + 1, True))
            else:
                eng.wait_ge(S["lo_pool"], POOL_LOS * p + los_before(s + 1, False))

        def make_lo(eng, p, s, first, sem):
            qb, kt = SCORE_STEPS[s % STEPS]
            w = BLK - P * max(0, kt - TPB * qb)
            eng.wait_ge(S["probs_hi"], 2 * STEPS * p + s + 1)
            if not (first and s < RING):
                eng.wait_ge(S["latent_used"], 2 * STEPS * p + s - RING + 1)
            eng.tensor_tensor(pl[:, s % RING, 0:w], pr[:, s % RING, 0:w], f32(ph[:, s % RING, 0:w]),
                              ALU.subtract).then_inc(sem, 1)

        with nc.Block() as block:
            @block.sync
            def _(sp):
                def stage(pair, projected):
                    if projected is not None:
                        sp.wait_ge(S["bank_made"], projected)
                    sp.dma_start(f32(stage_hi[:, :, :]), f32(T["m_hi"][:, pair, :, :])).then_inc(S["staged"], DMA)
                    sp.dma_start(f32(stage_lo[:, :, :]), f32(T["m_lo"][:, pair, :, :])).then_inc(S["staged"], DMA)

                def divide(p, half, qb):
                    n = 8 * p + 4 * half + qb
                    sp.wait_ge(S["y_copied"], n + 1)
                    sp.dma_start(sums[:, qb, :], y[LD:LD + 1, qb, :]).then_inc(S["sums_in"], DMA)
                    sp.wait_ge(S["recip"], n + 1)
                    sp.dma_start(recip_rows[qb], sums[:, qb, :]).then_inc(S["recip_out"], DMA)
                    sp.wait_ge(S["recip_out"], DMA * (n + 1))
                    sp.dma_start(rec[:, qb, :], recip_rows[qb:qb + 1, :, :].rearrange("a p j -> a (p j)").broadcast_to(
                        [LD, BLK])).then_inc(S["recip_in"], DMA)

                def store(p, half, qb):
                    sp.wait_ge(S["normed"], 8 * p + 4 * half + qb + 1)
                    sp.dma_start(y_seq[qb, half * LD:(half + 1) * LD, p, :], y[0:LD, qb, :]).then_inc(S[f"stored{qb}"], DMA)

                def turn(p, more, first=False):
                    for half in range(2):
                        for qb in range(QB):
                            divide(p, half, qb)
                            if half or qb:
                                store(p, half - (qb == 0), (qb - 1) % QB)
                            elif not first:
                                store(p - 1, 1, QB - 1)
                            if more and (half, qb) == (0, 2):
                                stage(p + 2, FIRST_JOBS + NJOBS * p + 8)

                for g in range(QB):
                    sp.dma_start(x[:, TPB * g:TPB * (g + 1), :],
                                 x_v[:, TPB * g:TPB * (g + 1), :]).then_inc(S[f"loaded{g}"], DMA)
                    if g == 0:
                        stage(0, None)
                stage(1, project_job(QB - 1) + 1)
                turn(0, True, first=True)
                with sp.Fori(1, PAIRS - 2) as p:
                    turn(p, True)
                with sp.Fori(PAIRS - 2, PAIRS) as p:
                    turn(p, False)
                store(PAIRS - 1, 1, QB - 1)
                for qb in range(QB):
                    sp.wait_ge(S[f"stored{qb}"], DMA * H)

            @block.tensor
            def _(pe):
                def project(pair, qb, job):
                    pe.wait_ge(S["staged"], 2 * DMA * (pair + 1))
                    if not isinstance(job, int) or job > 0:
                        pe.wait_ge(S["bank_read"], job)
                    c = slice(BLK * qb, BLK * (qb + 1))
                    terms = [(a, m, dt) for a, m in ((stage_hi, xh), (stage_hi, xl), (stage_lo, xh)) for dt in range(DT)]
                    for n, (a, m, dt) in enumerate(terms):
                        mm = pe.matmul(ps[:, BANK, :], a[:, dt, :], m[:, dt, c], start=n == 0, stop=n == len(terms) - 1)
                    mm.then_inc(S["bank_made"], 1)

                def row(qb, head, job):
                    if qb == 0:
                        pe.wait_ge(S["max_read"], STEPS * head + TPB)
                    else:
                        pe.wait_ge(S["block_max"], (QB - 1) * head + qb)
                    pe.wait_ge(S["bank_read"], job)
                    pe.transpose(ps[0:TPB, BANK, 0:P], mx[:, qb % 2, :], T["ident"][:, :]).then_inc(S["bank_made"], 1)

                def max_scores(half, m, split_no, n, first=False):
                    i, c = MAX_STEPS[m]
                    if c == 0 and i % TPB == 0:
                        pe.wait_ge(S["q_hi"], split_no + 1)
                        pe.wait_ge(S["q_lo"], split_no + 1)
                    if not first:
                        pe.wait_ge(S["max_read"], n - 1)
                    w = BLK if c < i // TPB else P * (i % TPB + 1)
                    pe.matmul(ps[:, MAX_BANK + m % 2, 0:w], qa[half][:, i * P:(i + 1) * P],
                              kh[:, c * BLK:c * BLK + w], start=True, stop=True).then_inc(S["max_scored"], 1)

                def scores(half, m, s, p, first, last):
                    qb, kt = SCORE_STEPS[m]
                    off = P * max(0, kt - TPB * qb)
                    if kt == 0:
                        pe.wait_ge(S["q_copy"], 8 * p + 4 * half + qb + 1)
                        pe.wait_ge(S[f"row_in{qb}"], DMA * (2 * p + half + 1))
                    if not (first and s < 3):
                        pe.wait_ge(S["probs_hi"], 2 * STEPS * p + same_bank_before(s) + 1)
                    out = ps[:, SCORE_BANK + s % 3, 0:BLK - off]
                    q = slice(BLK * qb + off, BLK * (qb + 1))
                    k = slice(kt * P, (kt + 1) * P)
                    pe.matmul(out, kh[:, k], qa[half][:, q], start=True, stop=False)
                    pe.matmul(out, kl[0:LD + 1, k], qc[half][:, q], start=False, stop=True).then_inc(S["scored"], 1)

                def use_latents(p, s):
                    half, m = s // STEPS, s % STEPS
                    qb, kt = SCORE_STEPS[m]
                    off = P * max(0, kt - TPB * qb)
                    pe.wait_ge(S["probs_hi"], 2 * STEPS * p + s + 1)
                    if ON_DVE[s]:
                        pe.wait_ge(S["lo_dve"], DVE_LOS * p + los_before(s + 1, True))
                    else:
                        pe.wait_ge(S["lo_pool"], POOL_LOS * p + los_before(s + 1, False))
                    if kt == 0:
                        n = 4 * half + qb
                        if not isinstance(p, int) or 8 * p + n >= 2:
                            pe.wait_ge(S["y_copied"], 8 * p + n - 1)
                    out = ps[:, Y_BANK + qb % 2, off:BLK]
                    b = s % RING
                    w = BLK - off
                    pe.matmul(out, va[:, kt, :], ph[:, b, 0:w], start=kt == 0, stop=False)
                    pe.matmul(out, vc[:, kt, :], ph[:, b, 0:w], start=False, stop=False)
                    pe.matmul(out, va[:, kt, :], pl[:, b, 0:w], start=False,
                              stop=kt == TPB * (qb + 1) - 1).then_inc(S["latent_used"], 1)

                def turn(p, first, last):
                    for s in range(2 * STEPS):
                        half, m = s // STEPS, s % STEPS
                        if not (last and half == 1):
                            split_no = 8 * p + 4 * (half + 1) + MAX_STEPS[m][0] // TPB
                            max_scores(1 - half, m, split_no, STEPS + 2 * STEPS * p + s)
                        for n, (_, kind, head, qb) in jobs_at(s, last):
                            job = FIRST_JOBS + NJOBS * p + n
                            if kind == "row":
                                row(qb, 2 * p + head, job)
                            else:
                                project(p + 1, qb, job)
                        scores(half, m, s, p, first, last)
                        if s >= LAG:
                            use_latents(p, s - LAG)
                        elif not first:
                            use_latents(p - 1, 2 * STEPS + s - LAG)

                def turn_x(g):
                    pe.wait_ge(S["x_normed"], TPB * (g + 1))
                    if g >= 2:
                        pe.wait_ge(S["x_lo"], DT * (g - 1))
                    for dt in range(DT):
                        for j in range(TPB):
                            mm = pe.transpose(ps[:, TURN_BANKS[g % 2][dt], j * P:(j + 1) * P],
                                              x[:, TPB * g + j, dt * P:(dt + 1) * P], T["ident"][:, :])
                    mm.then_inc(S["turned"], 1)

                def latents(g):
                    c = slice(BLK * g, BLK * (g + 1))
                    if g:
                        pe.wait_ge(S["v_lo"], g)
                    terms = [(a, m, dt) for a, m in (("wd_hi", xh), ("wd_hi", xl), ("wd_lo", xh)) for dt in range(DT)]
                    for n, (a, m, dt) in enumerate(terms):
                        mm = pe.matmul(ps[:, LAT_BANK, :], T[a][:, dt, :], m[:, dt, c],
                                       start=n == 0, stop=n == len(terms) - 1)
                    mm.then_inc(S["lat"], 1)

                def turn_latents(g):
                    pe.wait_ge(S["lat_copied"], g + 1)
                    for j in range(TPB):
                        t = TPB * g + j
                        mm = pe.transpose(ps[:, LAT_BANK, j * LD:(j + 1) * LD], lat[:, t * P:(t + 1) * P],
                                          T["ident"][0:LD, 0:LD])
                    mm.then_inc(S["lat_turned"], 1)

                def start_project(g):
                    pe.wait_ge(S["x_lo"], DT * (g + 1))
                    project(0, g, project_job(g))

                turn_x(0)
                turn_x(1)
                start_project(0)
                latents(0)
                turn_latents(0)
                for g in range(QB):
                    if g:
                        row(g - 1, 0, first_row_job(g - 1))
                    early, late = first_max_steps(g)
                    for n, m in enumerate(early + late):
                        max_scores(0, m, g, m, first=m < 2)
                        if n == 0 and g + 1 < QB:
                            start_project(g + 1)
                        if n == 1 and g + 1 < QB:
                            latents(g + 1)
                        if n == 2 and g + 2 < QB:
                            turn_x(g + 2)
                        if n == 3 and g + 1 < QB:
                            turn_latents(g + 1)
                pe.wait_ge(S["v_lo"], QB)
                pe.wait_ge(S["k_lo"], QB)
                pe.wait_ge(S["filled"], 3)
                turns(pe, turn)
                for s in range(2 * STEPS - LAG, 2 * STEPS):
                    use_latents(PAIRS - 1, s)

            @block.scalar
            def _(act):
                def read_queries(pair, qb, job, first=False):
                    act.wait_ge(S["bank_made"], job + 1)
                    if not first:
                        act.wait_ge(S["q_hi"], 8 * (pair - 1) + 4 + qb + 1)
                        act.wait_ge(S["q_lo"], 8 * (pair - 1) + 4 + qb + 1)
                        act.wait_ge(S["q_copy"], 8 * (pair - 1) + 4 + qb + 1)
                    act.activation(q_raw[:, BLK * qb:BLK * (qb + 1)], ps[:, BANK, :], ACT.Copy).then_inc(S["bank_read"], 1)

                def read_row(head, half, qb, job):
                    act.wait_ge(S["bank_made"], job + 1)
                    if not isinstance(head, int) or head >= 1:
                        act.wait_ge(S[f"row_in{qb}"], DMA * head)
                    act.activation(max_rows[:, qb, :], ps[0:TPB, BANK, 0:P], ACT.Copy).then_inc(S["bank_read"], 1)
                    act.wait_ge(S["bank_read"], job + 1)
                    act.dma_start(f32(qc[half][LD:LD + 1, BLK * qb:BLK * (qb + 1)]),
                                  f32(max_rows[:, qb, :])).then_inc(S[f"row_in{qb}"], DMA)

                def copy_queries(half, qb, read, scored):
                    if read is not None:
                        act.wait_ge(S["bank_read"], read)
                    if scored is not None:
                        act.wait_ge(S["scored"], scored)
                    c = slice(BLK * qb, BLK * (qb + 1))
                    act.activation(qc[half][0:LD, c], q_raw[half * LD:(half + 1) * LD, c], ACT.Copy).then_inc(S["q_copy"], 1)

                def copy_sums(p, half, qb):
                    act.wait_ge(S["latent_used"], 2 * STEPS * p + STEPS * half + block_end(qb) + 1)
                    if not isinstance(p, int) or 2 * p + half >= 1:
                        act.wait_ge(S[f"stored{qb}"], DMA * (2 * p + half))
                    act.activation(y[:, qb, :], ps[:, Y_BANK + qb % 2, :], ACT.Copy).then_inc(S["y_copied"], 1)

                def turn(p, first, last):
                    for s in range(2 * STEPS):
                        block_jobs(copy_sums, s, LAG + 1, p, first)
                        qb, kt = SCORE_STEPS[s % STEPS]
                        w = BLK - P * max(0, kt - TPB * qb)
                        if is_diagonal(s):
                            act.wait_ge(S["masked"], DIAGONALS * p + diagonals_before(s + 1))
                        else:
                            act.wait_ge(S["scored"], 2 * STEPS * p + s + 1)
                        src = ps[:, SCORE_BANK + s % 3, 0:w]
                        if not (first and s < RING):
                            wait_lo(act, p, s - RING)
                        act.activation(pr[:, s % RING, 0:w], src, ACT.Exp).then_inc(S["probs"], 1)
                        if not (first and s < RING):
                            act.wait_ge(S["latent_used"], 2 * STEPS * p + s - RING + 1)
                        act.activation(ph[:, s % RING, 0:w], src, ACT.Exp).then_inc(S["probs_hi"], 1)
                        for n, (_, kind, head, jqb) in jobs_at(s, last):
                            job = FIRST_JOBS + NJOBS * p + n
                            if kind == "row":
                                read_row(2 * p + head, head % 2, jqb, job)
                            else:
                                read_queries(p + 1, jqb, job)
                        for n, (_, head, jqb) in splits_at(s, last):
                            copy_queries(head % 2, jqb, *split_waits(p, head, jqb, first))

                def x_hi(g):
                    act.wait_ge(S["turned"], g + 1)
                    for dt in range(DT):
                        act.activation(xh[:, dt, BLK * g:BLK * (g + 1)], ps[:, TURN_BANKS[g % 2][dt], :],
                                       ACT.Copy).then_inc(S["x_hi"], 1)

                def latents_hi(g):
                    c = slice(BLK * g, BLK * (g + 1))
                    act.wait_ge(S["lat"], g + 1)
                    act.activation(kh[:, c], ps[:, LAT_BANK, :], ACT.Copy).then_inc(S["k_hi"], 1)
                    act.activation(lat[:, c], ps[0:LD, LAT_BANK, :], ACT.Copy).then_inc(S["lat_copied"], 1)

                def values_hi(g):
                    act.wait_ge(S["lat_turned"], g + 1)
                    act.activation(va[:, TPB * g:TPB * (g + 1), 0:LD],
                                   ps[:, LAT_BANK, 0:TPB * LD].rearrange("p (t c) -> p t c", c=LD),
                                   ACT.Copy).then_inc(S["v_hi"], 1)

                def start_group(g):
                    read_queries(0, g, project_job(g), first=True)
                    latents_hi(g)
                    copy_queries(0, g, project_job(g) + 1, None)

                x_hi(0)
                x_hi(1)
                start_group(0)
                values_hi(0)
                for g in range(QB):
                    if g:
                        read_row(0, 0, g - 1, first_row_job(g - 1))
                    if g + 1 < QB:
                        start_group(g + 1)
                    if g + 2 < QB:
                        x_hi(g + 2)
                    if g + 1 < QB:
                        values_hi(g + 1)
                for n in range(QB, FIRST_SPLITS):
                    copy_queries(1, n - QB, project_job(n - QB) + 1, None)
                turns(act, turn)
                late_jobs(copy_sums, LAG + 1)

            @block.gpsimd
            def _(pool):
                def split_lo(half, qb, no, los=None):
                    if los is not None:
                        pool.wait_ge(S["lo_pool"], los)
                    c = slice(BLK * qb, BLK * (qb + 1))
                    hi, lo = slice(half * LD, (half + 1) * LD), slice((1 - half) * LD, (2 - half) * LD)
                    pool.wait_ge(S["q_hi"], no + 1)
                    pool.tensor_tensor(qa[half][lo, c], q_raw[hi, c], f32(qa[half][hi, c]),
                                       ALU.subtract).then_inc(S["q_lo"], 1)
                    pool.wait_ge(S["q_lo"], no + 1)

                def turn(p, first, last):
                    for s in range(2 * STEPS):
                        if not ON_DVE[s]:
                            make_lo(pool, p, s, first, S["lo_pool"])
                        for n, (_, head, qb) in splits_at(s, last):
                            split_lo(head % 2, qb, FIRST_SPLITS + NSPLITS * p + n,
                                     POOL_LOS * p + los_before(s + 1, False))

                def fill():
                    pool.memset(f32(kl[LD:LD + 1, :]), -1.0).then_inc(S["filled"], 1)
                    pool.wait_ge(S["filled"], 1)
                    pool.memset(f32(va[:, :, LD:P]), 1.0).then_inc(S["filled"], 1)
                    pool.memset(f32(vc[:, :, LD:P]), 0.0).then_inc(S["filled"], 1)

                def rstd(g):
                    ts = slice(TPB * g, TPB * (g + 1))
                    pool.wait_ge(S["mean"], TPB * (g + 1))
                    pool.tensor_scalar(ve[:, ts, :], mv[:, ts, 1:2], LN_EPS, None, ALU.add).then_inc(S["var"], 1)
                    pool.wait_ge(S["var"], g + 1)
                    pool.tensor_tensor(rs[:, ts, :], ve[:, ts, :], T["minus_half"][:, 0:TPB, None],
                                       ALU.pow).then_inc(S["rstd"], 1)

                def keys_lo(g):
                    c = slice(BLK * g, BLK * (g + 1))
                    pool.wait_ge(S["lat_copied"], g + 1)
                    pool.tensor_tensor(kl[0:LD, c], lat[:, c], f32(kh[0:LD, c]), ALU.subtract).then_inc(S["k_lo"], 1)
                    pool.wait_ge(S["k_lo"], g + 1)

                fill()
                rstd(0)
                rstd(1)
                rstd(2)
                for g in range(QB):
                    pool.wait_ge(S["rstd"], QB if g >= 2 else QB - 1)
                    split_lo(0, g, g)
                    if g == 1:
                        rstd(QB - 1)
                    keys_lo(g)
                for n in range(QB, FIRST_SPLITS):
                    split_lo(1, n - QB, n)
                turns(pool, turn)

            @block.vector
            def _(dve):
                def split_hi(half, qb, read, scored):
                    dve.wait_ge(S["bank_read"], read)
                    if scored is not None:
                        dve.wait_ge(S["scored"], scored)
                    c = slice(BLK * qb, BLK * (qb + 1))
                    hi = slice(half * LD, (half + 1) * LD)
                    dve.tensor_copy(qa[half][hi, c], q_raw[hi, c]).then_inc(S["q_hi"], 1)

                def mask_scores(p, s):
                    src = ps[:, SCORE_BANK + s % 3, 0:P]
                    dve.wait_ge(S["scored"], 2 * STEPS * p + s + 1)
                    dve.tensor_tensor(src, src, T["mask_kq"][:, :], ALU.add).then_inc(S["masked"], 1)

                def invert(p, half, qb):
                    dve.wait_ge(S["sums_in"], DMA * (8 * p + 4 * half + qb + 1))
                    dve.reciprocal(sums[:, qb, :], sums[:, qb, :]).then_inc(S["recip"], 1)

                def divide(p, half, qb):
                    dve.wait_ge(S["recip_in"], DMA * (8 * p + 4 * half + qb + 1))
                    dve.tensor_tensor(y[0:LD, qb, :], y[0:LD, qb, :], rec[:, qb, :], ALU.mult).then_inc(S["normed"], 1)

                def turn(p, first, last):
                    for s in range(2 * STEPS):
                        half, m = s // STEPS, s % STEPS
                        if is_diagonal(s):
                            mask_scores(p, s)
                        if not (last and half == 1):
                            qb = MAX_STEPS[m][0] // TPB
                            h2, q2 = (half + 1, qb - 2) if qb >= 2 else (half, qb + 2)
                            kept = [j for j in BANK_JOBS if not (last and j[2] == 2)]
                            at = [k for k, j in enumerate(kept) if j[1:] == ("row", h2, q2)]
                            if at:
                                made = FIRST_JOBS + NJOBS * p + at[0] + 1
                            else:
                                made = FIRST_JOBS + NJOBS * p + row_job(h2, q2, last)
                            read_max(m, STEPS + 2 * STEPS * p + s, 8 * p + 4 * (half + 1) + qb, made)
                        for n, (_, head, qb) in splits_at(s, last):
                            split_hi(head % 2, qb, *split_waits(p, head, qb, first))
                        if s and ON_DVE[s - 1]:
                            make_lo(dve, p, s - 1, first, S["lo_dve"])
                        block_jobs(invert, s, INVERT_AFTER, p, first)
                        block_jobs(divide, s, DIVIDE_AFTER, p, first)

                def read_max(m, n, block_no, made):
                    i, c = MAX_STEPS[m]
                    j, qb = i % TPB, i // TPB
                    src = ps[:, MAX_BANK + m % 2, :]
                    dst = part[:, qb % 2, j, c:c + 1] if qb else mx[:, 0, j:j + 1]
                    dve.wait_ge(S["max_scored"], n + 1)
                    if qb == 0 and j == 0 and made is not None:
                        dve.wait_ge(S["bank_made"], made)
                    w = BLK if c < qb else P * (j + 1)
                    if c == qb:
                        dve.tensor_tensor(src[:, w - P:w], src[:, w - P:w], T["mask_qk"][:, :],
                                          ALU.add).then_inc(S["max_masked"], 1)
                        dve.wait_ge(S["max_masked"], TPB * block_no + j + 1)
                    ins = dve.tensor_reduce(dst, src[:, 0:w], AX.X, ALU.max)
                    ins.then_inc(S["max_read"], 1)
                    if j == TPB - 1 and c == qb and qb:
                        dve.wait_ge(S["max_read"], n + 1)
                        if made is not None:
                            dve.wait_ge(S["bank_made"], made)
                        dve.tensor_reduce(mx[:, qb % 2, :], part[:, qb % 2, :, 0:qb + 1], AX.X,
                                          ALU.max).then_inc(S["block_max"], 1)

                def moments(g):
                    ts = range(TPB * g, TPB * (g + 1))
                    dve.wait_ge(S[f"loaded{g}"], DMA)
                    for t in ts:
                        dve.bn_stats(st[:, t, :], x[:, t, :]).then_inc(S["stats"], 1)
                    for t in ts:
                        dve.wait_ge(S["stats"], t + 1)
                        dve.bn_aggr(mv[:, t, :], st[:, t, :]).then_inc(S["mean"], 1)

                def norm(g):
                    dve.wait_ge(S["rstd"], g + 1)
                    for t in range(TPB * g, TPB * (g + 1)):
                        dve.tensor_scalar(x[:, t, :], x[:, t, :], mv[:, t, 0:1], rs[:, t, :],
                                          ALU.subtract, ALU.mult).then_inc(S["x_normed"], 1)

                def x_lo(g):
                    for dt in range(DT):
                        dve.wait_ge(S["x_hi"], DT * g + dt + 1)
                        o = (slice(None), dt, slice(BLK * g, BLK * (g + 1)))
                        dve.tensor_tensor(xl[o], ps[:, TURN_BANKS[g % 2][dt], :], f32(xh[o]), ALU.subtract).then_inc(S["x_lo"], 1)

                def values_lo(g):
                    dve.wait_ge(S["v_hi"], g + 1)
                    o = (slice(None), slice(TPB * g, TPB * (g + 1)), slice(0, LD))
                    dve.tensor_tensor(vc[o], ps[:, LAT_BANK, 0:TPB * LD].rearrange("p (t c) -> p t c", c=LD),
                                      f32(va[o]), ALU.subtract).then_inc(S["v_lo"], 1)

                moments(0)
                norm(0)
                moments(1)
                x_lo(0)
                norm(1)
                moments(2)
                x_lo(1)
                split_hi(0, 0, project_job(0) + 1, None)
                values_lo(0)
                for g in range(QB):
                    if g + 2 < QB:
                        norm(g + 2)
                    early, late = first_max_steps(g)
                    made = first_row_job(g - 2) + 1 if g >= 2 else None
                    for m in early:
                        read_max(m, m, g, made)
                    if g + 1 < QB:
                        split_hi(0, g + 1, project_job(g + 1) + 1, None)
                    else:
                        for n in range(QB, FIRST_SPLITS):
                            split_hi(1, n - QB, project_job(n - QB) + 1, None)
                    if g == 0:
                        moments(QB - 1)
                    for m in late:
                        read_max(m, m, g, made)
                    if g + 2 < QB:
                        x_lo(g + 2)
                    if g + 1 < QB:
                        values_lo(g + 1)
                turns(dve, turn)
                late_jobs(invert, INVERT_AFTER)
                late_jobs(divide, DIVIDE_AFTER)
        clear_semaphores(nc, S.values())




def shared_tensors(nc, ctx):
    def sb(name, shape, dt=F32):
        return ctx.enter_context(nc.sbuf_tensor(name, shape, dt))
    return {
        "ps": ctx.enter_context(nc.psum_tensor("ps", [P, 8, BLK], F32)),
        "ident": sb("ident", [P, P]), "minus_half": sb("minus_half", [P, TPB]),
        "n_hi": sb("n_hi", [P, PAIRS, D], F32R), "n_lo": sb("n_lo", [P, PAIRS, D], F32R),
    }


def attention_tensors(nc, ctx):
    def sb(name, shape, dt=F32):
        return ctx.enter_context(nc.sbuf_tensor(name, shape, dt))
    return {
        "mask_kq": sb("mask_kq", [P, P]), "mask_qk": sb("mask_qk", [P, P]),
        "m_hi": sb("m_hi", [P, PAIRS, DT, P], F32R), "m_lo": sb("m_lo", [P, PAIRS, DT, P], F32R),
        "wd_hi": sb("wd_hi", [P, DT, P], F32R), "wd_lo": sb("wd_lo", [P, DT, P], F32R),
        "xt_hi": sb("xt_hi", [P, DT, L], F32R), "xt_lo": sb("xt_lo", [P, DT, L], F32R),
        "k_hi": sb("k_hi", [P, L], F32R), "k_lo": sb("k_lo", [LD + 1, L], F32R),
        "v_hi": sb("v_hi", [P, KT, P], F32R), "v_lo": sb("v_lo", [P, KT, P], F32R),
    }


UNITS = [(kind, e) for e in range(0, NE, 2) for kind in ("up", "gate", "down")]
FIRST_UNITS = 4
UNITS_AT = {0: [4], 1: [5, 6], 2: [7, 8], 3: [9, 10], 4: [11]}


def build_tokens(nc, W, F, w, y_v, x_v, out_v):
    with ExitStack() as ctx:
        names = ["small_in",
                 "slot0", "slot1", "slot2", "slot3", "slot4", "slot5", "slot6", "slot7",
                 "router_hi", "router_lo", "w_hi", "w_lo",
                 "filled",
                 "y_first0", "y_first1", "y_first2", "y_first3",
                 "y_in",
                 "x_in",
                 "y_hi", "y_lo_even", "y_lo_odd",
                 "proj",
                 "x1",
                 "stats", "mean", "var", "rstd",
                 "x_norm",
                 "x1_kept",
                 "turned",
                 "xt_hi", "xt_lo",
                 "up", "h", "h_hi", "h_lo",
                 "gate", "silu", "g", "g_hi", "g_lo",
                 "down",
                 "sum",
                 "routed", "route", "diff", "tanh", "weights",
                 "w_turned", "w_copied", "bias",
                 "seeded",
                 "squared", "squares", "scale_var", "scale",
                 "scaled",
                 "out_ready",
                 "stored",
                 "ones"]
        S = {n: ctx.enter_context(nc.semaphore("f_" + n)) for n in names}
        ps, ident = W["ps"], W["ident"]
        UP, GATE, DOWN, AUX = 0, 2, 4, 6
        PROJ = GATE
        h, s_, xn, xf, x1, x1_next, acc = (F[k] for k in ("h", "s", "xn", "xf", "x1", "x1_next", "acc"))
        y_raw, xth, xtl = F["y_raw"], F["xt_hi"], F["xt_lo"]
        parts = F["parts"]
        y_hi, y_lo = (parts[:, i].rearrange("p k m n -> p (k m) n") for i in range(2))
        H_HI, H_LO, G_HI, G_LO = range(4)
        full = slice(None)
        Q = ROUNDS * NE

        small = ["b_up", "b_gate", "b_down", "router_b", "gate_bias", "norm_w"]
        small_total = DMA * (len(small) + ROUNDS)

        def unit_parts(u):
            kind, e = UNITS[u]
            for n in range(e, min(e + 2, NE if kind == "up" else E + 1)):
                if n < E:
                    yield n, w["exp_" + kind][n]
                else:
                    yield n, w["share_" + kind][:, (n - E) * I:(n - E + 1) * I]

        def unit_slot(u):
            n = u if u < FIRST_UNITS else FIRST_UNITS + (u - FIRST_UNITS) % 4
            mem = F["hs"][:, n] if u < FIRST_UNITS else y_raw[:, 2 * (n - 4):2 * (n - 4) + 2, :]
            return n, mem.rearrange("p a (t i) -> p a t i", i=I)

        def unit_in(u):
            return DMA * sum(len(list(unit_parts(v))) for v in range(u + 1) if unit_slot(v)[0] == unit_slot(u)[0])

        def unit_experts(u):
            n = len(list(unit_parts(u)))
            return slice(UNITS[u][1], UNITS[u][1] + n), n

        def later(t, n):
            return not (isinstance(t, int) and t == 0) or n > 0

        def blocks(eng, turn):
            turn(0, False)
            with eng.Fori(1, NBLK - 1) as t:
                turn(t, False)
            turn(NBLK - 1, True)

        with nc.Block() as block:
            @block.sync
            def _(sp):
                def turn(t):
                    if not (isinstance(t, int) and t == NBLK - 1):
                        sp.wait_ge(S["x1_kept"], t + 1)
                        sp.dma_start(x1_next[:, :, :], x_v[t + 1]).then_inc(S["x_in"], DMA)
                    if not (isinstance(t, int) and t >= NBLK - 2):
                        sp.wait_ge(S["y_lo_even"], PAIRS // 2 * (t + 2))
                        sp.wait_ge(S["y_lo_odd"], PAIRS // 2 * (t + 2))
                        sp.dma_start(y_raw[:, :, :], y_v[t + 2]).then_inc(S["y_in"], DMA)
                    for j in range(TPB):
                        sp.wait_ge(S["out_ready"], TPB * t + j + 1)
                        sp.dma_start(out_v[t][:, j, :], xf[:, j, :]).then_inc(S["stored"], DMA)

                def load_unit(u):
                    n, mem = unit_slot(u)
                    for place, (_, src) in enumerate(unit_parts(u)):
                        sp.dma_start(mem[:, place], src.rearrange("(t p) i -> p t i", p=P)).then_inc(S[f"slot{n}"], DMA)

                for i in range(PAIRS // 2):
                    sp.dma_start(y_raw[:, 2 * i:2 * i + 2, :], y_v[0][:, 2 * i:2 * i + 2, :]).then_inc(S[f"y_first{i}"], DMA)
                sp.dma_start(x1_next[:, :, :], x_v[0]).then_inc(S["x_in"], DMA)
                load_unit(0)
                for n in small:
                    sp.dma_start(W[n][tuple(slice(None) for _ in W[n].shape)], w[n]).then_inc(S["small_in"], DMA)
                for c in range(ROUNDS):
                    sp.dma_start(F["router_raw"][:, c, :, :],
                                 w["router_w"][c].rearrange("(t p) e -> p t e", p=P)).then_inc(S["small_in"], DMA)
                for u in range(1, FIRST_UNITS):
                    load_unit(u)
                sp.wait_ge(S["y_lo_even"], PAIRS // 2)
                sp.wait_ge(S["y_lo_odd"], PAIRS // 2)
                for u in range(FIRST_UNITS, len(UNITS)):
                    if u >= FIRST_UNITS + 4:
                        sp.wait_ge(S["w_lo"], u - 3)
                    load_unit(u)
                sp.wait_ge(S["w_lo"], len(UNITS))
                sp.dma_start(y_raw[:, :, :], y_v[1]).then_inc(S["y_in"], DMA)
                with sp.Fori(0, NBLK - 2) as t:
                    turn(t)
                turn(NBLK - 2)
                turn(NBLK - 1)
                sp.wait_ge(S["stored"], DMA * TPB * NBLK)

            @block.tensor
            def _(pe):
                def project(t, pairs=range(PAIRS)):
                    for pair in pairs:
                        pe.wait_ge(S["y_hi"], PAIRS * t + pair + 1)
                        pe.wait_ge(S["y_lo_odd" if pair % 2 else "y_lo_even"], PAIRS // 2 * t + pair // 2 + 1)
                        if pair == 0 and later(t, 0):
                            pe.wait_ge(S["silu"], 2 * Q * t - Q)
                        for j in range(TPB):
                            for n, (a, b) in enumerate(((y_hi, "hi"), (y_hi, "lo"), (y_lo, "hi"))):
                                mm = pe.matmul(ps[:, PROJ + j // 2, (j % 2) * D:(j % 2 + 1) * D], a[:, pair, j * P:(j + 1) * P],
                                               W["n_" + b][:, pair, :], start=pair == 0 and n == 0 and j % 2 == 0,
                                               stop=pair == PAIRS - 1 and n == 2, skip_group_check=True)
                            if pair == PAIRS - 1 and j % 2:
                                mm.then_inc(S["proj"], 1)

                def turn_tokens(t, c):
                    r = ROUNDS * t + c
                    if later(t, r):
                        pe.wait_ge(S["seeded"], 2 * r)
                    for j in range(TPB):
                        src = xf if c else xn
                        if c:
                            pe.wait_ge(S["scaled"], TPB * r + j + 1 - TPB)
                        else:
                            pe.wait_ge(S["x_norm"], TPB * t + j + 1)
                        for dt in range(DT):
                            mm = pe.transpose(ps[:, AUX + dt, j * P:(j + 1) * P], src[:, j, dt * P:(dt + 1) * P], ident[:, :])
                    mm.then_inc(S["turned"], 1)

                def wide(out, w_hi, w_lo, m, hi, lo):
                    terms = [(a, b, dt) for a, b in ((w_hi, hi), (w_lo, hi), (w_hi, lo)) for dt in range(DT)]
                    for n, (a, b, dt) in enumerate(terms):
                        mm = pe.matmul(out, a[:, dt, m * P:(m + 1) * P], b[:, dt, :], start=n == 0, stop=n == len(terms) - 1)
                    return mm

                def wait_unit(t, c, kind, e):
                    if isinstance(t, int) and t == 0 and c == 0 and e % 2 == 0:
                        pe.wait_ge(S["w_lo"], UNITS.index((kind, e)) + 1)

                def up(t, c, e):
                    q = Q * t + NE * c + e
                    if e == 0:
                        pe.wait_ge(S["xt_hi"], DT * (ROUNDS * t + c + 1))
                        pe.wait_ge(S["xt_lo"], DT * (ROUNDS * t + c + 1))
                    wait_unit(t, c, "up", e)
                    for m in range(2):
                        if later(t, NE * c + e):
                            pe.wait_ge(S["h"], 2 * q - 1 + m)
                        wide(ps[:, UP + m, :], W["up_hi"][:, e], W["up_lo"][:, e], m, xth, xtl).then_inc(S["up"], 1)

                def gate(t, c, e):
                    q, k = Q * t + NE * c + e, min(e, E)
                    pe.wait_ge(S["h_hi"], 2 * q + 2)
                    pe.wait_ge(S["h_lo"], 2 * q + 2)
                    if not e and not (c and isinstance(t, int) and t == NBLK - 1):
                        pe.wait_ge(S["x1"], 2 * (t + c) + 2)
                    wait_unit(t, c, "gate", e)
                    for m in range(2):
                        if later(t, NE * c + e):
                            pe.wait_ge(S["silu"], 2 * q - 1 + m)
                        wide(ps[:, GATE + m, :], W["gate_hi"][:, k], W["gate_lo"][:, k], m,
                             parts[:, e % 2, H_HI], parts[:, e % 2, H_LO]).then_inc(S["gate"], 1)

                def down(t, c, e):
                    q, k = Q * t + NE * c + e, min(e, E)
                    pe.wait_ge(S["g_hi"], 2 * q + 2)
                    pe.wait_ge(S["g_lo"], 2 * q + 2)
                    wait_unit(t, c, "down", e)
                    for j in range(TPB):
                        if j % 2 == 0 and later(t, NE * c + e):
                            pe.wait_ge(S["sum"], TPB * q - TPB + j + 2)
                        terms = [(a, b, dt) for a, b in ((G_HI, "hi"), (G_HI, "lo"), (G_LO, "hi")) for dt in range(DT)]
                        for n, (a, b, dt) in enumerate(terms):
                            mm = pe.matmul(ps[:, DOWN + j // 2, (j % 2) * D:(j % 2 + 1) * D],
                                           parts[:, e % 2, a, dt, j * P:(j + 1) * P], W["down_" + b][:, k, dt, :],
                                           start=n == 0, stop=n == len(terms) - 1)
                        if j % 2:
                            mm.then_inc(S["down"], 1)

                def route(c):
                    for j in range(TPB):
                        terms = [(a, b, dt) for a, b in ((xth, "hi"), (xth, "lo"), (xtl, "hi")) for dt in range(DT)]
                        for n, (a, b, dt) in enumerate(terms):
                            mm = pe.matmul(ps[:, AUX, j * NE:j * NE + E], a[:, dt, j * P:(j + 1) * P],
                                           W["router_" + b][:, c, dt, :], start=n == 0, stop=n == len(terms) - 1)
                    mm.then_inc(S["routed"], 1)

                def turn_weights(t, c):
                    pe.wait_ge(S["weights"], ROUNDS * t + c + 1)
                    for j in range(TPB):
                        mm = pe.transpose(ps[0:NE, AUX + 1, j * P:(j + 1) * P], F["weights"][:, j, :], ident[:, :])
                    mm.then_inc(S["w_turned"], 1)

                def biases(t, c):
                    pe.wait_ge(S["w_copied"], ROUNDS * t + c + 1)
                    for j in range(TPB):
                        mm = pe.matmul(ps[:, AUX + j // 2, (j % 2) * D:(j % 2 + 1) * D], F["weights_t"][:, j * P:(j + 1) * P],
                                       W["b_down"][:, :], start=True, stop=True)
                        if j % 2:
                            mm.then_inc(S["bias"], 1)

                def turn(t, last):
                    for c in range(ROUNDS):
                        if c and not last:
                            project(t + 1, [1, *range(3, PAIRS - 1)])
                            turn_tokens(t, c)
                            project(t + 1, [PAIRS - 1])
                        elif c:
                            turn_tokens(t, c)
                        for e in range(NE + 2 - c):
                            if e == NE + 1 and not last:
                                project(t + 1, (0, 2))
                            if e < NE:
                                up(t, c, e)
                            if e == 0:
                                route(c)
                                if c == 0 and later(t, 0):
                                    down(t - 1, ROUNDS - 1, NE - 1)
                            if 1 <= e <= NE:
                                gate(t, c, e - 1)
                            if e == 1:
                                turn_weights(t, c)
                            if e == 2:
                                biases(t, c)
                            if e == NE and c and not last:
                                turn_tokens(t + 1, 0)
                            if e >= 2:
                                down(t, c, e - 2)

                project(0)
                turn_tokens(0, 0)
                pe.wait_ge(S["small_in"], small_total)
                pe.wait_ge(S["router_lo"], 1)
                blocks(pe, turn)
                down(NBLK - 1, ROUNDS - 1, NE - 1)

            @block.scalar
            def _(act):
                def split_y(t, pair):
                    if not later(t, 0) and pair % 2 == 0:
                        act.wait_ge(S[f"y_first{pair // 2}"], DMA)
                    elif pair == 0:
                        act.wait_ge(S["y_in"], DMA * t)
                    if later(t, 0):
                        if pair < PAIRS // 2:
                            act.wait_ge(S["gate"], 2 * Q * t - Q - 2)
                        else:
                            act.wait_ge(S["down"], 2 * Q * t - Q - 2)
                    act.activation(y_hi[:, pair, :], y_raw[:, pair, :], ACT.Copy).then_inc(S["y_hi"], 1)

                def unit_hi(u):
                    es, n = unit_experts(u)
                    act.wait_ge(S[f"slot{unit_slot(u)[0]}"], unit_in(u))
                    act.activation(W[UNITS[u][0] + "_hi"][:, es], unit_slot(u)[1][:, 0:n], ACT.Copy).then_inc(S["w_hi"], 1)

                def hidden(t, c, e):
                    q = Q * t + NE * c + e
                    for m in range(2):
                        act.wait_ge(S["up"], 2 * q + m + 1)
                        if later(t, NE * c + e - 1):
                            act.wait_ge(S["g"], 2 * q - 3 + m)
                            act.wait_ge(S["h_lo"], 2 * q - 3 + m)
                        act.activation(h[:, e % 2, m, :], ps[:, UP + m, :], ACT.Identity,
                                       bias=W["b_up"][:, 2 * e + m:2 * e + m + 1]).then_inc(S["h"], 1)

                def silu(t, c, e):
                    q = Q * t + NE * c + e
                    for m in range(2):
                        act.wait_ge(S["gate"], 2 * q + m + 1)
                        if later(t, NE * c + e - 1):
                            act.wait_ge(S["g_lo"], 2 * q - 3 + m)
                        act.activation(s_[:, e % 2, m, :], ps[:, GATE + m, :], ACT.Silu,
                                       bias=W["b_gate"][:, 2 * e + m:2 * e + m + 1]).then_inc(S["silu"], 1)

                def xt_hi(t, c):
                    act.wait_ge(S["turned"], ROUNDS * t + c + 1)
                    for dt in range(DT):
                        act.activation(xth[:, dt, :], ps[:, AUX + dt, :], ACT.Copy).then_inc(S["xt_hi"], 1)

                def turn(t, last):
                    for c in range(ROUNDS):
                        r = ROUNDS * t + c
                        if c:
                            xt_hi(t, c)
                        for e in range(NE + 1):
                            if e < NE:
                                hidden(t, c, e)
                            if e == 1:
                                act.wait_ge(S["diff"], r + 1)
                                act.activation(F["tanh"][:, :, :], F["diff"][:, :, :], ACT.Tanh, scale=0.5).then_inc(S["tanh"], 1)
                            if e >= 1:
                                silu(t, c, e - 1)
                            if isinstance(t, int) and t == 0 and c == 0:
                                for u in UNITS_AT.get(e, []):
                                    unit_hi(u)
                            if e == 1:
                                act.wait_ge(S["w_turned"], r + 1)
                                act.activation(F["weights_t"][:, :], ps[0:NE, AUX + 1, :], ACT.Copy).then_inc(S["w_copied"], 1)
                        if c == 0 and not last:
                            for pair in range(PAIRS):
                                split_y(t + 1, pair)
                        if c and not last:
                            xt_hi(t + 1, 0)

                for pair in range(PAIRS):
                    split_y(0, pair)
                act.wait_ge(S["small_in"], small_total)
                act.activation(W["router_hi"][:, :, :, :], F["router_raw"][:, :, :, :], ACT.Copy).then_inc(S["router_hi"], 1)
                unit_hi(0)
                xt_hi(0, 0)
                for u in range(1, FIRST_UNITS):
                    unit_hi(u)
                act.wait_ge(S["w_lo"], FIRST_UNITS)
                blocks(act, turn)

            def y_lo_parts(eng, t, pair):
                eng.wait_ge(S["y_hi"], PAIRS * t + pair + 1)
                if later(t, 0):
                    if pair < PAIRS // 2:
                        eng.wait_ge(S["gate"], 2 * Q * t - Q)
                    else:
                        eng.wait_ge(S["down"], 2 * Q * t - Q)
                eng.tensor_tensor(y_lo[:, pair, :], y_raw[:, pair, :], f32(y_hi[:, pair, :]),
                                  ALU.subtract).then_inc(S["y_lo_odd" if pair % 2 else "y_lo_even"], 1)

            @block.gpsimd
            def _(pool):
                def rstd(t):
                    pool.wait_ge(S["var"], t + 1)
                    pool.tensor_tensor(F["rs"][:, :, :], F["var"][:, :, :], W["minus_half"][:, :, None], ALU.pow).then_inc(S["rstd"], 1)

                def h_lo(t, c, e):
                    q = Q * t + NE * c + e
                    for m in range(2):
                        pool.wait_ge(S["h_hi"], 2 * q + m + 1)
                        pool.tensor_tensor(parts[:, e % 2, H_LO, m, :], h[:, e % 2, m, :],
                                           f32(parts[:, e % 2, H_HI, m, :]), ALU.subtract).then_inc(S["h_lo"], 1)

                def g_lo(t, c, e):
                    q = Q * t + NE * c + e
                    for m in range(2):
                        pool.wait_ge(S["g_hi"], 2 * q + m + 1)
                        pool.tensor_tensor(parts[:, e % 2, G_LO, m, :], s_[:, e % 2, m, :],
                                           f32(parts[:, e % 2, G_HI, m, :]), ALU.subtract).then_inc(S["g_lo"], 1)

                def rms(t, c):
                    r = ROUNDS * t + c
                    pool.wait_ge(S["scale_var"], r + 1)
                    pool.tensor_tensor(F["rms"][:, :], F["rms_var"][:, :], W["minus_half"][:, :], ALU.pow).then_inc(S["scale"], 1)

                def turn(t, last):
                    for c in range(ROUNDS):
                        for e in range(NE + 1):
                            if e < NE:
                                h_lo(t, c, e)
                            if e == 0 and c == 0 and later(t, 0):
                                rms(t - 1, ROUNDS - 1)
                            if e == 2 and c and not last:
                                rstd(t + 1)
                            if e >= 1:
                                g_lo(t, c, e - 1)
                        if c == 0:
                            if not last:
                                y_lo_parts(pool, t + 1, 1)
                                y_lo_parts(pool, t + 1, 3)
                            if not last:
                                y_lo_parts(pool, t + 1, 5)
                                y_lo_parts(pool, t + 1, 7)
                            rms(t, c)

                pool.memset(W["earlier"][:, :, :, :], 1.0).then_inc(S["filled"], 1)
                pool.wait_ge(S["filled"], 1)
                pool.affine_select(out=W["earlier"][:, :, :, :], in_=W["earlier"][:, :, :, :], compare_op=ALU.is_gt, fill=0.0,
                                   base=0, pattern=[[0, TPB], [1, E], [-1, E]], channel_multiplier=0).then_inc(S["filled"], 1)
                for pair in range(1, PAIRS, 2):
                    y_lo_parts(pool, 0, pair)
                rstd(0)
                blocks(pool, turn)
                rms(NBLK - 1, ROUNDS - 1)

            @block.vector
            def _(dve):
                ROUTE_STEPS = 12

                def choose(t, c):
                    g, b, r, pair, eq = F["g"], F["biased"], F["rank"], F["beaten"], F["equal"]
                    src = ps[:, AUX, 0:TPB * NE].rearrange("p (j e) -> p j e", e=NE)[:, :, 0:E]
                    other = b[:, :, None, :].broadcast_to([P, TPB, E, E])
                    own = b[:, :, :, None].broadcast_to([P, TPB, E, E])
                    base = ROUTE_STEPS * (ROUNDS * t + c)
                    dve.wait_ge(S["routed"], ROUNDS * t + c + 1)
                    dve.tensor_tensor(g[:, :, :], src, W["router_b"][:, c, None, :].broadcast_to([P, TPB, E]), ALU.add).then_inc(S["route"], 1)
                    dve.wait_ge(S["route"], base + 1)
                    dve.tensor_tensor(b[:, :, :], g[:, :, :], W["gate_bias"][:, c, None, :].broadcast_to([P, TPB, E]), ALU.add).then_inc(S["route"], 1)
                    dve.wait_ge(S["route"], base + 2)
                    dve.tensor_tensor(pair[:, :, :, :], other, own, ALU.is_gt).then_inc(S["route"], 1)
                    dve.tensor_tensor(eq[:, :, :, :], other, own, ALU.is_equal).then_inc(S["route"], 1)
                    dve.wait_ge(S["route"], base + 4)
                    dve.tensor_tensor(eq[:, :, :, :], eq[:, :, :, :], W["earlier"][:, :, :, :], ALU.mult).then_inc(S["route"], 1)
                    dve.wait_ge(S["route"], base + 5)
                    dve.tensor_tensor(pair[:, :, :, :], pair[:, :, :, :], eq[:, :, :, :], ALU.add).then_inc(S["route"], 1)
                    dve.wait_ge(S["route"], base + 6)
                    dve.tensor_reduce(r[:, :, :], pair[:, :, :, :], AX.X, ALU.add).then_inc(S["route"], 1)
                    dve.wait_ge(S["route"], base + 7)
                    dve.tensor_scalar(F["chosen"][:, :, :], r[:, :, :], 2.0, None, ALU.is_lt).then_inc(S["route"], 1)
                    dve.wait_ge(S["route"], base + 8)
                    dve.tensor_tensor(b[:, :, :], F["chosen"][:, :, :], g[:, :, :], ALU.mult).then_inc(S["route"], 1)
                    dve.wait_ge(S["route"], base + 9)
                    dve.tensor_reduce(F["both"][:, :], b[:, :, :], AX.X, ALU.add).then_inc(S["route"], 1)
                    dve.wait_ge(S["route"], base + 10)
                    dve.tensor_tensor(b[:, :, :], g[:, :, :], F["both"][:, :, None].broadcast_to([P, TPB, E]), ALU.subtract).then_inc(S["route"], 1)
                    dve.wait_ge(S["route"], base + 11)
                    dve.tensor_tensor(F["diff"][:, :, :], b[:, :, :], g[:, :, :], ALU.add).then_inc(S["diff"], 1)

                def weigh(t, c):
                    r = ROUNDS * t + c
                    dve.wait_ge(S["tanh"], r + 1)
                    dve.tensor_scalar(F["tanh"][:, :, :], F["tanh"][:, :, :], 0.5, 0.5, ALU.mult, ALU.add).then_inc(S["route"], 1)
                    dve.wait_ge(S["route"], ROUTE_STEPS * (r + 1))
                    dve.tensor_tensor(F["weights"][:, :, 0:E], F["tanh"][:, :, :], F["chosen"][:, :, :],
                                      ALU.mult).then_inc(S["weights"], 1)

                def split_hidden(t, c, e):
                    q = Q * t + NE * c + e
                    for m in range(2):
                        dve.wait_ge(S["h"], 2 * q + m + 1)
                        if later(t, NE * c + e - 1):
                            dve.wait_ge(S["gate"], 2 * q - 2)
                        if e < 2 and not (c and isinstance(t, int) and t == NBLK - 1):
                            dve.wait_ge(S["proj"], 2 * (t + c) + 2)
                        dve.tensor_copy(parts[:, e % 2, H_HI, m, :], h[:, e % 2, m, :]).then_inc(S["h_hi"], 1)

                def gated(t, c, e):
                    q = Q * t + NE * c + e
                    for m in range(2):
                        dve.wait_ge(S["silu"], 2 * q + m + 1)
                        dve.tensor_tensor(s_[:, e % 2, m, :], s_[:, e % 2, m, :], h[:, e % 2, m, :], ALU.mult).then_inc(S["g"], 1)
                    for m in range(2):
                        dve.wait_ge(S["g"], 2 * q + m + 1)
                        if later(t, NE * c + e - 1):
                            dve.wait_ge(S["down"], 2 * q - 2)
                        dve.tensor_copy(parts[:, e % 2, G_HI, m, :], s_[:, e % 2, m, :]).then_inc(S["g_hi"], 1)

                def seed(t, c, moments_next):
                    if moments_next:
                        dve.wait_ge(S["stats"], TPB * (t + 2))
                    for k in range(2):
                        dve.wait_ge(S["bias"], 2 * (ROUNDS * t + c) + k + 1)
                        two = (full, slice(2 * k, 2 * k + 2), full)
                        dve.tensor_tensor(acc[two], ps[:, AUX + k, :].rearrange("p (j d) -> p j d", d=D), (xf if c else xn)[two],
                                          ALU.add).then_inc(S["seeded"], 1)

                def add_expert(t, c, e):
                    q = Q * t + NE * c + e
                    for j in range(TPB):
                        dve.wait_ge(S["down"], 2 * q + j // 2 + 1)
                        if e:
                            dve.wait_ge(S["sum"], TPB * (q - 1) + j + 1)
                        else:
                            dve.wait_ge(S["seeded"], 2 * (ROUNDS * t + c) + j // 2 + 1)
                        dve.scalar_tensor_tensor(out=acc[:, j, :], in0=ps[:, DOWN + j // 2, (j % 2) * D:(j % 2 + 1) * D],
                                                 scalar=F["weights"][:, j, e:e + 1], in1=acc[:, j, :],
                                                 op0=ALU.mult, op1=ALU.add).then_inc(S["sum"], 1)

                def square(t, c):
                    r = ROUNDS * t + c
                    if not c and later(t, 0):
                        dve.wait_ge(S["stored"], DMA * TPB * t)
                    dve.wait_ge(S["sum"], TPB * (Q * t + NE * (c + 1)))
                    dve.tensor_tensor(xf[:, :, :], acc[:, :, :], acc[:, :, :], ALU.mult).then_inc(S["squared"], 1)
                    dve.wait_ge(S["squared"], r + 1)
                    dve.tensor_reduce(F["ss"][:, :], xf[:, :, :], AX.X, ALU.add).then_inc(S["squares"], 1)
                    dve.wait_ge(S["squares"], r + 1)
                    dve.tensor_scalar(F["rms_var"][:, :], F["ss"][:, :], 1.0 / D, RMS_EPS, ALU.mult, ALU.add).then_inc(S["scale_var"], 1)

                def normalize(t, c):
                    r = ROUNDS * t + c
                    dve.wait_ge(S["scale"], r + 1)
                    for j in range(TPB):
                        dve.scalar_tensor_tensor(out=xf[:, j, :], in0=acc[:, j, :], scalar=F["rms"][:, j:j + 1],
                                                 in1=W["norm_w"][:, c, :], op0=ALU.mult, op1=ALU.mult).then_inc(S["scaled"], 1)
                    if c:
                        for j in range(TPB):
                            dve.wait_ge(S["scaled"], TPB * r + j + 1)
                            dve.tensor_tensor(xf[:, j, :], xf[:, j, :], x1[:, j, :], ALU.add).then_inc(S["out_ready"], 1)

                def residual(t):
                    dve.wait_ge(S["x_in"], DMA * (t + 1))
                    for k in range(2):
                        dve.wait_ge(S["proj"], 2 * t + k + 1)
                        two = (full, slice(2 * k, 2 * k + 2), full)
                        dve.tensor_tensor(x1_next[two], ps[:, PROJ + k, :].rearrange("p (j d) -> p j d", d=D), x1_next[two],
                                          ALU.add).then_inc(S["x1"], 1)

                def stats(t):
                    for j in range(TPB):
                        dve.wait_ge(S["x1"], 2 * t + j // 2 + 1)
                        dve.bn_stats(F["st"][:, j, :], x1_next[:, j, :]).then_inc(S["stats"], 1)

                def moments(t):
                    for j in range(TPB):
                        dve.bn_aggr(F["mv"][:, j, :], F["st"][:, j, :]).then_inc(S["mean"], 1)
                    dve.wait_ge(S["mean"], TPB * (t + 1))
                    dve.tensor_scalar(F["var"][:, :, :], F["mv"][:, :, 1:2], LN_EPS, None, ALU.add).then_inc(S["var"], 1)

                def layernorm(t):
                    dve.wait_ge(S["rstd"], t + 1)
                    for j in range(TPB):
                        dve.tensor_scalar(xn[:, j, :], x1_next[:, j, :], F["mv"][:, j, 0:1], F["rs"][:, j, :],
                                          ALU.subtract, ALU.mult).then_inc(S["x_norm"], 1)

                def xt_lo(t, c):
                    for dt in range(DT):
                        dve.wait_ge(S["xt_hi"], DT * (ROUNDS * t + c) + dt + 1)
                        dve.tensor_tensor(xtl[:, dt, :], ps[:, AUX + dt, :], f32(xth[:, dt, :]), ALU.subtract).then_inc(S["xt_lo"], 1)

                def keep_residual(t):
                    if later(t, 0):
                        dve.wait_ge(S["out_ready"], TPB * t)
                    dve.wait_ge(S["x1"], 2 * t + 2)
                    dve.tensor_copy(x1[:, :, :], x1_next[:, :, :]).then_inc(S["x1_kept"], 1)

                def unit_lo(u):
                    es, n = unit_experts(u)
                    dve.wait_ge(S["w_hi"], u + 1)
                    dve.tensor_tensor(W[UNITS[u][0] + "_lo"][:, es], unit_slot(u)[1][:, 0:n], f32(W[UNITS[u][0] + "_hi"][:, es]),
                                      ALU.subtract).then_inc(S["w_lo"], 1)

                def turn(t, last):
                    for c in range(ROUNDS):
                        if c:
                            xt_lo(t, c)
                            if not last:
                                residual(t + 1)
                        for e in range(NE + 2 - c):
                            if e < NE:
                                split_hidden(t, c, e)
                            if e == 0:
                                choose(t, c)
                                if c == 0 and later(t, 0):
                                    add_expert(t - 1, ROUNDS - 1, NE - 1)
                                    square(t - 1, ROUNDS - 1)
                            if e == 1:
                                weigh(t, c)
                            if 1 <= e <= NE:
                                gated(t, c, e - 1)
                            if e == 1 and c == 0:
                                if later(t, 0):
                                    normalize(t - 1, ROUNDS - 1)
                                keep_residual(t)
                            if e == 2:
                                if c and not last:
                                    stats(t + 1)
                                seed(t, c, c and not last)
                                if c and not last:
                                    moments(t + 1)
                            if e == 3 and c and not last:
                                layernorm(t + 1)
                            if e == NE and c and not last:
                                xt_lo(t + 1, 0)
                            if e == NE and c == 0 and not last:
                                y_lo_parts(dve, t + 1, 0)
                                y_lo_parts(dve, t + 1, 2)
                            if e >= 2:
                                add_expert(t, c, e - 2)
                            if isinstance(t, int) and t == 0 and c == 0:
                                for u in UNITS_AT.get(e, []):
                                    unit_lo(u)
                        if c == 0:
                            if not last:
                                y_lo_parts(dve, t + 1, 4)
                            square(t, c)
                            if not last:
                                y_lo_parts(dve, t + 1, 6)
                            normalize(t, c)

                dve.memset(F["weights"][:, :, E:NE], 1.0).then_inc(S["ones"], 1)
                for pair in range(0, PAIRS, 2):
                    y_lo_parts(dve, 0, pair)
                dve.wait_ge(S["router_hi"], 1)
                dve.tensor_tensor(W["router_lo"][:, :, :, :], F["router_raw"][:, :, :, :], f32(W["router_hi"][:, :, :, :]),
                                  ALU.subtract).then_inc(S["router_lo"], 1)
                residual(0)
                stats(0)
                dve.wait_ge(S["stats"], TPB)
                moments(0)
                layernorm(0)
                unit_lo(0)
                xt_lo(0, 0)
                for u in range(1, FIRST_UNITS):
                    unit_lo(u)
                dve.wait_ge(S["filled"], 2)
                blocks(dve, turn)
                add_expert(NBLK - 1, ROUNDS - 1, NE - 1)
                square(NBLK - 1, ROUNDS - 1)
                normalize(NBLK - 1, ROUNDS - 1)
        clear_semaphores(nc, S.values())


def build_mixture(nc, W, w, y_dram, out):
    with ExitStack() as ctx:
        def sb(name, shape, dt=F32):
            return ctx.enter_context(nc.sbuf_tensor(name, shape, dt))
        W = dict(W)
        for k, n in (("up", NE), ("gate", E + 1), ("down", E + 1)):
            W[k + "_hi"] = sb(k + "_hi", [P, n, DT, I], F32R)
            W[k + "_lo"] = sb(k + "_lo", [P, n, DT, I], F32R)
        W["router_hi"] = sb("router_hi", [P, ROUNDS, DT, E], F32R)
        W["router_lo"] = sb("router_lo", [P, ROUNDS, DT, E], F32R)
        W["b_up"], W["b_gate"] = sb("b_up", [P, 2 * NE]), sb("b_gate", [P, 2 * NE])
        W["b_down"] = sb("b_down", [NE, D])
        W["router_b"], W["gate_bias"] = sb("router_b", [P, ROUNDS, E]), sb("gate_bias", [P, ROUNDS, E])
        W["norm_w"] = sb("norm_w", [P, ROUNDS, D])
        W["earlier"] = sb("earlier", [P, TPB, E, E])
        F = {"y_raw": sb("y_raw", [P, PAIRS, BLK]), "x1": sb("x1", [P, TPB, D]),
             "x1_next": sb("x1_next", [P, TPB, D]), "xn": sb("xn", [P, TPB, D]),
             "xf": sb("xf", [P, TPB, D]), "acc": sb("acc", [P, TPB, D]),
             "parts": sb("parts", [P, 2, 4, 2, BLK], F32R), "hs": sb("hidden_and_silu", [P, 4, 2, BLK]), "router_raw": sb("router_raw", [P, ROUNDS, DT, E]),
             "xt_hi": sb("xft_hi", [P, DT, BLK], F32R), "xt_lo": sb("xft_lo", [P, DT, BLK], F32R),
             "st": sb("st", [P, TPB, 6]), "mv": sb("mv", [P, TPB, 2]), "var": sb("var", [P, TPB, 1]),
             "rs": sb("rs", [P, TPB, 1]), "ss": sb("ss", [P, TPB]), "rms": sb("rms", [P, TPB]), "rms_var": sb("rms_var", [P, TPB]),
             "g": sb("g", [P, TPB, E]), "biased": sb("biased", [P, TPB, E]), "rank": sb("rank", [P, TPB, E]),
             "chosen": sb("chosen", [P, TPB, E]), "both": sb("both", [P, TPB]), "diff": sb("diff", [P, TPB, E]),
             "tanh": sb("tanh", [P, TPB, E]), "beaten": sb("beaten", [P, TPB, E, E]), "equal": sb("equal", [P, TPB, E, E]),
             "weights": sb("weights", [P, TPB, NE]), "weights_t": sb("weights_t", [NE, BLK])}
        x_v = w["x"].rearrange("b (q j p) d -> (b q) p j d", p=P, j=TPB)
        out_v = out.rearrange("b (q j p) d -> (b q) p j d", p=P, j=TPB)
        y_v = y_dram.rearrange("b q p h n -> (b q) p h n")
        F["h"], F["s"] = F["hs"][:, 0:2], F["hs"][:, 2:4]
        nc.disable_value_cache = True
        build_tokens(nc, W, F, w, y_v, x_v, out_v)
        nc.disable_value_cache = False


def build(nc, w, out):
    y_dram = nc.dram_tensor("y_latent", [B, QB, P, PAIRS, BLK], F32).ap()
    recip_rows = nc.dram_tensor("recip_rows", [QB, P, TPB], F32).ap()
    with ExitStack() as ctx:
        T = shared_tensors(nc, ctx)
        with ExitStack() as attention:
            A = dict(T) | attention_tensors(nc, attention)
            build_weights(nc, A, w)
            with nc.Fori(0, B) as b:
                nc.disable_value_cache = True
                build_attention(nc, A, w["x"][b], y_dram[b], recip_rows)
                nc.disable_value_cache = False
        build_mixture(nc, T, w, y_dram, out)


def kernel(L0_attn_x_bld, L0_attn_Wq, L0_attn_Wkv_down, L0_attn_Wk_up, L0_attn_Wv_up, L0_attn_Wout,
           L0_ffn_router_W, L0_ffn_router_b, L0_ffn_gate_bias, L0_ffn_exp_Wup, L0_ffn_exp_bup, L0_ffn_exp_Wg,
           L0_ffn_exp_bg, L0_ffn_exp_Wdown, L0_ffn_exp_bdown, L0_ffn_share_Wup, L0_ffn_share_bup, L0_ffn_share_Wg,
           L0_ffn_share_bg, L0_ffn_share_Wdown, L0_ffn_share_bdown, L0_ffn_norm_w):
    import concourse.bacc as bacc
    from concourse.bass_utils import run_bass_kernel_spmd as run

    def per_partition(*biases):
        rows = np.concatenate([np.asarray(b).reshape(-1, 2, P) for b in biases])
        return rows.transpose(2, 0, 1).reshape(P, -1)

    def every_partition(a):
        return np.broadcast_to(np.asarray(a)[None], (P, *np.asarray(a).shape))

    a = np.asarray
    arrays = {
        "x": a(L0_attn_x_bld), "wqT": a(L0_attn_Wq).transpose(1, 2, 0), "wkT": a(L0_attn_Wk_up).transpose(1, 2, 0),
        "wvT": a(L0_attn_Wv_up).transpose(1, 2, 0), "wout": a(L0_attn_Wout), "wdown": a(L0_attn_Wkv_down),
        "router_w": a(L0_ffn_router_W), "router_b": every_partition(L0_ffn_router_b),
        "gate_bias": every_partition(L0_ffn_gate_bias), "norm_w": every_partition(L0_ffn_norm_w),
        "exp_up": a(L0_ffn_exp_Wup), "exp_gate": a(L0_ffn_exp_Wg), "exp_down": a(L0_ffn_exp_Wdown),
        "share_up": a(L0_ffn_share_Wup), "share_gate": a(L0_ffn_share_Wg), "share_down": a(L0_ffn_share_Wdown),
        "b_up": per_partition(L0_ffn_exp_bup, L0_ffn_share_bup),
        "b_gate": per_partition(L0_ffn_exp_bg, L0_ffn_share_bg, L0_ffn_share_bg),
        "b_down": np.concatenate([a(L0_ffn_exp_bdown), a(L0_ffn_share_bdown)[None], a(L0_ffn_share_bdown)[None]]),
    }
    arrays = {n: np.ascontiguousarray(v) for n, v in arrays.items()}
    nc = bacc.Bacc("TRN2", target_bir_lowering=False, num_devices=1)
    w = {n: nc.dram_tensor("in_" + n, v.shape, mybir.dt.from_np(v.dtype), kind="ExternalInput").ap() for n, v in arrays.items()}
    out = nc.dram_tensor("out", (B, L, D), F32, kind="ExternalOutput").ap()
    build(nc, w, out)
    r = run(nc, [{"in_" + n: v for n, v in arrays.items()}], core_ids=[0])
    return r.results[0]["out"]
```
